# Optimizing a Trainium2 kernel written in Bass

```python
import numpy as np
import jax
import jax.numpy as jnp

def _softmax(x, axis=-1):
    return jax.nn.softmax(x, axis=axis)

def _gelu(x):
    return jax.nn.gelu(x, approximate=True)

def _silu(x):
    return jax.nn.silu(x)

def _sigmoid(x):
    return jax.nn.sigmoid(x)

def _layernorm(x, axis=-1, eps=1e-05):
    m = jnp.mean(x, axis=axis, keepdims=True)
    v = jnp.var(x, axis=axis, keepdims=True)
    return (x - m) / jnp.sqrt(v + eps)

def _scatter_add(tgt, idx, src, axis=0):
    return tgt.at[idx].add(src)

def _segment_sum(src, seg, n):
    return jax.ops.segment_sum(src, seg, n)
kernel_name = 'mk_decoder_preln_d1_seqx_r8_63d117'

def setup_inputs(seed: int=0):
    np.random.seed(seed)
    _w = jnp.asarray

    def _rec_inputs():
        import jax
        import jax.numpy as jnp
        _rk = jax.random.key(seed)
        x = -0.0002928 + 1 * jax.random.normal(jax.random.fold_in(_rk, 1), (4, 512, 128), jnp.float32)
        _lenS = 512 - jax.random.randint(jax.random.fold_in(_rk, 7), (4,), 0, max(1, 512 // 4) + 1, jnp.int32)
        _lenS2 = 77 - jax.random.randint(jax.random.fold_in(_rk, 8), (4,), 0, max(1, 77 // 4) + 1, jnp.int32)
        _ctx_1024P = jax.random.normal(jax.random.fold_in(_rk, 11), (4, 16, 128), jnp.float32)
        _ctx_1024c = jax.random.dirichlet(jax.random.fold_in(_rk, 511), 0.3 * jnp.ones((16,), jnp.float32), (4, 77))
        _ctx_1024t = jnp.einsum('bsk,bkd->bsd', _ctx_1024c, _ctx_1024P)
        _ctx_1024t = _ctx_1024t * jax.lax.rsqrt(jnp.mean(jnp.square(_ctx_1024t)) + 1e-12) * 0.953939
        ctx_1024 = -1.39393e-06 + 0.999914 * (_ctx_1024t + 0.3 * jax.random.normal(jax.random.fold_in(_rk, 611), (4, 77, 128), jnp.float32))
        return (x, ctx_1024)
    x, ctx_1024 = _rec_inputs()

    def _L0_attn_setup():
        import jax, jax.numpy as jnp
        import numpy as np
        N_HEADS = 16
        HIDDEN = 128
        HEAD_DIM = 64
        BSZ = 4
        SEQ = 128
        SCALE = HEAD_DIM ** (-0.5)
        key = jax.random.key(seed)
        k_x, k_q, k_k, k_v, k_o = jax.random.split(key, 5)
        s = HIDDEN ** (-0.5)
        return {'x': jax.random.normal(k_x, (BSZ, SEQ, HIDDEN), dtype=jnp.float32), 'wq': jax.random.normal(k_q, (N_HEADS * HEAD_DIM, HIDDEN), dtype=jnp.float32) * s, 'wk': jax.random.normal(k_k, (N_HEADS * HEAD_DIM, HIDDEN), dtype=jnp.float32) * s, 'wv': jax.random.normal(k_v, (N_HEADS * HEAD_DIM, HIDDEN), dtype=jnp.float32) * s, 'wo': jax.random.normal(k_o, (HIDDEN, N_HEADS * HEAD_DIM), dtype=jnp.float32) * s}
    _L0_attn_all = _L0_attn_setup()
    _L0_attn_in = {k: v for k, v in _L0_attn_all.items() if k in ('wq', 'wk', 'wv', 'wo')}
    del _L0_attn_all

    def _L0_xattn_setup():
        import jax, jax.numpy as jnp
        import numpy as np
        D_MODEL = 128
        H = 16
        D_K = D_MODEL // H
        NEG = -1000000000.0

        def _softplus_t(x):
            return jnp.where(x > 20.0, x, jax.nn.softplus(x))
        key = jax.random.key(seed)
        ks = jax.random.split(key, 12)
        B, S = (2, 256)
        sc = 1.0 / np.sqrt(D_MODEL)
        inp = {'query': jax.random.normal(ks[0], (B, S, D_MODEL), jnp.float32), 'key': jax.random.normal(ks[1], (B, S, D_MODEL), jnp.float32), 'value': jax.random.normal(ks[2], (B, S, D_MODEL), jnp.float32), 'Wq': jax.random.normal(ks[3], (D_MODEL, D_MODEL), jnp.float32) * sc, 'bq': jnp.zeros((D_MODEL,), jnp.float32), 'Wk': jax.random.normal(ks[4], (D_MODEL, D_MODEL), jnp.float32) * sc, 'bk': jnp.zeros((D_MODEL,), jnp.float32), 'Wv': jax.random.normal(ks[5], (D_MODEL, D_MODEL), jnp.float32) * sc, 'bv': jnp.zeros((D_MODEL,), jnp.float32), 'Wo': jax.random.normal(ks[6], (D_MODEL, D_MODEL), jnp.float32) * sc, 'bo': jnp.zeros((D_MODEL,), jnp.float32), 'raw_thresholds': jnp.full((H, 1, 1), 0.1, jnp.float32)}
        return inp
    _L0_xattn_all = _L0_xattn_setup()
    _L0_xattn_in = {k: v for k, v in _L0_xattn_all.items() if k in ('Wq', 'bq', 'Wk', 'bk', 'Wv', 'bv', 'Wo', 'bo', 'raw_thresholds')}
    del _L0_xattn_all

    def _L0_ffn_setup():
        import jax, jax.numpy as jnp
        import numpy as np
        D, H, E, K, S = (128, 256, 8, 2, 1)
        B, L = (4, 256)
        key = jax.random.key(seed)
        ks = jax.random.split(key, 9)
        std = 0.02
        return {'x': jax.random.normal(ks[0], (B, L, D), dtype=jnp.float32), 'router_w': jax.random.normal(ks[1], (E, D), dtype=jnp.float32) * std, 'experts_bias': jnp.zeros((E,), dtype=jnp.float32), 'w1': jax.random.normal(ks[2], (E, D, H), dtype=jnp.float32) * std, 'w3': jax.random.normal(ks[3], (E, D, H), dtype=jnp.float32) * std, 'w2': jax.random.normal(ks[4], (E, H, D), dtype=jnp.float32) * std, 'sw1': jax.random.normal(ks[5], (S, D, H), dtype=jnp.float32) * std, 'sw3': jax.random.normal(ks[6], (S, D, H), dtype=jnp.float32) * std, 'sw2': jax.random.normal(ks[7], (S, H, D), dtype=jnp.float32) * std}
    _L0_ffn_all = _L0_ffn_setup()
    _L0_ffn_in = {k: v for k, v in _L0_ffn_all.items() if k in ('router_w', 'experts_bias', 'w1', 'w3', 'w2', 'sw1', 'sw3', 'sw2')}
    del _L0_ffn_all
    return {'x': x, 'ctx_1024': ctx_1024, 'L0_attn_wq': _L0_attn_in['wq'], 'L0_attn_wk': _L0_attn_in['wk'], 'L0_attn_wv': _L0_attn_in['wv'], 'L0_attn_wo': _L0_attn_in['wo'], 'L0_xattn_Wq': _L0_xattn_in['Wq'], 'L0_xattn_bq': _L0_xattn_in['bq'], 'L0_xattn_Wk': _L0_xattn_in['Wk'], 'L0_xattn_bk': _L0_xattn_in['bk'], 'L0_xattn_Wv': _L0_xattn_in['Wv'], 'L0_xattn_bv': _L0_xattn_in['bv'], 'L0_xattn_Wo': _L0_xattn_in['Wo'], 'L0_xattn_bo': _L0_xattn_in['bo'], 'L0_xattn_raw_thresholds': _L0_xattn_in['raw_thresholds'], 'L0_ffn_router_w': _L0_ffn_in['router_w'], 'L0_ffn_experts_bias': _L0_ffn_in['experts_bias'], 'L0_ffn_w1': _L0_ffn_in['w1'], 'L0_ffn_w3': _L0_ffn_in['w3'], 'L0_ffn_w2': _L0_ffn_in['w2'], 'L0_ffn_sw1': _L0_ffn_in['sw1'], 'L0_ffn_sw3': _L0_ffn_in['sw3'], 'L0_ffn_sw2': _L0_ffn_in['sw2']}

def reference(x, ctx_1024, L0_attn_wq, L0_attn_wk, L0_attn_wv, L0_attn_wo, L0_xattn_Wq, L0_xattn_bq, L0_xattn_Wk, L0_xattn_bk, L0_xattn_Wv, L0_xattn_bv, L0_xattn_Wo, L0_xattn_bo, L0_xattn_raw_thresholds, L0_ffn_router_w, L0_ffn_experts_bias, L0_ffn_w1, L0_ffn_w3, L0_ffn_w2, L0_ffn_sw1, L0_ffn_sw3, L0_ffn_sw2):
    import jax
    import jax.numpy as jnp

    def _L0_attn_ref(x, wq, wk, wv, wo):
        import jax, jax.numpy as jnp
        import numpy as np
        N_HEADS = 16
        HIDDEN = 128
        HEAD_DIM = 64
        BSZ = 4
        SEQ = 128
        SCALE = HEAD_DIM ** (-0.5)
        bsz, seqlen, _ = x.shape
        xq = jnp.einsum('bsh,oh->bso', x, wq)
        xk = jnp.einsum('bsh,oh->bso', x, wk)
        xv = jnp.einsum('bsh,oh->bso', x, wv)
        xq = xq.reshape(bsz, N_HEADS, seqlen, HEAD_DIM)
        xk = xk.reshape(bsz, N_HEADS, seqlen, HEAD_DIM)
        xv = xv.reshape(bsz, N_HEADS, seqlen, HEAD_DIM)
        scores = jnp.einsum('bhid,bhjd->bhij', xq, xk) * SCALE
        scores = jax.nn.softmax(scores, axis=-1)
        out = jnp.einsum('bhij,bhjd->bhid', scores, xv)
        out = out.reshape(bsz, seqlen, N_HEADS * HEAD_DIM)
        return jnp.einsum('bso,ho->bsh', out, wo)

    def _L0_xattn_ref(query, key, value, Wq, bq, Wk, bk, Wv, bv, Wo, bo, raw_thresholds):
        import jax, jax.numpy as jnp
        import numpy as np
        D_MODEL = 128
        H = 16
        D_K = D_MODEL // H
        NEG = -1000000000.0

        def _softplus_t(x):
            return jnp.where(x > 20.0, x, jax.nn.softplus(x))
        B, S, _ = query.shape

        def proj(x, W, b):
            return (x @ W.T + b).reshape(B, -1, H, D_K).transpose(0, 2, 1, 3)
        Q = proj(query, Wq, bq)
        K = proj(key, Wk, bk)
        V = proj(value, Wv, bv)
        scores = jnp.einsum('bhqd,bhkd->bhqk', Q, K) / jnp.sqrt(jnp.float32(D_K))
        thr = _softplus_t(raw_thresholds)[None]
        scores = jnp.where(scores <= thr, NEG, scores)
        attn = jax.nn.softmax(scores, axis=-1)
        x = jnp.einsum('bhqk,bhkd->bhqd', attn, V)
        x = x.transpose(0, 2, 1, 3).reshape(B, S, H * D_K)
        return x @ Wo.T + bo

    def _L0_ffn_ref(x, router_w, experts_bias, w1, w3, w2, sw1, sw3, sw2):
        import jax, jax.numpy as jnp
        import numpy as np
        D, H, E, K, S = (128, 256, 8, 2, 1)
        B, L = (4, 256)
        b, l, d = x.shape
        xf = x.reshape(-1, d)
        sg = jnp.einsum('td,sdh->tsh', xf, sw1)
        su = jnp.einsum('td,sdh->tsh', xf, sw3)
        shared_out = jnp.einsum('tsh,shd->td', jax.nn.silu(sg) * su, sw2)
        logits = xf @ router_w.T + experts_bias
        rw, sel = jax.lax.top_k(logits, K)
        rw = jax.nn.softmax(rw.astype(jnp.float32), axis=-1).astype(x.dtype)
        cw = (jax.nn.one_hot(sel, E, dtype=x.dtype) * rw[..., None]).sum(axis=1)
        g = jnp.einsum('td,edh->teh', xf, w1)
        u = jnp.einsum('td,edh->teh', xf, w3)
        eo = jax.nn.silu(g) * u
        moe_out = jnp.einsum('te,teh,ehd->td', cw, eo, w2)
        return (moe_out + shared_out).reshape(b, l, d)
    x = x + _L0_attn_ref(_layernorm(x, axis=-1), L0_attn_wq, L0_attn_wk, L0_attn_wv, L0_attn_wo)
    x = x + _L0_xattn_ref(_layernorm(x, axis=-1), ctx_1024, ctx_1024, L0_xattn_Wq, L0_xattn_bq, L0_xattn_Wk, L0_xattn_bk, L0_xattn_Wv, L0_xattn_bv, L0_xattn_Wo, L0_xattn_bo, L0_xattn_raw_thresholds)
    x = x + _L0_ffn_ref(_layernorm(x, axis=-1), L0_ffn_router_w, L0_ffn_experts_bias, L0_ffn_w1, L0_ffn_w3, L0_ffn_w2, L0_ffn_sw1, L0_ffn_sw3, L0_ffn_sw2)
    return x

_drawn_inputs = setup_inputs


def setup_inputs(seed=0):
    import zlib

    import numpy as np

    out = dict(_drawn_inputs(seed))
    spreads = {'L0_xattn_bq': (0.0, 0.1),
     'L0_xattn_bk': (0.0, 0.1),
     'L0_xattn_bv': (0.0, 0.1),
     'L0_xattn_bo': (0.0, 0.1),
     'L0_xattn_raw_thresholds': (0.10000000149011612, 0.2),
     'L0_ffn_experts_bias': (0.0, 0.8)}
    factors = {'L0_ffn_router_w': 8.0,
     'L0_ffn_w1': 8.0,
     'L0_ffn_w3': 8.0,
     'L0_ffn_w2': 8.0,
     'L0_ffn_sw1': 8.0,
     'L0_ffn_sw3': 8.0,
     'L0_ffn_sw2': 8.0}
    for name, (base, spread) in spreads.items():
        noise = np.random.default_rng([zlib.crc32(name.encode()), seed]).standard_normal(out[name].shape)
        drawn = base * np.exp(spread * noise) if base else spread * noise
        out[name] = jnp.asarray(drawn.astype(out[name].dtype))
    for name, factor in factors.items():
        out[name] = (out[name] * factor).astype(out[name].dtype)
    return out
```

```python
from contextlib import ExitStack

import concourse.bass as bass
from concourse import mybir

F32 = mybir.dt.float32
F32R = mybir.dt.float32r
U32 = mybir.dt.uint32
ALU = mybir.AluOpType
ACT = mybir.ActivationFunctionType
AX = mybir.AxisListType

P = 128
B, S, D = 4, 512, 128
NT = B * S // P
EPS = 1e-5

C, DH = 16, 64
GT = 32
POS = GT * C
HG = 8
PT = HG * GT
PARTS = B * S // PT
KB = POS // P
STEPS = HG * KB
LAG_ST, LAG_SM = 2, 8

XH, XD, XK = 16, 8, 77
XF = XH * XK
XC = (XF + P - 1) // P
XL = XF - (XC - 1) * P

E, HID = 8, 256
HC = (E + 1) * HID // P


def wait_for(eng, sem, count):
    if not (isinstance(count, int) and count <= 0):
        eng.wait_ge(sem, count)


class Chain:

    def __init__(self, eng, sem):
        self.eng, self.sem, self.count = eng, sem, 0

    def link(self, instruction):
        self.count += 1
        instruction.then_inc(self.sem, 1)
        return instruction

    def wait(self):
        self.eng.wait_ge(self.sem, self.count)


def normalize(dve, chain, x, stats, moments, rstd, work, xn, root_wanted, root_ready, xn_ready):
    for t in range(NT):
        chain.link(dve.bn_stats(stats[:, t, :], x[:, t, :]))
    chain.wait()
    for t in range(NT):
        chain.link(dve.bn_aggr(moments[:, t, :], stats[:, t, :]))
    chain.wait()
    var = work[:, 0, :]
    dve.tensor_scalar(var, moments[:, :, 1], EPS, None, ALU.add).then_inc(root_wanted, 1)
    dve.wait_ge(root_ready, 1)
    chain.link(dve.reciprocal(rstd[:, 0, :], work[:, 2, :]))
    chain.wait()
    chain.link(dve.tensor_tensor(work[:, 1, :], rstd[:, 0, :], rstd[:, 0, :], ALU.mult))
    chain.wait()
    chain.link(dve.tensor_tensor(work[:, 1, :], work[:, 1, :], var, ALU.mult))
    chain.wait()
    chain.link(dve.tensor_scalar(work[:, 1, :], work[:, 1, :], -0.5, 1.5, ALU.mult, ALU.add))
    chain.wait()
    chain.link(dve.tensor_tensor(rstd[:, 1, :], rstd[:, 0, :], work[:, 1, :], ALU.mult))
    chain.wait()
    for t in range(NT):
        last = dve.tensor_scalar(xn[:, t, :], x[:, t, :], moments[:, t, 0:1],
                                 rstd[:, 1, t:t + 1], ALU.subtract, ALU.mult)
    last.then_inc(xn_ready, 1)


def transpose_tokens(pe, xn, ident, banks, xn_ready, xnT_full, xnT_ready):
    pe.wait_ge(xn_ready, 1)
    for q in range(NT // 4):
        if q >= 2:
            pe.wait_ge(xnT_ready, q - 1)
        for i in range(4):
            last = pe.transpose(banks[:, q % 2, i * P:(i + 1) * P], xn[:, 4 * q + i, :], ident[:])
        last.then_inc(xnT_full, 1)


def round_tokens(act, banks, xnT_hi, xnT_full, xnT_hi_ready):
    for q in range(NT // 4):
        act.wait_ge(xnT_full, q + 1)
        act.activation(xnT_hi[:, q * 512:(q + 1) * 512], banks[:, q % 2, :], ACT.Copy).then_inc(xnT_hi_ready, 1)


def token_rests(dve, banks, xnT_hi, xnT_lo, xnT_hi_ready, xnT_ready):
    for q in range(NT // 4):
        cols = slice(q * 512, (q + 1) * 512)
        dve.wait_ge(xnT_hi_ready, q + 1)
        dve.tensor_tensor(xnT_lo[:, cols], banks[:, q % 2, :], xnT_hi[:, cols].bitcast(F32),
                          ALU.subtract).then_inc(xnT_ready, 1)


JOBS = {0: ("qk", 0), 1: ("qk", 1), 2: ("wo", 0), 3: ("wo", 1),
        **{s: ("qk", s - 2) for s in range(4, 18)},
        18: ("v", 0), 19: ("v", 1), 24: ("v", 2), 31: ("v", 3)}


def jobs_of(has_before, has_next):
    return {s: j for s, j in JOBS.items() if (has_before if j[0] == "wo" else has_next)}


FIRST_JOBS = [("qk", i) for i in range(C)] + [("v", i) for i in range(HG // 2)]


def jobs_before(part):
    return (part + 1) * len(FIRST_JOBS)


def self_attention(nc, sb, psum, sem, t):
    x = t["x"]
    xnT_hi, xnT_lo = sb("xnT_hi", [P, B * S], F32R), sb("xnT_lo", [P, B * S], F32R)
    w_hi = sb("wqk_hi", [P, 2, C, 2, DH], F32R)
    w_lo = sb("wqk_lo", [P, 2, C, 2, DH], F32R)
    wvT, woT = sb("wvT", [P, C * DH], F32), sb("woT", [P, C // 2, D], F32)
    qk = [sb(f"qk{s}", [P, 2, HG, C, GT], F32R) for s in range(2)]
    q_lo = [sb(f"q_lo{s}", [P, HG, C, GT], F32R) for s in range(2)]
    values = sb("values", [P, HG, KB, 2, DH], F32)
    probs = sb("probs", [P, 4, POS], F32)
    attn = sb("attn", [P, C // 2, PT], F32)
    diag = sb("diag", [P, 2, KB, P], F32R)
    neg_max = sb("neg_max", [P, 4, KB], F32)
    ln_sum, inv_sum = sb("ln_sum", [DH, POS], F32), sb("inv_sum", [DH, 2, POS], F32)
    x_part = sb("x_part", [P, PT], F32)
    ones_f, ones = sb("ones_f", [P, P], F32), sb("ones", [P, P], F32R)
    stats, moments = sb("stats", [P, NT, 6], F32), sb("moments", [P, NT, 2], F32)
    rstd, work = sb("rstd", [P, 2, NT], F32), sb("work", [P, 3, NT], F32)
    ident = t["ident"]
    w_raw = probs[:].rearrange("p a b -> p (a b)").rearrange("p (w c d) -> p w c d", w=2, c=C)
    xn = attn[:].rearrange("p a b -> p (a b)").rearrange("p (t d) -> p t d", t=NT)

    sc = psum("scores", [P, 2, POS], F32)
    st = psum("scoresT", [P, 2, POS], F32)
    ov = psum("out_and_sum", [P, 2, POS], F32)
    pj = psum("projected", [P, 2, POS], F32)

    x_loaded, w_loaded, wv_loaded = sem("x_loaded"), sem("w_loaded"), sem("wv_loaded")
    root_wanted, root_ready = sem("root_wanted"), sem("root_ready")
    dve_chain = sem("dve_chain")
    xn_ready, xnT_full, xnT_hi_ready, xnT_ready = sem("xn_ready"), sem("xnT_full"), sem("xnT_hi_ready"), sem("xnT_ready")
    w_hi_ready, w_ready, ones_ready = sem("w_hi_ready"), sem("w_ready"), sem("ones_ready")
    x_part_ready = sem("x_part_ready")
    job_full, hi_ready, qk_ready, v_ready = sem("job_full"), sem("hi_ready"), sem("qk_ready"), sem("v_ready")
    x_added = sem("x_added")
    sc_full, max_ready, diag_ready = sem("sc_full"), sem("max_ready"), sem("diag_ready")
    st_full, probs_ready = sem("st_full"), sem("probs_ready")
    ov_full, ln_ready, inv_ready, attn_ready = sem("ov_full"), sem("ln_ready"), sem("inv_ready"), sem("attn_ready")
    wo_full = sem("wo_full")

    def freed(job, part):
        kind, i = job
        if kind == "qk":
            return qk_ready, (part + 1) * C + i + 1
        if kind == "v":
            return v_ready, (part + 1) * (HG // 2) + i + 1
        return x_added, (part - 1) * 2 + i + 1

    def for_parts(eng, steps):
        steps(0, 0, False, True)
        with eng.Fori(0, (PARTS - 2) // 2) as r:
            steps(r * 2 + 1, 1, True, True)
            steps(r * 2 + 2, 0, True, True)
        steps(PARTS - 1, (PARTS - 1) % 2, True, False)

    with nc.Block() as block:
        @block.sync
        def _(sp):
            for q in range(4):
                sp.dma_start(x[:, 4 * q:4 * q + 4, :], t["x_in"][:, 4 * q:4 * q + 4, :]).then_inc(x_loaded, 16)
            sp.dma_start(ident[:], t["ident_in"]).then_inc(w_loaded, 16)
            sp.dma_start(w_raw[:, 0], t["wqT_in"]).then_inc(w_loaded, 16)
            sp.dma_start(w_raw[:, 1], t["wkT_in"]).then_inc(w_loaded, 16)
            sp.dma_start(wvT[:], t["wvT_in"]).then_inc(wv_loaded, 16)
            sp.dma_start(woT[:], t["woT_in"]).then_inc(wv_loaded, 16)

        @block.gpsimd
        def _(pool):
            pool.memset(ones_f[:], 1.0).then_inc(ones_ready, 1)
            pool.memset(values[:, :, :, 1, :], 1.0).then_inc(ones_ready, 1)
            pool.wait_ge(ones_ready, 2)
            pool.tensor_copy(ones[:], ones_f[:]).then_inc(ones_ready, 1)

            def part_of_x(part):
                at = bass.ds(part * PT, PT)
                pool.tensor_tensor(x_part[:], xnT_hi[:, at].bitcast(F32), xnT_lo[:, at].bitcast(F32),
                                   ALU.add).then_inc(x_part_ready, 1)

            def diagonal(g, gl):
                pool.wait_ge(max_ready, (g + 1) * KB)
                wait_for(pool, st_full, (g - 1) * KB)
                pool.tensor_tensor(diag[:, gl % 2], ident[:].rearrange("p (o d) -> p o d", o=1).broadcast_to([P, KB, P]),
                                   neg_max[:, gl % 4].rearrange("p (b o) -> p b o", o=1).broadcast_to([P, KB, P]),
                                   ALU.mult).then_inc(diag_ready, 1)

            def steps(part, slot, has_before, has_next):
                if has_next:
                    pool.wait_ge(v_ready, (part + 1) * (HG // 2))
                    part_of_x(part + 1)
                for gl in range(2, HG + 2 if has_next else HG):
                    diagonal(part * HG + gl, gl)

            pool.wait_ge(xnT_ready, 4)
            part_of_x(0)
            pool.wait_ge(w_loaded, 48)
            for g in range(2):
                diagonal(g, g)
            for_parts(pool, steps)

        @block.scalar
        def _(act):
            act.wait_ge(root_wanted, 1)
            act.activation(work[:, 2, :], work[:, 0, :], ACT.Sqrt).then_inc(root_ready, 1)
            act.wait_ge(w_loaded, 48)
            for w in range(2):
                act.activation(w_hi[:, w], w_raw[:, w].rearrange("p c (o d) -> p c o d", o=1).broadcast_to([P, C, 2, DH]),
                               ACT.Copy).then_inc(w_hi_ready, 1)
            round_tokens(act, pj, xnT_hi, xnT_full, xnT_hi_ready)

            def evacuate(job, slot, bank, part):
                kind, i = job
                if kind == "qk":
                    act.activation(qk[slot][:, :, :, i, :], pj[:, bank, :].rearrange("p (w g t) -> p w g t", w=2, g=HG),
                                   ACT.Copy).then_inc(hi_ready, 1)
                elif kind == "v":
                    act.activation(values[:, 2 * i:2 * i + 2, :, 0, :],
                                   pj[:, bank, :].rearrange("p (g b d) -> p g b d", g=2, b=KB),
                                   ACT.Copy).then_inc(v_ready, 1)

            def exponentials(m, ml):
                act.wait_ge(st_full, m + 1)
                act.activation(probs[:, ml % 4, :], st[:, ml % 2, :], ACT.Exp, scale=DH ** -0.5).then_inc(probs_ready, 1)

            def invert_sum(g, gl):
                act.wait_ge(ov_full, g + 1)
                act.activation(ln_sum[:], ov[DH:P, gl % 2, :], ACT.Ln).then_inc(ln_ready, 1)
                act.wait_ge(ln_ready, g + 1)
                act.activation(inv_sum[:, gl % 2, :], ln_sum[:], ACT.Exp, scale=-1.0).then_inc(inv_ready, 1)

            def steps(part, slot, has_before, has_next):
                jobs = jobs_of(has_before, has_next)
                order = list(jobs)
                for k in range(STEPS):
                    if k in jobs and jobs[k][0] != "wo":
                        act.wait_ge(job_full, jobs_before(part) + FIRST_JOBS.index(jobs[k]) + 1)
                        evacuate(jobs[k], 1 - slot, order.index(k) % 2, part)
                    if has_next or k + LAG_ST < STEPS:
                        exponentials(part * STEPS + k + LAG_ST, k + LAG_ST)
                    if k % KB == KB - 1:
                        invert_sum(part * HG + k // KB, k // KB)

            for n, job in enumerate(FIRST_JOBS):
                act.wait_ge(job_full, n + 1)
                evacuate(job, 0, n % 2, -1)
            for m in range(LAG_ST):
                exponentials(m, m)
            for_parts(act, steps)

        @block.vector
        def _(dve):
            chain = Chain(dve, dve_chain)
            dve.wait_ge(x_loaded, 64)
            normalize(dve, chain, x, stats, moments, rstd, work, xn, root_wanted, root_ready, xn_ready)
            for w in range(2):
                dve.wait_ge(w_hi_ready, w + 1)
                dve.tensor_tensor(w_lo[:, w], w_raw[:, w].rearrange("p c (o d) -> p c o d", o=1).broadcast_to([P, C, 2, DH]),
                                  w_hi[:, w].bitcast(F32), ALU.subtract).then_inc(w_ready, 1)
            token_rests(dve, pj, xnT_hi, xnT_lo, xnT_hi_ready, xnT_ready)

            def maximum(m, ml):
                dve.wait_ge(sc_full, m + 1)
                dve.tensor_reduce(neg_max[:, ml // KB % 4, ml % KB:ml % KB + 1], sc[:, ml % 2, :], AX.X, ALU.max,
                                  negate=True).then_inc(max_ready, 1)

            def rest(job, slot, bank, part):
                kind, i = job
                half = pj[:, bank, :].rearrange("p (w g t) -> p w g t", w=2, g=HG)
                if kind == "qk":
                    dve.wait_ge(hi_ready, (part + 1) * C + i + 1)
                    dve.tensor_tensor(q_lo[slot][:, :, i, :], half[:, 0], qk[slot][:, 0, :, i, :].bitcast(F32),
                                      ALU.subtract)
                    k_lo = qk[slot][DH:P, 1, :, i, :]
                    dve.tensor_tensor(k_lo, half[DH:P, 1], k_lo.bitcast(F32), ALU.subtract).then_inc(qk_ready, 1)
                elif kind == "wo":
                    dve.wait_ge(wo_full, (part - 1) * 2 + i + 1)
                    tile = bass.ds((part - 1) * 2 + i, 1)
                    dve.tensor_tensor(x[:, tile, :], x[:, tile, :], pj[:, bank, 0:D].rearrange("p (o d) -> p o d", o=1),
                                      ALU.add).then_inc(x_added, 1)

            def divide(g, gl):
                dve.wait_ge(inv_ready, g + 1)
                for odd in range(2):
                    view = lambda a: a.rearrange("p (c t) -> p c t", c=C)[:, odd::2, :]
                    out = dve.tensor_tensor(attn[DH * odd:DH * odd + DH, :, gl * GT:(gl + 1) * GT],
                                            view(ov[0:DH, gl % 2, :]), view(inv_sum[:, gl % 2, :]), ALU.mult)
                out.then_inc(attn_ready, 1)

            def steps(part, slot, has_before, has_next):
                jobs = jobs_of(has_before, has_next)
                order = list(jobs)
                for k in range(STEPS):
                    if has_next or k + LAG_SM < STEPS:
                        maximum(part * STEPS + k + LAG_SM, k + LAG_SM)
                    if k in jobs:
                        rest(jobs[k], 1 - slot, order.index(k) % 2, part)
                    if k % KB == KB - 1:
                        if k == KB - 1:
                            wait_for(dve, wo_full, part * 2)
                        divide(part * HG + k // KB, k // KB)

            for n, job in enumerate(FIRST_JOBS):
                rest(job, 0, n % 2, -1)
            for m in range(LAG_SM):
                maximum(m, m)
            for_parts(dve, steps)
            for i in range(2):
                rest(("wo", i), 0, i, PARTS)

        @block.tensor
        def _(pe):
            pe.wait_ge(w_loaded, 48)
            transpose_tokens(pe, xn, ident, pj, xn_ready, xnT_full, xnT_ready)

            def project(job, target, bank, free, part):
                kind, i = job
                if free is not None:
                    wait_for(pe, *free)
                if kind == "qk":
                    at = bass.ds(target * PT, PT)
                    for w in range(2):
                        out = pj[:, bank, w * PT:(w + 1) * PT]
                        hi = w_hi[:, w, i].rearrange("p o d -> p (o d)")
                        lo = w_lo[:, w, i].rearrange("p o d -> p (o d)")
                        pe.matmul(out, hi, xnT_hi[:, at], start=True, stop=False)
                        pe.matmul(out, hi, xnT_lo[:, at], start=False, stop=False)
                        last = pe.matmul(out, lo, xnT_hi[:, at], start=False, stop=True)
                elif kind == "v":
                    if i == 0:
                        pe.wait_ge(x_part_ready, target + 1)
                    wv = wvT[:].rearrange("p (b j d) -> p b j d", b=KB, j=4)
                    for e in range(2):
                        gl = 2 * i + e
                        for j in range(4):
                            last = pe.matmul(pj[GT * j:GT * j + GT, bank, e * 256:(e + 1) * 256],
                                             x_part[:, gl * GT:(gl + 1) * GT], wv[:, :, j, :], start=True, stop=True)
                else:
                    pe.wait_ge(attn_ready, (target + 1) * HG)
                    for c in range(C // 2):
                        last = pe.matmul(pj[:, bank, 0:D], attn[:, c, i * P:(i + 1) * P], woT[:, c, :],
                                         start=(c == 0), stop=(c == C // 2 - 1))
                    last.then_inc(wo_full, 1)
                    return
                last.then_inc(job_full, 1)

            def scores(m, ml, slot):
                b, g = ml % KB, ml // KB % HG
                wait_for(pe, max_ready, m - 1)
                flat = lambda w: qk[slot][:, w, g].rearrange("p c t -> p (c t)")
                pe.matmul(sc[:, ml % 2, :], flat(0)[:, b * P:(b + 1) * P], flat(1), start=True, stop=True)\
                  .then_inc(sc_full, 1)

            def weighted(m, ml, g):
                b, gl = ml % KB, ml // KB
                pe.wait_ge(probs_ready, m + 1)
                if b == 0:
                    wait_for(pe, attn_ready, g - 1)
                last = pe.matmul(ov[:, gl % 2, :], values[:, gl, b].rearrange("p o d -> p (o d)"),
                                 probs[:, ml % 4, :], start=(b == 0), stop=(b == KB - 1))
                if b == KB - 1:
                    last.then_inc(ov_full, 1)

            def scores_t_of(part, k, slot):
                b = k % KB
                g_of = k // KB % HG
                s = slot if k < STEPS else 1 - slot
                flat = lambda w: qk[s][:, w, g_of].rearrange("p c t -> p (c t)")
                keys = flat(1)[:, b * P:(b + 1) * P]
                out = st[:, k % 2, :]
                pe.matmul(out, keys, flat(0), start=True, stop=False)
                pe.matmul(out, keys, q_lo[s][:, g_of].rearrange("p c t -> p (c t)"), start=False, stop=False)
                if b == 0:
                    pe.wait_ge(diag_ready, part * HG + k // KB + 1)
                pe.matmul(out, ones[:], diag[:, k // KB % 2].rearrange("p b q -> p (b q)"), start=False, stop=True)\
                  .then_inc(st_full, 1)

            def steps(part, slot, has_before, has_next):
                jobs = jobs_of(has_before, has_next)
                order = list(jobs)
                for k in range(STEPS):
                    if k == 0:
                        pe.wait_ge(v_ready, (part + 1) * (HG // 2))
                    weighted(part * STEPS + k, k, part * HG + k // KB)
                    if has_next or k + LAG_ST < STEPS:
                        scores_t_of(part, k + LAG_ST, slot)
                    if has_next or k + LAG_SM < STEPS:
                        ahead = k + LAG_SM
                        if ahead == STEPS:
                            pe.wait_ge(qk_ready, (part + 2) * C)
                        scores(part * STEPS + ahead, ahead, slot if ahead < STEPS else 1 - slot)
                    if k in jobs:
                        n = order.index(k)
                        free = (freed(jobs[order[n - 2]], part) if n >= 2 else
                                freed(("v", HG // 2 - 2 + n), part - 1))
                        target = part - 1 if jobs[k][0] == "wo" else part + 1
                        project(jobs[k], target, n % 2, free, part)

            pe.wait_ge(w_ready, 2)
            pe.wait_ge(xnT_ready, 4)
            pe.wait_ge(wv_loaded, 32)
            for n, job in enumerate(FIRST_JOBS):
                project(job, 0, n % 2, freed(FIRST_JOBS[n - 2], -1) if n >= 2 else None, -1)
            pe.wait_ge(qk_ready, C)
            pe.wait_ge(ones_ready, 3)
            for m in range(LAG_SM):
                scores(m, m, 0)
            for m in range(LAG_ST):
                scores_t_of(0, m, 0)
            for_parts(pe, steps)
            for i in range(2):
                project(("wo", i), PARTS - 1, i, freed(("wo", i), PARTS - 1), PARTS)


PREP = [("v", 0, (0,)), ("v", 1, (1,)), ("v", 2, (2,)), ("q", 0, (0,)), ("wo", 0, (1,)),
        ("max", 0, (0, 1, 2)), ("max", 1, (0, 1, 2)), ("max", 2, (0, 1, 2)), ("max", 3, (0, 1, 2)), ("turn", 0, (0,))]
V_CHUNKS = [range(0, 4), range(4, 8), range(8, XC)]
MAX_HEADS = [range(0, 6), range(6, 12), range(12, 16)]


def prepare_plan():
    plan, reader = [], {}
    for round_ in range(-1, B + 1):
        for kind, i, banks in PREP:
            batch = round_ - 1 if kind == "wo" else round_ + 1
            if 0 <= batch < B:
                needs = max([reader[b] + 1 for b in banks if b in reader], default=0)
                for b in banks:
                    reader[b] = len(plan)
                plan.append((kind, i, batch, banks, needs, round_))
    return plan


PLAN = prepare_plan()


def rows_of(j):
    return P if j < XC - 1 else XL


def cross_attention(nc, sb, psum, sem, t):
    x, ident = t["x"], t["ident"]
    xn = sb("xn2", [P, NT, D], F32)
    xnT_hi, xnT_lo = sb("xnT2_hi", [P, B * S], F32R), sb("xnT2_lo", [P, B * S], F32R)
    stats, moments = sb("stats2", [P, NT, 6], F32), sb("moments2", [P, NT, 2], F32)
    rstd, work = sb("rstd2", [P, 2, NT], F32), sb("work2", [P, 3, NT], F32)
    wqT, wkT, wvT, woT = (sb(f"x{n}", [P, D], F32) for n in ("wqT", "wkT", "wvT", "woT"))
    wq_hi, wq_lo = sb("xwq_hi", [P, D], F32R), sb("xwq_lo", [P, D], F32R)
    bias = sb("xbias", [P, 3], F32)
    bo = sb("bo", [P, D], F32)
    ctxT = sb("ctxT", [P, B, XK], F32)
    ctx_rep = sb("ctx_rep", [P, B, XF], F32)
    ctx_sum, v_sum = sb("ctx_sum", [P, B], F32), sb("v_sum", [P, B], F32)
    own_head = sb("own_head", [P, XC, D], F32)
    head_row, head_row_r = sb("head_row", [XH, XF], F32), sb("head_row_r", [XH, XF], F32R)
    head_col = sb("head_col", [P, XH], F32)
    k_all = sb("k_all", [P, B, XK], F32)
    k_hi, k_lo = sb("k_hi", [P, B, XK], F32R), sb("k_lo", [P, B, XK], F32R)
    keys_hi, keys_lo = sb("keys_hi", [P, 2, XH, XK], F32R), sb("keys_lo", [P, 2, XH, XK], F32R)
    vals = sb("vals", [P, 2, XC, D], F32)
    q_hi, q_lo = sb("q2_hi", [P, 2, S], F32R), sb("q2_lo", [P, 2, S], F32R)
    neg_max, neg_maxT = sb("neg_max2", [P, 4, XH], F32), sb("neg_maxT", [XH, 2, S], F32R)
    thr = sb("thr", [XH, 6], F32)
    thr_col = sb("thr_col", [P, XC], F32)
    mask = sb("mask", [P, 3, S], mybir.dt.bfloat16)
    e, p = sb("e", [P, 3, S], F32), sb("p", [P, 3, S], F32)
    none, total, inv, num = (sb(n, [P, S], F32) for n in ("none", "total", "inv", "num"))
    out_T = sb("out_T", [P, S], F32)

    sc = psum("scores2", [P, 3, S], F32)
    pb = psum("prepare", [P, 3, S], F32)
    ov, z = psum("out2", [P, S], F32), psum("sum2", [P, S], F32)

    w_in, c_in, h_in, rep_in = sem("xw_loaded"), sem("ctx_loaded"), sem("heads_loaded"), sem("rep_loaded")
    root_wanted, root_ready, dve_chain = sem("root_wanted2"), sem("root_ready2"), sem("dve_chain2")
    xn_ready, xnT_full, xnT_hi_ready, xnT_ready = sem("xn_ready2"), sem("xnT_full2"), sem("xnT_hi_ready2"), sem("xnT_ready2")
    w_hi_ready, w_ready, head_row_ready = sem("xw_hi_ready"), sem("xw_ready"), sem("head_row_ready")
    sum_ready, first_full, k_ready, k_hi_ready, k_split = sem("sum_ready"), sem("first_full"), sem("k_ready"), sem("k_hi_ready"), sem("k_split")
    thr_step, thr_done, thr_full, setup_read = sem("thr_step"), sem("thr_done"), sem("thr_full"), sem("setup_read")
    bo_added, keys_ready = sem("bo_added"), sem("keys_ready")
    prep_full, prep_read, q_hi_ready = sem("prep_full"), sem("prep_read"), sem("q2_hi_ready")
    raw_full, mask_ready, shifted, e_ready, p_ready = sem("raw_full"), sem("mask_ready"), sem("shifted"), sem("e_ready"), sem("p_ready")
    group_read, num_ready, outT_ready = sem("group_read"), sem("num_ready"), sem("outT_ready")
    chunk_done = sem("chunk_done")

    index = {(kind, i, batch): n for n, (kind, i, batch, *_) in enumerate(PLAN)}
    cuts = [slice(h.start, h.stop) for h in MAX_HEADS]

    def prep_of(round_):
        return [(n, *j[:4], j[4]) for n, j in enumerate(PLAN) if j[5] == round_]

    with nc.Block() as block:
        @block.sync
        def _(sp):
            for dst, src in ((wqT, "xwqT_in"), (wkT, "xwkT_in"), (wvT, "xwvT_in"), (woT, "xwoT_in"), (bias, "xbias_in")):
                sp.dma_start(dst[:], t[src]).then_inc(w_in, 16)
            sp.dma_start(ctxT[:], t["ctxT_in"]).then_inc(c_in, 16)
            sp.dma_start(thr[:, 0:1], t["thr_in"]).then_inc(c_in, 16)
            sp.dma_start(head_row[:], t["head_row_in"]).then_inc(h_in, 16)
            sp.dma_start(head_col[:], t["head_col_in"]).then_inc(h_in, 16)
            sp.dma_start(bo[:], t["bo_in"].partition_broadcast(P)).then_inc(h_in, 16)
            sp.dma_start(own_head[:], t["own_head_in"]).then_inc(h_in, 16)
            for b in range(B):
                src = t["ctxT_in"][:, b, :].rearrange("p (o k) -> p o k", o=1).broadcast_to([P, XH, XK])
                sp.dma_start(ctx_rep[:, b, :].rearrange("p (h k) -> p h k", h=XH), src).then_inc(rep_in, 16)

        @block.gpsimd
        def _(pool):
            def keys(b, part):
                w, half = part // 2, slice(8 * (part % 2), 8 * (part % 2) + 8)
                src, dst = ((k_hi, keys_hi), (k_lo, keys_lo))[w]
                pool.tensor_tensor(dst[:, b % 2, half, :],
                                   src[:, b, :].bitcast(F32).rearrange("p (o k) -> p o k", o=1).broadcast_to([P, 8, XK]),
                                   head_col[:, half].rearrange("p (h o) -> p h o", o=1).broadcast_to([P, 8, XK]),
                                   ALU.mult).then_inc(keys_ready, 1)

            pool.wait_ge(h_in, 64)
            pool.wait_ge(k_split, 1)
            for part in range(4):
                keys(0, part)
            pool.wait_ge(xn_ready, 1)
            pool.tensor_tensor(x[:], x[:], bo[:].rearrange("p (o d) -> p o d", o=1).broadcast_to([P, NT, D]),
                               ALU.add).then_inc(bo_added, 1)
            for b in range(B):
                for j in range(XC):
                    n, r = b * XC + j, rows_of(j)
                    if 1 <= j < 5 and b + 1 < B:
                        keys(b + 1, j - 1)
                    pool.wait_ge(e_ready, n + 1)
                    wait_for(pool, chunk_done, n - 2)
                    pool.tensor_tensor(p[0:r, n % 3], e[0:r, n % 3], mask[0:r, n % 3], ALU.mult).then_inc(p_ready, 1)

        @block.scalar
        def _(act):
            act.wait_ge(thr_done, 2)
            act.activation(thr[:, 3:4], thr[:, 2:3], ACT.Exp).then_inc(thr_step, 1)
            act.wait_ge(thr_step, 1)
            act.activation(thr[:, 4:5], thr[:, 3:4], ACT.Ln, bias=1.0).then_inc(thr_step, 1)
            act.wait_ge(root_wanted, 1)
            act.activation(work[:, 2, :], work[:, 0, :], ACT.Sqrt).then_inc(root_ready, 1)
            act.wait_ge(w_in, 80)
            act.activation(wq_hi[:], wqT[:], ACT.Copy).then_inc(w_hi_ready, 1)
            act.wait_ge(h_in, 64)
            act.activation(head_row_r[:], head_row[:], ACT.Copy).then_inc(head_row_ready, 1)
            act.wait_ge(k_ready, 1)
            act.activation(k_hi[:], k_all[:], ACT.Copy).then_inc(k_hi_ready, 1)
            act.wait_ge(setup_read, 1)
            round_tokens(act, pb, xnT_hi, xnT_full, xnT_hi_ready)

            def q_high(n, b):
                act.wait_ge(prep_full, n + 1)
                act.activation(q_hi[:, b % 2, :], pb[:, 0, :], ACT.Identity, bias=bias[:, 0:1]).then_inc(q_hi_ready, 1)

            for round_ in range(-1, B):
                if round_ >= 0:
                    for j in range(XC):
                        n, r = round_ * XC + j, rows_of(j)
                        if j == 4 and round_ + 1 < B:
                            q_high(index["q", 0, round_ + 1], round_ + 1)
                        act.wait_ge(shifted, n + 1)
                        wait_for(act, p_ready, n - 2)
                        act.activation(e[0:r, n % 3], sc[0:r, n % 3], ACT.Exp, scale=XD ** -0.5).then_inc(e_ready, 1)
                    act.wait_ge(num_ready, round_ + 1)
                    act.activation(out_T[:], num[:], ACT.Identity, bias=bias[:, 2:3]).then_inc(outT_ready, 1)
                else:
                    q_high(index["q", 0, 0], 0)

        @block.vector
        def _(dve):
            chain = Chain(dve, dve_chain)
            dve.wait_ge(c_in, 32)
            chain.link(dve.tensor_scalar(thr[:, 1:2], thr[:, 0:1], -1.0, None, ALU.mult))
            dve.tensor_reduce(ctx_sum[:], ctxT[:], AX.X, ALU.add).then_inc(sum_ready, 1)
            chain.wait()
            dve.tensor_tensor(thr[:, 2:3], thr[:, 0:1], thr[:, 1:2], ALU.min).then_inc(thr_done, 1)
            dve.tensor_scalar(thr[:, 5:6], thr[:, 0:1], 0.0, None, ALU.max).then_inc(thr_done, 1)
            normalize(dve, chain, x, stats, moments, rstd, work, xn, root_wanted, root_ready, xn_ready)
            dve.wait_ge(thr_done, 2)
            dve.wait_ge(thr_step, 2)
            chain.link(dve.tensor_tensor(thr[:, 1:2], thr[:, 4:5], thr[:, 5:6], ALU.add))
            chain.wait()
            dve.tensor_scalar(thr[:, 0:1], thr[:, 1:2], XD ** 0.5, None, ALU.mult).then_inc(thr_done, 1)
            dve.wait_ge(first_full, 1)
            dve.wait_ge(w_in, 80)
            dve.tensor_scalar(k_all[:].rearrange("p b k -> p (b k)"), pb[:, 0, 0:B * XK], bias[:, 1:2], None,
                              ALU.add).then_inc(k_ready, 1)
            dve.tensor_copy(v_sum[:], pb[:, 1, 0:B])
            dve.wait_ge(w_hi_ready, 1)
            dve.tensor_tensor(wq_lo[:], wqT[:], wq_hi[:].bitcast(F32), ALU.subtract).then_inc(w_ready, 1)
            dve.wait_ge(k_ready, 1)
            dve.wait_ge(k_hi_ready, 1)
            dve.tensor_tensor(k_lo[:], k_all[:], k_hi[:].bitcast(F32), ALU.subtract).then_inc(k_split, 1)
            dve.wait_ge(thr_full, 1)
            dve.tensor_copy(thr_col[:, 0:XC - 1], pb[:, 2, 0:XC - 1])
            dve.tensor_copy(thr_col[0:XL, XC - 1:XC], pb[0:XL, 2, XC - 1:XC]).then_inc(setup_read, 1)
            dve.wait_ge(setup_read, 1)
            token_rests(dve, pb, xnT_hi, xnT_lo, xnT_hi_ready, xnT_ready)

            def read(n, kind, i, b, banks):
                dve.wait_ge(prep_full, n + 1)
                if kind == "q":
                    dve.wait_ge(q_hi_ready, b + 1)
                    last = dve.scalar_tensor_tensor(out=q_lo[:, b % 2, :], in0=pb[:, 0, :], scalar=bias[:, 0:1],
                                                    in1=q_hi[:, b % 2, :].bitcast(F32), op0=ALU.add, op1=ALU.subtract)
                elif kind == "v":
                    js = V_CHUNKS[i]
                    full = min(js.stop, XC - 1)
                    last = dve.tensor_tensor(vals[:, b % 2, js.start:full, :],
                                             pb[:, banks[0], 0:(full - js.start) * D].rearrange("p (j d) -> p j d", d=D),
                                             own_head[:, js.start:full, :], ALU.mult)
                    if full < js.stop:
                        last = dve.tensor_tensor(vals[0:XL, b % 2, full, :], pb[0:XL, banks[0], (full - js.start) * D:][:, 0:D],
                                                 own_head[0:XL, full, :], ALU.mult)
                elif kind == "max":
                    for c, heads in enumerate(cuts):
                        w = (heads.stop - heads.start) * XK
                        last = dve.tensor_reduce(neg_max[:, i, heads], pb[:, c, 0:w].rearrange("p (h k) -> p h k", k=XK),
                                                 AX.X, ALU.max, negate=True)
                elif kind == "turn":
                    last = dve.tensor_copy(neg_maxT[:, b % 2, :], pb[0:XH, 0, :])
                else:
                    if b == 0:
                        dve.wait_ge(bo_added, 1)
                    last = dve.tensor_tensor(x[:, 4 * b:4 * b + 4, :], x[:, 4 * b:4 * b + 4, :],
                                             pb[:, banks[0], :].rearrange("p (t d) -> p t d", t=4), ALU.add)
                last.then_inc(prep_read, 1)

            def finish(b):
                dve.wait_ge(chunk_done, (b + 1) * XC)
                chain.link(dve.tensor_scalar(none[:], z[:], 0.0, None, ALU.is_equal))
                chain.wait()
                chain.link(dve.scalar_tensor_tensor(out=total[:], in0=none[:], scalar=float(XK), in1=z[:],
                                                    op0=ALU.mult, op1=ALU.add))
                wait_for(dve, outT_ready, b)
                dve.scalar_tensor_tensor(out=num[:], in0=none[:], scalar=v_sum[:, b:b + 1], in1=ov[:],
                                         op0=ALU.mult, op1=ALU.add).then_inc(group_read, 1)
                chain.wait()
                chain.link(dve.reciprocal(inv[:], total[:]))
                chain.wait()
                dve.wait_ge(group_read, b + 1)
                dve.tensor_tensor(num[:], num[:], inv[:], ALU.mult).then_inc(num_ready, 1)

            for n, kind, i, b, banks, _ in prep_of(-1):
                read(n, kind, i, b, banks)
            for round_ in range(B + 1):
                jobs = prep_of(round_)
                for j in range(XC if round_ < B else 0):
                    n, r = round_ * XC + j, rows_of(j)
                    dve.wait_ge(raw_full, n + 1)
                    wait_for(dve, p_ready, n - 2)
                    dve.tensor_scalar(mask[0:r, n % 3], sc[0:r, n % 3], thr_col[0:r, j:j + 1], None,
                                      ALU.is_gt).then_inc(mask_ready, 1)
                    for n_, kind, i, b, banks, _ in jobs:
                        if PREP.index((kind, i, banks)) == j:
                            read(n_, kind, i, b, banks)
                if round_ < B:
                    finish(round_)
                else:
                    for n_, kind, i, b, banks, _ in jobs:
                        read(n_, kind, i, b, banks)

        @block.tensor
        def _(pe):
            pe.wait_ge(w_in, 80)
            pe.wait_ge(c_in, 32)
            pe.wait_ge(h_in, 64)
            pe.wait_ge(sum_ready, 1)
            pe.matmul(pb[:, 0, 0:B * XK], wkT[:], ctxT[:].rearrange("p b k -> p (b k)"), start=True, stop=True)
            pe.matmul(pb[:, 1, 0:B], wvT[:], ctx_sum[:], start=True, stop=True).then_inc(first_full, 1)
            pe.wait_ge(thr_done, 3)
            for j in range(XC):
                r = rows_of(j)
                last = pe.matmul(pb[0:r, 2, j:j + 1], head_row[:, j * P:j * P + r], thr[:, 0:1], start=True, stop=True)
            last.then_inc(thr_full, 1)
            pe.wait_ge(setup_read, 1)
            transpose_tokens(pe, xn, ident, pb, xn_ready, xnT_full, xnT_ready)

            def prepare(n, kind, i, b, banks, needs):
                wait_for(pe, prep_read, needs)
                if kind == "q":
                    if b == 0:
                        pe.wait_ge(w_ready, 1)
                    at = slice(b * S, (b + 1) * S)
                    pe.matmul(pb[:, 0, :], wq_hi[:], xnT_hi[:, at], start=True, stop=False)
                    pe.matmul(pb[:, 0, :], wq_hi[:], xnT_lo[:, at], start=False, stop=False)
                    last = pe.matmul(pb[:, 0, :], wq_lo[:], xnT_hi[:, at], start=False, stop=True)
                elif kind == "v":
                    if i == 0:
                        pe.wait_ge(rep_in, 64)
                    for c, j in enumerate(V_CHUNKS[i]):
                        r = rows_of(j)
                        last = pe.matmul(pb[0:r, banks[0], c * D:(c + 1) * D], ctx_rep[:, b, j * P:j * P + r], wvT[:],
                                         start=True, stop=True)
                elif kind == "max":
                    if i == 0:
                        pe.wait_ge(q_hi_ready, b + 1)
                        pe.wait_ge(keys_ready, 4 * b + 4)
                    for c, heads in enumerate(cuts):
                        w = (heads.stop - heads.start) * XK
                        last = pe.matmul(pb[:, c, 0:w], q_hi[:, b % 2, i * P:(i + 1) * P],
                                         keys_hi[:, b % 2, heads, :].rearrange("p h k -> p (h k)"), start=True, stop=True)
                elif kind == "turn":
                    pe.wait_ge(prep_read, index["max", 3, b] + 1)
                    for i in range(4):
                        last = pe.transpose(pb[0:XH, 0, i * P:(i + 1) * P], neg_max[:, i, :], ident[:])
                else:
                    pe.wait_ge(outT_ready, b + 1)
                    for i in range(4):
                        last = pe.matmul(pb[:, banks[0], i * D:(i + 1) * D], out_T[:, i * P:(i + 1) * P], woT[:],
                                         start=True, stop=True)
                last.then_inc(prep_full, 1)

            flat = lambda a, b: a[:, b % 2].rearrange("p h k -> p (h k)")

            def raw(b, j):
                n, r = b * XC + j, rows_of(j)
                cut = slice(j * P, j * P + r)
                wait_for(pe, e_ready, n - 2)
                if j == 0:
                    pe.wait_ge(prep_read, index["turn", 0, b] + 1)
                out = sc[0:r, n % 3, :]
                pe.matmul(out, flat(keys_hi, b)[:, cut], q_hi[:, b % 2, :], start=True, stop=False)
                pe.matmul(out, flat(keys_hi, b)[:, cut], q_lo[:, b % 2, :], start=False, stop=False)
                pe.matmul(out, flat(keys_lo, b)[:, cut], q_hi[:, b % 2, :], start=False, stop=True).then_inc(raw_full, 1)

            def shift(b, j):
                n, r = b * XC + j, rows_of(j)
                pe.wait_ge(mask_ready, n + 1)
                pe.matmul(sc[0:r, n % 3, :], head_row_r[:, j * P:j * P + r], neg_maxT[:, b % 2, :], start=False,
                          stop=True, skip_group_check=True).then_inc(shifted, 1)

            def weighted(b, j):
                n, r = b * XC + j, rows_of(j)
                pe.wait_ge(p_ready, n + 1)
                if j == 0:
                    wait_for(pe, group_read, b)
                pe.matmul(ov[:], vals[0:r, b % 2, j, :], p[0:r, n % 3, :], start=(j == 0), stop=(j == XC - 1))
                last = pe.matmul(z[:], own_head[0:r, j, :], p[0:r, n % 3, :], start=(j == 0), stop=(j == XC - 1))
                last.then_inc(chunk_done, 1)

            pe.wait_ge(xnT_ready, 4)
            for job in prep_of(-1):
                prepare(*job)
            pe.wait_ge(head_row_ready, 1)
            for b in range(B):
                for j in range(XC + 2):
                    if j < XC:
                        raw(b, j)
                        for job in prep_of(b):
                            if PREP.index((job[1], job[2], job[4])) == j:
                                prepare(*job)
                    if 1 <= j <= XC:
                        shift(b, j - 1)
                    if j >= 2:
                        weighted(b, j - 2)
            for job in prep_of(B):
                prepare(*job)


def mixture(nc, sb, psum, sem, t):
    x, ident = t["x"], t["ident"]
    xn = sb("xn3", [P, NT, D], F32)
    xnT_hi, xnT_lo = sb("xnT3_hi", [P, B * S], F32R), sb("xnT3_lo", [P, B * S], F32R)
    stats, moments = sb("stats3", [P, NT, 6], F32), sb("moments3", [P, NT, 2], F32)
    rstd, work = sb("rstd3", [P, 2, NT], F32), sb("work3", [P, 3, NT], F32)
    up = sb("up", [P, E + 1, 2, HID], F32)
    up_hi, up_lo = sb("up_hi", [P, E + 1, 2, HID], F32R), sb("up_lo", [P, E + 1, 2, HID], F32R)
    down = sb("down", [P, HC, D], F32)
    router, router_hi, router_lo = sb("router", [P, E], F32), sb("router_hi", [P, E], F32R), sb("router_lo", [P, E], F32R)
    route_bias, expert_no = sb("route_bias", [P, E], F32), sb("expert_no", [P, E], F32)
    logits, top, place = sb("logits", [P, NT, E], F32), sb("top", [P, NT, 8], F32), sb("place", [P, NT, 8], U32)
    place_f = sb("place_f", [P, NT, 2], F32)
    gap, gap_e, weight = sb("gap", [P, NT], F32), sb("gap_e", [P, 2, NT], F32), sb("weight", [P, 2, NT], F32)
    hit, cw = sb("hit", [P, 2, NT, E], F32), sb("cw", [P, NT, E], F32)
    gate = sb("gate", [P, 3, S], F32)
    hidden = sb("hidden", [P, 3, S], F32)

    g, u, y = psum("g", [P, 3, S], F32), psum("u", [P, 3, S], F32), psum("y", [P, 2, S], F32)

    w_in, router_in, up_in = sem("down_loaded"), sem("router_loaded"), sem("up_loaded")
    root_wanted, root_ready, dve_chain = sem("root_wanted3"), sem("root_ready3"), sem("dve_chain3")
    xn_ready, xnT_full, xnT_hi_ready, xnT_ready = sem("xn_ready3"), sem("xnT_full3"), sem("xnT_hi_ready3"), sem("xnT_ready3")
    router_hi_ready, router_ready, up_hi_ready, up_ready = sem("router_hi_ready"), sem("router_ready"), sem("up_hi_ready"), sem("up_ready")
    logits_full, gap_ready, gap_e_ready, cw_ready = sem("logits_full"), sem("gap_ready"), sem("gap_e_ready"), sem("cw_ready")
    gu_full, gate_ready, hidden_ready = sem("gu_full"), sem("gate_ready"), sem("hidden_ready")
    y_full, y_added, stored = sem("y_full"), sem("y_added"), sem("stored")
    NE = E + 1

    with nc.Block() as block:
        @block.sync
        def _(sp):
            sp.dma_start(router[:], t["router_in"]).then_inc(router_in, 16)
            sp.dma_start(route_bias[:], t["route_bias_in"].partition_broadcast(P)).then_inc(router_in, 16)
            sp.dma_start(expert_no[:], t["expert_no_in"].partition_broadcast(P)).then_inc(router_in, 16)
            for w in range(2):
                sp.dma_start(up[:, 0:E, w, :], t[f"up{w}_in"]).then_inc(up_in, 16)
                sp.dma_start(up[:, E, w, :], t[f"shared{w}_in"]).then_inc(up_in, 16)
            sp.dma_start(down[:, 0:2 * E, :], t["down_in"]).then_inc(w_in, 16)
            sp.dma_start(down[:, 2 * E:HC, :], t["shared_down_in"]).then_inc(w_in, 16)
            with sp.Fori(0, B) as b:
                sp.wait_ge(y_added, (b + 1) * NE)
                sp.dma_start(t["out"][:, bass.ds(b * 4, 4), :], x[:, bass.ds(b * 4, 4), :]).then_inc(stored, 16)
            sp.wait_ge(stored, 16 * B)

        @block.gpsimd
        def _(pool):
            pass

        @block.scalar
        def _(act):
            act.wait_ge(root_wanted, 1)
            act.activation(work[:, 2, :], work[:, 0, :], ACT.Sqrt).then_inc(root_ready, 1)
            act.wait_ge(router_in, 48)
            act.activation(router_hi[:], router[:], ACT.Copy).then_inc(router_hi_ready, 1)
            act.wait_ge(up_in, 64)
            for n in range(NE):
                act.activation(up_hi[:, n], up[:, n], ACT.Copy).then_inc(up_hi_ready, 1)
            round_tokens(act, g, xnT_hi, xnT_full, xnT_hi_ready)
            act.wait_ge(gap_ready, 1)
            act.activation(gap_e[:, 0, :], gap[:], ACT.Exp).then_inc(gap_e_ready, 1)
            with act.Fori(0, B) as b:
                for c in range(HC):
                    n = b * HC + c
                    act.wait_ge(gu_full, n + 1)
                    act.activation(gate[:, c % 3, :], g[:, c % 3, :], ACT.Silu).then_inc(gate_ready, 1)

        @block.vector
        def _(dve):
            chain = Chain(dve, dve_chain)
            normalize(dve, chain, x, stats, moments, rstd, work, xn, root_wanted, root_ready, xn_ready)
            dve.wait_ge(router_hi_ready, 1)
            dve.tensor_tensor(router_lo[:], router[:], router_hi[:].bitcast(F32), ALU.subtract).then_inc(router_ready, 1)
            token_rests(dve, g, xnT_hi, xnT_lo, xnT_hi_ready, xnT_ready)
            for n in range(NE):
                dve.wait_ge(up_hi_ready, n + 1)
                dve.tensor_tensor(up_lo[:, n], up[:, n], up_hi[:, n].bitcast(F32), ALU.subtract).then_inc(up_ready, 1)
            row = lambda a: a.rearrange("p (o e) -> p o e", o=1).broadcast_to([P, NT, E])
            col = lambda a: a.rearrange("p (t o) -> p t o", o=1).broadcast_to([P, NT, E])
            dve.wait_ge(logits_full, 1)
            chain.link(dve.tensor_tensor(logits[:], y[:, 0, 0:NT * E].rearrange("p (t e) -> p t e", e=E),
                                         row(route_bias[:]), ALU.add))
            chain.wait()
            for i in range(NT):
                chain.link(dve.max(top[:, i, :], logits[:, i, :]))
            chain.wait()
            dve.tensor_tensor(gap[:], top[:, :, 1], top[:, :, 0], ALU.subtract).then_inc(gap_ready, 1)
            for i in range(NT):
                chain.link(dve.max_index(place[:, i, :], top[:, i, :], logits[:, i, :]))
            chain.wait()
            chain.link(dve.tensor_copy(place_f[:], place[:, :, 0:2]))
            dve.wait_ge(gap_e_ready, 1)
            chain.link(dve.tensor_scalar(gap_e[:, 1, :], gap_e[:, 0, :], 1.0, None, ALU.add))
            chain.wait()
            chain.link(dve.reciprocal(weight[:, 0, :], gap_e[:, 1, :]))
            chain.wait()
            chain.link(dve.tensor_tensor(weight[:, 1, :], weight[:, 0, :], gap_e[:, 0, :], ALU.mult))
            for i in range(2):
                chain.link(dve.tensor_tensor(hit[:, i], row(expert_no[:]), col(place_f[:, :, i]), ALU.is_equal))
            chain.wait()
            for i in range(2):
                chain.link(dve.tensor_tensor(hit[:, i], hit[:, i], col(weight[:, i, :]), ALU.mult))
            chain.wait()
            dve.tensor_tensor(cw[:], hit[:, 0], hit[:, 1], ALU.add).then_inc(cw_ready, 1)
            dve.wait_ge(cw_ready, 1)
            with dve.Fori(0, B) as b:
                def add(e):
                    dve.wait_ge(y_full, b * NE + e + 1)
                    tiles = bass.ds(b * 4, 4)
                    if e > 0:
                        dve.wait_ge(y_added, b * NE + e)
                    if e == E:
                        last = dve.tensor_tensor(x[:, tiles, :], x[:, tiles, :],
                                                 y[:, e % 2, :].rearrange("p (t d) -> p t d", t=4), ALU.add)
                    else:
                        for i in range(4):
                            tile = bass.ds(b * 4 + i, 1)
                            rows = x[:, tile, :].rearrange("p o d -> p (o d)")
                            last = dve.scalar_tensor_tensor(out=rows, in0=y[:, e % 2, i * D:(i + 1) * D],
                                                            scalar=cw[:, tile, e:e + 1].rearrange("p o e -> p (o e)"),
                                                            in1=rows, op0=ALU.mult, op1=ALU.add)
                    last.then_inc(y_added, 1)

                for c in range(HC):
                    n = b * HC + c
                    dve.wait_ge(gate_ready, n + 1)
                    dve.tensor_tensor(hidden[:, c % 3, :], gate[:, c % 3, :], u[:, c % 3, :],
                                      ALU.mult).then_inc(hidden_ready, 1)
                    if c >= 3 and c % 2 == 1:
                        add((c - 3) // 2)
                add(E)

        @block.tensor
        def _(pe):
            transpose_tokens(pe, xn, ident, g, xn_ready, xnT_full, xnT_ready)
            pe.wait_ge(xnT_ready, 4)
            pe.wait_ge(router_ready, 1)
            for i in range(NT):
                cut, out = slice(i * P, (i + 1) * P), y[:, 0, i * E:(i + 1) * E]
                pe.matmul(out, xnT_hi[:, cut], router_hi[:], start=True, stop=False)
                pe.matmul(out, xnT_lo[:, cut], router_hi[:], start=False, stop=False)
                last = pe.matmul(out, xnT_hi[:, cut], router_lo[:], start=False, stop=True)
            last.then_inc(logits_full, 1)
            pe.wait_ge(up_ready, NE)
            pe.wait_ge(w_in, 32)

            def up_project(b, c):
                e, half = c // 2, slice(c % 2 * P, c % 2 * P + P)
                if c >= 3:
                    pe.wait_ge(hidden_ready, b * HC + c - 2)
                else:
                    wait_for(pe, hidden_ready, b * HC)
                at = bass.ds(b * S, S)
                for w, bank in enumerate((g, u)):
                    out = bank[:, c % 3, :]
                    pe.matmul(out, up_hi[:, e, w, half], xnT_hi[:, at], start=True, stop=False)
                    pe.matmul(out, up_hi[:, e, w, half], xnT_lo[:, at], start=False, stop=False)
                    last = pe.matmul(out, up_lo[:, e, w, half], xnT_hi[:, at], start=False, stop=True)
                last.then_inc(gu_full, 1)

            def down_project(b, c):
                e = c // 2
                pe.wait_ge(hidden_ready, b * HC + c + 1)
                if c % 2 == 0:
                    if e >= 2:
                        pe.wait_ge(y_added, b * NE + e - 1)
                    else:
                        pe.wait_ge(y_added, b * NE)
                        pe.wait_ge(cw_ready, 1)
                for i in range(4):
                    last = pe.matmul(y[:, e % 2, i * D:(i + 1) * D], hidden[:, c % 3, i * P:(i + 1) * P],
                                     down[:, c, :], start=(c % 2 == 0 and i == 0), stop=(c % 2 == 1),
                                     skip_group_check=True)
                if c % 2 == 1:
                    last.then_inc(y_full, 1)

            with pe.Fori(0, B) as b:
                for c in range(HC + 2):
                    if c < HC:
                        up_project(b, c)
                    if c >= 2:
                        down_project(b, c - 2)


def build(nc, t):
    with ExitStack() as all_:
        t["x"] = all_.enter_context(nc.sbuf_tensor("x_res", [P, NT, D], F32))
        t["ident"] = all_.enter_context(nc.sbuf_tensor("ident", [P, P], F32))
        for layer in (self_attention, cross_attention, mixture):
            with ExitStack() as own:
                layer(nc, lambda n, s, d: own.enter_context(nc.sbuf_tensor(n, s, d)),
                      lambda n, s, d: own.enter_context(nc.psum_tensor(n, s, d)),
                      lambda n: all_.enter_context(nc.semaphore(n)), t)


def kernel(**inputs):
    import numpy as np
    import concourse.bacc as bacc
    from concourse.bass_utils import run_bass_kernel_spmd

    def get(name):
        return np.asarray(inputs[name])

    def constant(a):
        return np.asarray(a, np.float32)

    pairs = np.arange(XC * P)
    pair_head = np.where(pairs < XF, pairs // XK, -1)
    feature_head = np.arange(D) // XD
    arrays = {
        "wqT": get("L0_attn_wq").T.reshape(D, C, DH),
        "wkT": get("L0_attn_wk").T.reshape(D, C, DH),
        "wvT": get("L0_attn_wv").T,
        "woT": get("L0_attn_wo").T.reshape(C // 2, P, D).transpose(1, 0, 2),
        "ident": constant(np.eye(P)),
        "xwqT": get("L0_xattn_Wq").T, "xwkT": get("L0_xattn_Wk").T,
        "xwvT": get("L0_xattn_Wv").T, "xwoT": get("L0_xattn_Wo").T,
        "xbias": np.stack([get("L0_xattn_bq"), get("L0_xattn_bk"), get("L0_xattn_bv")], 1),
        "bo": get("L0_xattn_bo"),
        "ctxT": get("ctx_1024").transpose(2, 0, 1),
        "thr": get("L0_xattn_raw_thresholds").reshape(XH, 1),
        "head_row": constant(pair_head[None, :XF] == np.arange(XH)[:, None]),
        "head_col": constant(feature_head[:, None] == np.arange(XH)[None]),
        "own_head": constant(pair_head[:, None] == feature_head[None]).reshape(XC, P, D).transpose(1, 0, 2),
        "router": get("L0_ffn_router_w").T,
        "route_bias": get("L0_ffn_experts_bias"),
        "expert_no": constant(np.arange(E)),
        "up0": get("L0_ffn_w1").transpose(1, 0, 2), "up1": get("L0_ffn_w3").transpose(1, 0, 2),
        "shared0": get("L0_ffn_sw1")[0], "shared1": get("L0_ffn_sw3")[0],
        "down": get("L0_ffn_w2").reshape(2 * E, P, D).transpose(1, 0, 2),
        "shared_down": get("L0_ffn_sw2")[0].reshape(2, P, D).transpose(1, 0, 2),
        "x": get("x"),
    }
    nc = bacc.Bacc("TRN2", target_bir_lowering=False, num_devices=1)
    t, feeds = {}, {}
    for name, a in arrays.items():
        a = np.ascontiguousarray(a)
        feeds[f"in_{name}"] = a
        t[f"{name}_in"] = nc.dram_tensor(f"in_{name}", a.shape, F32, kind="ExternalInput").ap()
    by_tile = "b (t p) d -> p (b t) d"
    t["x_in"] = t["x_in"].rearrange(by_tile, p=P)
    t["out"] = nc.dram_tensor("out", (B, S, D), F32, kind="ExternalOutput").ap().rearrange(by_tile, p=P)
    build(nc, t)
    result = run_bass_kernel_spmd(nc, [feeds], core_ids=[0])
    return result.results[0]["out"]
```

```python
from contextlib import ExitStack

import concourse.bass as bass
from concourse import mybir

F32 = mybir.dt.float32
F32R = mybir.dt.float32r
U32 = mybir.dt.uint32
BF16 = mybir.dt.bfloat16
ALU = mybir.AluOpType
ACT = mybir.ActivationFunctionType
AX = mybir.AxisListType

P = 128
B, S, D = 4, 512, 128
NT = B * S // P
EPS = 1e-5
MASKED = -1e30

C, DH = 16, 64
GT = 32
POS = GT * C
HG = 8
PT = HG * GT
PARTS = B * S // PT
KB = POS // P
STEPS = HG * KB
LAG_ST, LAG_SM = 3, 11
VL = DH + 2

XH, XD, XK = 16, 8, 77
XF = XH * XK
XC = (XF + P - 1) // P
XL = XF - (XC - 1) * P

E, HID = 8, 256
HC = (E + 1) * HID // P


def wait_for(eng, sem, count):
    if not (isinstance(count, int) and count <= 0):
        eng.wait_ge(sem, count)


class Chain:

    def __init__(self, eng, sem):
        self.eng, self.sem, self.count = eng, sem, 0

    def link(self, instruction):
        self.count += 1
        instruction.then_inc(self.sem, 1)
        return instruction

    def wait(self):
        self.eng.wait_ge(self.sem, self.count)


def statistics(dve, chain, x, stats, moments, rstd, work, root_wanted, root_ready):
    for t in range(NT):
        chain.link(dve.bn_stats(stats[:, t, :], x[:, t, :]))
    chain.wait()
    for t in range(NT):
        chain.link(dve.bn_aggr(moments[:, t, :], stats[:, t, :]))
    chain.wait()
    var = work[:, 0, :]
    dve.tensor_scalar(var, moments[:, :, 1], EPS, None, ALU.add).then_inc(root_wanted, 1)
    dve.wait_ge(root_ready, 1)
    chain.link(dve.reciprocal(rstd[:, 0, :], work[:, 2, :]))
    chain.wait()
    chain.link(dve.tensor_tensor(work[:, 1, :], rstd[:, 0, :], rstd[:, 0, :], ALU.mult))
    chain.wait()
    chain.link(dve.tensor_tensor(work[:, 1, :], work[:, 1, :], var, ALU.mult))
    chain.wait()
    chain.link(dve.tensor_scalar(work[:, 1, :], work[:, 1, :], -0.5, 1.5, ALU.mult, ALU.add))
    chain.wait()
    chain.link(dve.tensor_tensor(rstd[:, 1, :], rstd[:, 0, :], work[:, 1, :], ALU.mult))
    chain.wait()


def normalize(dve, chain, x, stats, moments, rstd, work, xn, root_wanted, root_ready, xn_ready):
    statistics(dve, chain, x, stats, moments, rstd, work, root_wanted, root_ready)
    for t in range(NT):
        last = dve.tensor_scalar(xn[:, t, :], x[:, t, :], moments[:, t, 0:1],
                                 rstd[:, 1, t:t + 1], ALU.subtract, ALU.mult)
    last.then_inc(xn_ready, 1)


def transpose_tokens(pe, xn, ident, banks, xn_ready, xnT_full, xnT_ready):
    pe.wait_ge(xn_ready, 1)
    for q in range(NT // 4):
        if q >= 2:
            pe.wait_ge(xnT_ready, q - 1)
        for i in range(4):
            last = pe.transpose(banks[:, q % 2, i * P:(i + 1) * P], xn[:, 4 * q + i, :], ident[:])
        last.then_inc(xnT_full, 1)


def round_tokens(act, banks, xnT_hi, xnT_full, xnT_hi_ready):
    for q in range(NT // 4):
        act.wait_ge(xnT_full, q + 1)
        act.activation(xnT_hi[:, q * 512:(q + 1) * 512], banks[:, q % 2, :], ACT.Copy).then_inc(xnT_hi_ready, 1)


def token_rests(dve, banks, xnT_hi, xnT_lo, xnT_hi_ready, xnT_ready):
    for q in range(NT // 4):
        cols = slice(q * 512, (q + 1) * 512)
        dve.wait_ge(xnT_hi_ready, q + 1)
        dve.tensor_tensor(xnT_lo[:, cols], banks[:, q % 2, :], xnT_hi[:, cols].bitcast(F32),
                          ALU.subtract).then_inc(xnT_ready, 1)


JOBS = {1: ("xt", 0), 2: ("wo", 0), **{s: ("qk", s - 3) for s in range(3, 19)},
        19: ("v", 0), 22: ("v", 1), 26: ("v", 2), 31: ("v", 3)}
ORDER = list(JOBS.values())
FIRST_JOBS = [j for j in ORDER if j[0] != "wo"]


def bank_of(job):
    return ORDER.index(job) % 2


def jobs_of(has_before, has_next):
    return {s: j for s, j in JOBS.items() if (has_before if j[0] == "wo" else has_next)}


def jobs_before(part):
    return (part + 1) * len(FIRST_JOBS)


def job_before(job, part, jobs):
    n = ORDER.index(job) - 2
    while n >= 0 and ORDER[n] not in jobs:
        n -= 2
    return (ORDER[n], part) if n >= 0 else (ORDER[n], part - 1)


def self_attention(nc, sb, psum, sem, t):
    x = t["x"]
    xn = sb("xn_part", [P, PT // P, D], F32)
    xT_hi, xT_lo = sb("xT_hi", [P, PT], F32R), sb("xT_lo", [P, PT], F32R)
    x_part = sb("x_part", [P, PT], F32)
    w_hi = sb("wqk_hi", [P, 2, C, 2, DH], F32R)
    w_lo = sb("wqk_lo", [P, 2, C, 2, DH], F32R)
    wvT, woT = sb("wvT", [P, C * DH], F32), sb("woT", [P, C // 2, D], F32)
    qk = [sb(f"qk{s}", [P, 2, HG, C, GT], F32R) for s in range(2)]
    q_lo = [sb(f"q_lo{s}", [P, HG, C, GT], F32R) for s in range(2)]
    keys_ones = sb("keys_ones", [P, 2, POS], F32R)
    v_hi = sb("v_hi", [P, HG, KB, 2, DH], F32R)
    v_lo = sb("v_lo", [P, HG, KB, VL], F32R)
    probs = sb("probs", [P, 2, POS], F32)
    p_hi, p_lo = sb("p_hi", [P, 4, POS], F32R), sb("p_lo", [P, 4, POS], F32R)
    attn = sb("attn", [P, C // 2, PT], F32)
    neg_max = sb("neg_max", [P, 4, KB], F32)
    turned_and_inverse = sb("turned_and_inverse", [P, POS], F32)
    turned, inv_sum = turned_and_inverse[0:DH, :], turned_and_inverse[DH:P, 0:POS // 32]
    moments, rstd = sb("moments", [P, NT, 2], F32), sb("rstd", [P, 2, NT], F32)
    stats = probs[:, 0, 0:NT * 6].rearrange("p (t n) -> p t n", n=6)
    work = probs[:, 1, 0:NT * 3].rearrange("p (n t) -> p n t", t=NT)
    ident = t["ident"]
    w_raw = attn[:].rearrange("p a b -> p (a b)").rearrange("p (w c d) -> p w c d", w=2, c=C)

    sc = psum("scores", [P, 2, POS], F32)
    st = psum("scoresT", [P, 2, POS], F32)
    ov = psum("out_and_sum", [P, 2, POS], F32)
    pj = psum("projected", [P, 2, POS], F32)

    x_loaded, w_loaded, wv_loaded = sem("x_loaded"), sem("w_loaded"), sem("wv_loaded")
    root_wanted, root_ready = sem("root_wanted"), sem("root_ready")
    dve_chain = sem("dve_chain")
    xn_ready, xT_hi_ready, xT_ready = sem("xn_ready"), sem("xT_hi_ready"), sem("xT_ready")
    w_hi_ready, w_ready, ones_ready = sem("w_hi_ready"), sem("w_ready"), sem("ones_ready")
    x_part_ready = sem("x_part_ready")
    job_full, hi_ready, qk_ready, v_hi_ready, v_ready = sem("job_full"), sem("hi_ready"), sem("qk_ready"), sem("v_hi_ready"), sem("v_ready")
    x_added = sem("x_added")
    sc_full, max_ready = sem("sc_full"), sem("max_ready")
    max_turned, max_rows_ready = sem("max_turned"), sem("max_rows_ready")
    keys_ones_ready = sem("keys_ones_ready")
    st_full, p_hi_ready, p_lo_ready = sem("st_full"), sem("p_hi_ready"), sem("p_lo_ready")
    ov_full, div_step, inv_ready, attn_ready = sem("ov_full"), sem("div_step"), sem("inv_ready"), sem("attn_ready")
    wo_full = sem("wo_full")

    def freed(job, part):
        kind, i = job
        if kind == "xt":
            return xT_ready, part + 2
        if kind == "qk":
            return qk_ready, (part + 1) * C + i + 1
        if kind == "v":
            return v_ready, (part + 1) * (HG // 2) + i + 1
        return x_added, part

    def for_parts(eng, steps):
        steps(0, 0, False, True)
        with eng.Fori(0, (PARTS - 2) // 2) as r:
            steps(r * 2 + 1, 1, True, True)
            steps(r * 2 + 2, 0, True, True)
        steps(PARTS - 1, (PARTS - 1) % 2, True, False)

    with nc.Block() as block:
        @block.sync
        def _(sp):
            for q in range(4):
                sp.dma_start(x[:, 4 * q:4 * q + 4, :], t["x_in"][:, 4 * q:4 * q + 4, :]).then_inc(x_loaded, 16)
            sp.dma_start(ident[:], t["ident_in"]).then_inc(w_loaded, 16)
            sp.dma_start(w_raw[:, 0], t["wqT_in"]).then_inc(w_loaded, 16)
            sp.dma_start(w_raw[:, 1], t["wkT_in"]).then_inc(w_loaded, 16)
            sp.dma_start(wvT[:], t["wvT_in"]).then_inc(wv_loaded, 16)
            sp.dma_start(woT[:], t["woT_in"]).then_inc(wv_loaded, 16)

        @block.gpsimd
        def _(pool):
            for s in range(2):
                pool.memset(q_lo[s][:].bitcast(F32), 0.0).then_inc(ones_ready, 1)
            pool.memset(keys_ones[:].bitcast(F32), 1.0).then_inc(ones_ready, 1)
            pool.memset(v_hi[:, :, :, 1, :].bitcast(F32), 1.0).then_inc(ones_ready, 1)
            pool.memset(v_lo[:, :, :, DH:VL].bitcast(F32), 0.0).then_inc(ones_ready, 1)

            def whole_tokens(target):
                pool.wait_ge(xT_ready, target + 1)
                pool.tensor_tensor(x_part[:], xT_hi[:].bitcast(F32), xT_lo[:].bitcast(F32), ALU.add)\
                    .then_inc(x_part_ready, 1)

            def low_probs(m, ml):
                pool.wait_ge(p_hi_ready, m + 1)
                pool.tensor_tensor(p_lo[:, ml % 4], probs[:, ml % 2], p_hi[:, ml % 4].bitcast(F32),
                                   ALU.subtract).then_inc(p_lo_ready, 1)

            def steps(part, slot, has_before, has_next):
                for k in range(STEPS):
                    if has_next or k + LAG_ST < STEPS:
                        low_probs(part * STEPS + k + LAG_ST, k + LAG_ST)
                    if k == 6 and has_next:
                        whole_tokens(part + 1)

            whole_tokens(0)
            for m in range(LAG_ST):
                low_probs(m, m)
            for_parts(pool, steps)

        @block.scalar
        def _(act):
            act.wait_ge(root_wanted, 1)
            act.activation(work[:, 2, :], work[:, 0, :], ACT.Sqrt).then_inc(root_ready, 1)
            act.wait_ge(w_loaded, 48)
            for w in range(2):
                act.activation(w_hi[:, w], w_raw[:, w].rearrange("p c (o d) -> p c o d", o=1).broadcast_to([P, C, 2, DH]),
                               ACT.Copy).then_inc(w_hi_ready, 1)

            def evacuate(job, slot, part):
                (kind, i), bank = job, bank_of(job)
                if kind == "xt":
                    act.activation(xT_hi[:], pj[:, bank, 0:PT], ACT.Copy).then_inc(xT_hi_ready, 1)
                elif kind == "qk":
                    act.activation(qk[slot][:, :, :, i, :], pj[:, bank, :].rearrange("p (w g t) -> p w g t", w=2, g=HG),
                                   ACT.Copy).then_inc(hi_ready, 1)
                elif kind == "v":
                    act.activation(v_hi[:, 2 * i:2 * i + 2, :, 0, :],
                                   pj[:, bank, :].rearrange("p (g b d) -> p g b d", g=2, b=KB),
                                   ACT.Copy).then_inc(v_hi_ready, 1)

            def exponentials(m, ml):
                act.wait_ge(st_full, m + 1)
                wait_for(act, p_lo_ready, m - 1)
                act.activation(probs[:, ml % 2, :], st[:, ml % 2, :], ACT.Exp, scale=DH ** -0.5)
                act.activation(p_hi[:, ml % 4, :], st[:, ml % 2, :], ACT.Exp, scale=DH ** -0.5).then_inc(p_hi_ready, 1)

            def steps(part, slot, has_before, has_next):
                jobs = jobs_of(has_before, has_next)
                for k in range(STEPS):
                    if has_next or k + LAG_ST < STEPS:
                        exponentials(part * STEPS + k + LAG_ST, k + LAG_ST)
                    if k % KB == 1 and (has_next or k + 2 * KB < STEPS):
                        ahead = k // KB + 2
                        high_keys(part * HG + ahead, ahead, part + ahead // HG, slot)
                    if k in jobs and jobs[k][0] != "wo":
                        act.wait_ge(job_full, jobs_before(part) + FIRST_JOBS.index(jobs[k]) + 1)
                        evacuate(jobs[k], 1 - slot, part)
                    if k % KB == 2 and (has_next or k // KB + 2 < HG):
                        ahead = k // KB + 2
                        max_rows(part * HG + ahead, ahead, slot)

            def max_rows(g, gl, slot):
                act.wait_ge(max_turned, g + 1)
                row = q_lo[slot if gl < HG else 1 - slot][0:KB, gl % HG].rearrange("p c t -> p (c t)")
                for b in range(KB):
                    last = act.activation(row[:, b * P:(b + 1) * P], ov[0:KB, (gl + 1) % 2, 0:P], ACT.Copy,
                                          scale=ident[0:KB, b:b + 1])
                last.then_inc(max_rows_ready, 1)

            def high_keys(g, gl, own_part, slot):
                s = slot if gl < HG else 1 - slot
                act.wait_ge(hi_ready, (own_part + 1) * C)
                act.activation(keys_ones[DH:P, gl % 2, :], qk[s][0:DH, 1, gl % HG].rearrange("p c t -> p (c t)"),
                               ACT.Copy).then_inc(keys_ones_ready, 1)

            for n, job in enumerate(FIRST_JOBS):
                act.wait_ge(job_full, n + 1)
                evacuate(job, 0, -1)
            act.wait_ge(ones_ready, 5)
            for g in range(2):
                max_rows(g, g, 0)
                high_keys(g, g, 0, 0)
            for m in range(LAG_ST):
                exponentials(m, m)
            for_parts(act, steps)

        @block.vector
        def _(dve):
            chain = Chain(dve, dve_chain)
            dve.wait_ge(x_loaded, 64)
            statistics(dve, chain, x, stats, moments, rstd, work, root_wanted, root_ready)

            def tokens(target):
                for i in range(PT // P):
                    tile = bass.ds(target * (PT // P) + i, 1)
                    last = dve.tensor_scalar(xn[:, i, :], x[:, tile, :].rearrange("p o d -> p (o d)"),
                                             moments[:, tile, 0:1].rearrange("p o e -> p (o e)"),
                                             rstd[:, 1, tile], ALU.subtract, ALU.mult)
                last.then_inc(xn_ready, 1)

            tokens(0)
            for w in range(2):
                dve.wait_ge(w_hi_ready, w + 1)
                dve.tensor_tensor(w_lo[:, w], w_raw[:, w].rearrange("p c (o d) -> p c o d", o=1).broadcast_to([P, C, 2, DH]),
                                  w_hi[:, w].bitcast(F32), ALU.subtract).then_inc(w_ready, 1)

            def maximum(m, ml):
                dve.wait_ge(sc_full, m + 1)
                dve.tensor_reduce(neg_max[:, ml // KB % 4, ml % KB:ml % KB + 1], sc[:, ml % 2, :], AX.X, ALU.max,
                                  negate=True).then_inc(max_ready, 1)

            def rest(job, slot, part):
                (kind, i), bank = job, bank_of(job)
                half = pj[:, bank, :].rearrange("p (w g t) -> p w g t", w=2, g=HG)
                if kind == "xt":
                    dve.wait_ge(xT_hi_ready, part + 2)
                    dve.tensor_tensor(xT_lo[:], pj[:, bank, 0:PT], xT_hi[:].bitcast(F32), ALU.subtract).then_inc(xT_ready, 1)
                elif kind == "v":
                    dve.wait_ge(v_hi_ready, (part + 1) * (HG // 2) + i + 1)
                    flat = lambda a: a.rearrange("p g b d -> p (g b) d")
                    dve.tensor_tensor(flat(v_lo[:, 2 * i:2 * i + 2, :, 0:DH]),
                                      pj[:, bank, :].rearrange("p (n d) -> p n d", d=DH),
                                      flat(v_hi[:, 2 * i:2 * i + 2, :, 0, :]).bitcast(F32),
                                      ALU.subtract).then_inc(v_ready, 1)
                elif kind == "qk":
                    dve.wait_ge(hi_ready, (part + 1) * C + i + 1)
                    dve.tensor_tensor(q_lo[slot][DH:P, :, i, :], half[DH:P, 0], qk[slot][DH:P, 0, :, i, :].bitcast(F32),
                                      ALU.subtract)
                    k_lo = qk[slot][DH:P, 1, :, i, :]
                    dve.tensor_tensor(k_lo, half[DH:P, 1], k_lo.bitcast(F32), ALU.subtract).then_inc(qk_ready, 1)
                elif kind == "wo":
                    dve.wait_ge(wo_full, part)
                    tiles = bass.ds((part - 1) * (PT // P), PT // P)
                    dve.tensor_tensor(x[:, tiles, :], x[:, tiles, :], pj[:, bank, 0:PT].rearrange("p (n d) -> p n d", d=D),
                                      ALU.add).then_inc(x_added, 1)

            def divide_first(g, gl):
                done = g * 2
                dve.wait_ge(ov_full, g + 1)
                wait_for(dve, attn_ready, g)
                dve.transpose(turned, ov[DH:P, gl % 2, :]).then_inc(div_step, 1)
                dve.wait_ge(div_step, done + 1)
                dve.reciprocal(inv_sum, turned.rearrange("p (n r) -> p n r", r=32)[:, :, 0]).then_inc(div_step, 1)

            def divide_last(g, gl):
                dve.wait_ge(div_step, g * 2 + 2)
                dve.transpose(turned, inv_sum.rearrange("p (n o) -> p n o", o=1).broadcast_to([DH, POS // 32, 32]))\
                   .then_inc(inv_ready, 1)
                dve.wait_ge(inv_ready, g + 1)
                for odd in range(2):
                    view = lambda a: a.rearrange("p (c t) -> p c t", c=C)[:, odd::2, :]
                    out = dve.tensor_tensor(attn[DH * odd:DH * odd + DH, :, gl * GT:(gl + 1) * GT],
                                            view(ov[0:DH, gl % 2, :]), view(turned), ALU.mult)
                out.then_inc(attn_ready, 1)

            def steps(part, slot, has_before, has_next):
                jobs = jobs_of(has_before, has_next)
                for k in range(STEPS):
                    if k == 0 and has_next:
                        tokens(part + 1)
                    if has_next or k + LAG_SM < STEPS:
                        maximum(part * STEPS + k + LAG_SM, k + LAG_SM)
                    if k % KB == KB - 1:
                        divide_first(part * HG + k // KB, k // KB)
                    if k in jobs:
                        rest(jobs[k], 1 - slot, part)
                    if k % KB == 0 and (k > 0 or has_before):
                        if k == KB:
                            wait_for(dve, wo_full, part)
                        divide_last(part * HG + k // KB - 1, (k // KB - 1) % HG)

            dve.wait_ge(ones_ready, 5)
            for job in FIRST_JOBS:
                rest(job, 0, -1)
            for m in range(LAG_SM):
                maximum(m, m)
            for_parts(dve, steps)
            divide_last(PARTS * HG - 1, HG - 1)
            rest(("wo", 0), 0, PARTS)

        @block.tensor
        def _(pe):
            pe.wait_ge(w_loaded, 48)

            def project(job, target, free, part):
                (kind, i), bank = job, bank_of(job)
                if free is not None:
                    wait_for(pe, *free)
                if kind == "xt":
                    pe.wait_ge(xn_ready, target + 1)
                    for n in range(PT // P):
                        last = pe.transpose(pj[:, bank, n * P:(n + 1) * P], xn[:, n, :], ident[:])
                elif kind == "qk":
                    if i == 0:
                        pe.wait_ge(xT_ready, target + 1)
                        pe.wait_ge(w_ready, 2)
                    for w in range(2):
                        out = pj[:, bank, w * PT:(w + 1) * PT]
                        hi = w_hi[:, w, i].rearrange("p o d -> p (o d)")
                        lo = w_lo[:, w, i].rearrange("p o d -> p (o d)")
                        pe.matmul(out, hi, xT_hi[:], start=True, stop=False)
                        pe.matmul(out, hi, xT_lo[:], start=False, stop=False)
                        last = pe.matmul(out, lo, xT_hi[:], start=False, stop=True)
                elif kind == "v":
                    if i == 0:
                        pe.wait_ge(x_part_ready, target + 1)
                    wv = wvT[:].rearrange("p (b j d) -> p b j d", b=KB, j=4)
                    for e in range(2):
                        gl = 2 * i + e
                        for j in range(4):
                            last = pe.matmul(pj[GT * j:GT * j + GT, bank, e * 256:(e + 1) * 256],
                                             x_part[:, gl * GT:(gl + 1) * GT], wv[:, :, j, :], start=True, stop=True)
                else:
                    pe.wait_ge(attn_ready, (target + 1) * HG)
                    for n in range(PT // P):
                        for c in range(C // 2):
                            last = pe.matmul(pj[:, bank, n * D:(n + 1) * D], attn[:, c, n * P:(n + 1) * P], woT[:, c, :],
                                             start=(c == 0), stop=(c == C // 2 - 1))
                    last.then_inc(wo_full, 1)
                    return
                last.then_inc(job_full, 1)

            def scores(m, ml, slot):
                b, g = ml % KB, ml // KB % HG
                wait_for(pe, max_ready, m - 1)
                flat = lambda w: qk[slot][:, w, g].rearrange("p c t -> p (c t)")
                pe.matmul(sc[:, ml % 2, :], flat(0)[:, b * P:(b + 1) * P], flat(1), start=True, stop=True)\
                  .then_inc(sc_full, 1)

            def turn_maxima(g, gl):
                pe.wait_ge(max_ready, (g + 1) * KB)
                pe.transpose(ov[0:KB, (gl + 1) % 2, 0:P], neg_max[:, gl % 4, :], ident[:]).then_inc(max_turned, 1)

            def weighted(m, ml, g, has_next):
                b, gl = ml % KB, ml // KB % HG
                pe.wait_ge(p_hi_ready, m + 1)
                if b == 0:
                    wait_for(pe, attn_ready, g - 1)
                    if has_next or gl + 1 < HG:
                        pe.wait_ge(max_rows_ready, g + 2)
                hi = v_hi[:, gl, b].rearrange("p o d -> p (o d)")
                pe.matmul(ov[:, gl % 2, :], hi, p_hi[:, ml % 4, :], start=(b == 0), stop=False)
                pe.matmul(ov[0:VL, gl % 2, :], v_lo[:, gl, b], p_hi[:, ml % 4, :], start=False, stop=False)
                pe.wait_ge(p_lo_ready, m + 1)
                last = pe.matmul(ov[:, gl % 2, :], hi, p_lo[:, ml % 4, :], start=False, stop=(b == KB - 1))
                if b == KB - 1:
                    last.then_inc(ov_full, 1)

            def scores_t_of(part, k, slot):
                b = k % KB
                g_of = k // KB % HG
                s = slot if k < STEPS else 1 - slot
                flat = lambda w: qk[s][:, w, g_of].rearrange("p c t -> p (c t)")
                keys = flat(1)[:, b * P:(b + 1) * P]
                out = st[:, k % 2, :]
                wait_for(pe, p_hi_ready, part * STEPS + k - 1)
                pe.matmul(out, keys, flat(0), start=True, stop=False)
                if b == 0:
                    pe.wait_ge(max_rows_ready, part * HG + k // KB + 1)
                    pe.wait_ge(keys_ones_ready, part * HG + k // KB + 1)
                pe.matmul(out, keys_ones[:, k // KB % 2, b * P:(b + 1) * P],
                          q_lo[s][:, g_of].rearrange("p c t -> p (c t)"), start=False, stop=True).then_inc(st_full, 1)

            def steps(part, slot, has_before, has_next):
                jobs = jobs_of(has_before, has_next)
                for k in range(STEPS):
                    if k % (2 * KB) == 0:
                        pe.wait_ge(v_ready, part * (HG // 2) + k // (2 * KB) + 1)
                    weighted(part * STEPS + k, k, part * HG + k // KB, has_next)
                    if has_next or k + LAG_ST < STEPS:
                        scores_t_of(part, k + LAG_ST, slot)
                    if has_next or k + LAG_SM < STEPS:
                        ahead = k + LAG_SM
                        if ahead == STEPS:
                            pe.wait_ge(qk_ready, (part + 2) * C)
                        scores(part * STEPS + ahead, ahead, slot if ahead < STEPS else 1 - slot)
                    if k in jobs:
                        job = jobs[k]
                        project(job, part - 1 if job[0] == "wo" else part + 1,
                                freed(*job_before(job, part, jobs.values())), part)
                    if k % KB == 2 and (has_next or k // KB + 2 < HG):
                        wait_for(pe, attn_ready, part * HG + k // KB)
                        turn_maxima(part * HG + k // KB + 2, k // KB + 2)

            pe.wait_ge(wv_loaded, 32)
            for job in FIRST_JOBS:
                before, part = job_before(job, -1, FIRST_JOBS)
                project(job, 0, freed(before, -1) if part == -1 else None, -1)
            pe.wait_ge(qk_ready, C)
            pe.wait_ge(ones_ready, 5)
            for m in range(LAG_SM):
                scores(m, m, 0)
            for g in range(2):
                turn_maxima(g, g)
            for m in range(LAG_ST):
                scores_t_of(0, m, 0)
            for_parts(pe, steps)
            project(("wo", 0), PARTS - 1, freed(("wo", 0), PARTS - 1), PARTS)


PREP = [("v", 0, (0,)), ("v", 1, (1,)), ("v", 2, (2,)), ("q", 0, (0,)),
        ("max", 0, (0, 1, 2)), ("max", 1, (0, 1, 2)), ("max", 2, (0, 1, 2)), ("max", 3, (0, 1, 2)), ("turn", 0, (0,)),
        ("wo", 0, (1,))]
V_CHUNKS = [range(0, 4), range(4, 8), range(8, XC)]
MAX_HEADS = [range(0, 6), range(6, 12), range(12, 16)]


def prepare_plan():
    plan, reader = [], {}
    for round_ in range(-1, B + 1):
        for kind, i, banks in PREP:
            batch = round_ - 1 if kind == "wo" else round_ + 1
            if 0 <= batch < B:
                needs = max([reader[b] + 1 for b in banks if b in reader], default=0)
                for b in banks:
                    reader[b] = len(plan)
                plan.append((kind, i, batch, banks, needs, round_))
    return plan


PLAN = prepare_plan()


def rows_of(j):
    return P if j < XC - 1 else XL


def cross_attention(nc, sb, psum, sem, t):
    x, ident = t["x"], t["ident"]
    xn = sb("xn2", [P, NT, D], F32)
    xnT_hi, xnT_lo = sb("xnT2_hi", [P, B * S], F32R), sb("xnT2_lo", [P, B * S], F32R)
    stats, moments = sb("stats2", [P, NT, 6], F32), sb("moments2", [P, NT, 2], F32)
    rstd, work = sb("rstd2", [P, 2, NT], F32), sb("work2", [P, 3, NT], F32)
    wqT, wkT, wvT, woT = (sb(f"x{n}", [P, D], F32) for n in ("wqT", "wkT", "wvT", "woT"))
    wq_hi, wq_lo = sb("xwq_hi", [P, D], F32R), sb("xwq_lo", [P, D], F32R)
    bias = sb("xbias", [P, 3], F32)
    bo = sb("bo", [P, D], F32)
    ctxT = sb("ctxT", [P, B, XK], F32)
    ctx_rep = sb("ctx_rep", [P, B, XF], F32)
    ctx_sum, v_sum = sb("ctx_sum", [P, B], F32), sb("v_sum", [P, B], F32)
    own_head = sb("own_head", [P, XC, D], F32)
    own_head_r = sb("own_head_r", [P, XC, D], F32R)
    head_row, head_row_r = sb("head_row", [XH, XF], F32), sb("head_row_r", [XH, XF], F32R)
    head_col = sb("head_col", [P, XH], F32)
    k_all = sb("k_all", [P, B, XK], F32)
    k_hi, k_lo = sb("k_hi", [P, B, XK], F32R), sb("k_lo", [P, B, XK], F32R)
    keys_hi, keys_lo = sb("keys_hi", [P, 2, XH, XK], F32R), sb("keys_lo", [P, 2, XH, XK], F32R)
    vals = sb("vals", [P, XC, D], F32)
    vals_hi, vals_lo = sb("vals_hi", [P, 2, XC, D], F32R), sb("vals_lo", [P, 2, XC, D], F32R)
    q_hi, q_lo = sb("q2_hi", [P, 2, S], F32R), sb("q2_lo", [P, 2, S], F32R)
    neg_max, neg_maxT = sb("neg_max2", [P, 4, XH], F32), sb("neg_maxT", [XH, 2, S], F32R)
    thr = sb("thr", [XH, 6], F32)
    thr_col = sb("thr_col", [P, XC], F32)
    ident_b, mask = sb("ident_b", [P, P], BF16), sb("mask", [P, 3, S], BF16)
    e, p_hi, p_lo = sb("e", [P, 2, S], F32), sb("e_hi", [P, 4, S], F32R), sb("e_lo", [P, 4, S], F32R)
    none, total, inv, num = (sb(n, [P, S], F32) for n in ("none", "total", "inv", "num"))
    out_T = sb("out_T", [P, S], F32)

    sc = psum("scores2", [P, 3, S], F32)
    pb = psum("prepare", [P, 3, S], F32)
    ov, z = psum("out2", [P, S], F32), psum("sum2", [P, S], F32)

    w_in, c_in, h_in, rep_in = sem("xw_loaded"), sem("ctx_loaded"), sem("heads_loaded"), sem("rep_loaded")
    root_wanted, root_ready, dve_chain = sem("root_wanted2"), sem("root_ready2"), sem("dve_chain2")
    xn_ready, xnT_full, xnT_hi_ready, xnT_ready = sem("xn_ready2"), sem("xnT_full2"), sem("xnT_hi_ready2"), sem("xnT_ready2")
    w_hi_ready, w_ready, head_row_ready = sem("xw_hi_ready"), sem("xw_ready"), sem("head_row_ready")
    sum_ready, first_full, k_ready, k_hi_ready, k_split = sem("sum_ready"), sem("first_full"), sem("k_ready"), sem("k_hi_ready"), sem("k_split")
    thr_step, thr_done, thr_full, setup_read = sem("thr_step"), sem("thr_done"), sem("thr_full"), sem("setup_read")
    bo_added, keys_ready = sem("bo_added"), sem("keys_ready")
    prep_full, prep_read, q_hi_ready = sem("prep_full"), sem("prep_read"), sem("q2_hi_ready")
    raw_full, mask_ready, shifted, p_hi_ready, p_lo_ready = sem("raw_full"), sem("mask_ready"), sem("shifted"), sem("e_hi_ready"), sem("e_lo_ready")
    vals_hi_ready, vals_ready = sem("vals_hi_ready"), sem("vals_ready")
    group_read, num_ready, outT_ready = sem("group_read"), sem("num_ready"), sem("outT_ready")
    chunk_done, consts_ready = sem("chunk_done"), sem("consts_ready")

    index = {(kind, i, batch): n for n, (kind, i, batch, *_) in enumerate(PLAN)}
    cuts = [slice(h.start, h.stop) for h in MAX_HEADS]

    def v_pieces(i):
        js = V_CHUNKS[i]
        if js.stop < XC:
            return [(P, slice(js.start, js.stop))]
        return [(P, slice(js.start, XC - 1)), (XL, slice(XC - 1, XC))]

    def prep_of(round_):
        return [(n, *j[:4], j[4]) for n, j in enumerate(PLAN) if j[5] == round_]

    with nc.Block() as block:
        @block.sync
        def _(sp):
            for dst, src in ((wqT, "xwqT_in"), (wkT, "xwkT_in"), (wvT, "xwvT_in"), (woT, "xwoT_in"), (bias, "xbias_in")):
                sp.dma_start(dst[:], t[src]).then_inc(w_in, 16)
            sp.dma_start(ctxT[:], t["ctxT_in"]).then_inc(c_in, 16)
            sp.dma_start(thr[:, 0:1], t["thr_in"]).then_inc(c_in, 16)
            sp.dma_start(head_row[:], t["head_row_in"]).then_inc(h_in, 16)
            sp.dma_start(head_col[:], t["head_col_in"]).then_inc(h_in, 16)
            sp.dma_start(bo[:], t["bo_in"].partition_broadcast(P)).then_inc(h_in, 16)
            sp.dma_start(own_head[:], t["own_head_in"]).then_inc(h_in, 16)
            for b in range(B):
                src = t["ctxT_in"][:, b, :].rearrange("p (o k) -> p o k", o=1).broadcast_to([P, XH, XK])
                sp.dma_start(ctx_rep[:, b, :].rearrange("p (h k) -> p h k", h=XH), src).then_inc(rep_in, 16)
            sp.dma_start(t["router"][:], t["router_in"]).then_inc(t["loaded"], 16)
            sp.dma_start(t["route_bias"][:], t["route_bias_in"].partition_broadcast(P)).then_inc(t["loaded"], 16)
            sp.dma_start(t["expert_no"][:], t["expert_no_in"].partition_broadcast(P)).then_inc(t["loaded"], 16)
            for w in range(2):
                sp.dma_start(t["up"][:, 0:E, w, :], t[f"up{w}_in"]).then_inc(t["loaded"], 16)
                sp.dma_start(t["up"][:, E, w, :], t[f"shared{w}_in"]).then_inc(t["loaded"], 16)
            sp.dma_start(t["down"][:, 0:2 * E, :], t["down_in"]).then_inc(t["loaded"], 16)
            sp.dma_start(t["down"][:, 2 * E:HC, :], t["shared_down_in"]).then_inc(t["loaded"], 16)

        @block.gpsimd
        def _(pool):
            def keys(b, part):
                w, half = part // 2, slice(8 * (part % 2), 8 * (part % 2) + 8)
                src, dst = ((k_hi, keys_hi), (k_lo, keys_lo))[w]
                pool.tensor_tensor(dst[:, b % 2, half, :],
                                   src[:, b, :].bitcast(F32).rearrange("p (o k) -> p o k", o=1).broadcast_to([P, 8, XK]),
                                   head_col[:, half].rearrange("p (h o) -> p h o", o=1).broadcast_to([P, 8, XK]),
                                   ALU.mult).then_inc(keys_ready, 1)

            pool.wait_ge(h_in, 64)
            pool.wait_ge(k_split, 1)
            for part in range(4):
                keys(0, part)
            pool.wait_ge(xn_ready, 1)
            pool.tensor_tensor(x[:], x[:], bo[:].rearrange("p (o d) -> p o d", o=1).broadcast_to([P, NT, D]),
                               ALU.add).then_inc(bo_added, 1)

            def values_low(b, i):
                pool.wait_ge(vals_hi_ready, b * len(V_CHUNKS) + i + 1)
                for r, js in v_pieces(i):
                    last = pool.tensor_tensor(vals_lo[0:r, b % 2, js], vals[0:r, js], vals_hi[0:r, b % 2, js].bitcast(F32),
                                              ALU.subtract)
                last.then_inc(vals_ready, 1)

            for i in range(len(V_CHUNKS)):
                values_low(0, i)
            for n in range(B * XC):
                b, j, r = n // XC, n % XC, rows_of(n % XC)
                if b + 1 < B:
                    if j < 4:
                        keys(b + 1, j)
                    elif j < 4 + len(V_CHUNKS):
                        values_low(b + 1, j - 4)
                pool.wait_ge(p_hi_ready, n + 1)
                pool.tensor_tensor(p_lo[0:r, n % 4], e[0:r, n % 2], p_hi[0:r, n % 4].bitcast(F32), ALU.subtract)\
                    .then_inc(p_lo_ready, 1)

        @block.scalar
        def _(act):
            act.wait_ge(thr_done, 2)
            act.activation(thr[:, 3:4], thr[:, 2:3], ACT.Exp).then_inc(thr_step, 1)
            act.wait_ge(thr_step, 1)
            act.activation(thr[:, 4:5], thr[:, 3:4], ACT.Ln, bias=1.0).then_inc(thr_step, 1)
            act.wait_ge(root_wanted, 1)
            act.activation(work[:, 2, :], work[:, 0, :], ACT.Sqrt).then_inc(root_ready, 1)
            act.wait_ge(w_in, 80)
            act.activation(wq_hi[:], wqT[:], ACT.Copy).then_inc(w_hi_ready, 1)
            act.wait_ge(h_in, 64)
            act.activation(head_row_r[:], head_row[:], ACT.Copy).then_inc(head_row_ready, 1)
            act.wait_ge(k_ready, 1)
            act.activation(k_hi[:], k_all[:], ACT.Copy).then_inc(k_hi_ready, 1)
            act.wait_ge(setup_read, 1)
            round_tokens(act, pb, xnT_hi, xnT_full, xnT_hi_ready)

            def q_high(n, b):
                act.wait_ge(prep_full, n + 1)
                act.activation(q_hi[:, b % 2, :], pb[:, 0, :], ACT.Identity, bias=bias[:, 0:1]).then_inc(q_hi_ready, 1)

            def values_high(b, i):
                act.wait_ge(prep_read, index["v", i, b] + 1)
                for r, js in v_pieces(i):
                    last = act.activation(vals_hi[0:r, b % 2, js], vals[0:r, js], ACT.Copy)
                last.then_inc(vals_hi_ready, 1)

            def outputs(b):
                act.wait_ge(num_ready, b + 1)
                act.activation(out_T[:], num[:], ACT.Identity, bias=bias[:, 2:3]).then_inc(outT_ready, 1)

            act.activation(ident_b[:], ident[:], ACT.Copy)
            act.activation(own_head_r[:], own_head[:], ACT.Copy).then_inc(consts_ready, 1)
            for i in range(len(V_CHUNKS)):
                values_high(0, i)
            q_high(index["q", 0, 0], 0)
            for n in range(B * XC):
                b, j, r = n // XC, n % XC, rows_of(n % XC)
                if b + 1 < B:
                    if 1 <= j < 1 + len(V_CHUNKS):
                        values_high(b + 1, j - 1)
                    if j == 3:
                        q_high(index["q", 0, b + 1], b + 1)
                if j == 8 and b > 0:
                    outputs(b - 1)
                act.wait_ge(shifted, n + 1)
                wait_for(act, p_lo_ready, n - 1)
                act.activation(e[0:r, n % 2], sc[0:r, n % 3], ACT.Exp, scale=XD ** -0.5)
                act.activation(p_hi[0:r, n % 4], sc[0:r, n % 3], ACT.Exp, scale=XD ** -0.5).then_inc(p_hi_ready, 1)
            outputs(B - 1)

        @block.vector
        def _(dve):
            chain = Chain(dve, dve_chain)
            dve.wait_ge(c_in, 32)
            chain.link(dve.tensor_scalar(thr[:, 1:2], thr[:, 0:1], -1.0, None, ALU.mult))
            dve.tensor_reduce(ctx_sum[:], ctxT[:], AX.X, ALU.add).then_inc(sum_ready, 1)
            chain.wait()
            dve.tensor_tensor(thr[:, 2:3], thr[:, 0:1], thr[:, 1:2], ALU.min).then_inc(thr_done, 1)
            dve.tensor_scalar(thr[:, 5:6], thr[:, 0:1], 0.0, None, ALU.max).then_inc(thr_done, 1)
            normalize(dve, chain, x, stats, moments, rstd, work, xn, root_wanted, root_ready, xn_ready)
            dve.wait_ge(thr_done, 2)
            dve.wait_ge(thr_step, 2)
            chain.link(dve.tensor_tensor(thr[:, 1:2], thr[:, 4:5], thr[:, 5:6], ALU.add))
            chain.wait()
            dve.tensor_scalar(thr[:, 0:1], thr[:, 1:2], XD ** 0.5, None, ALU.mult).then_inc(thr_done, 1)
            dve.wait_ge(first_full, 1)
            dve.wait_ge(w_in, 80)
            dve.tensor_scalar(k_all[:].rearrange("p b k -> p (b k)"), pb[:, 0, 0:B * XK], bias[:, 1:2], None,
                              ALU.add).then_inc(k_ready, 1)
            dve.tensor_copy(v_sum[:], pb[:, 1, 0:B])
            dve.wait_ge(w_hi_ready, 1)
            dve.tensor_tensor(wq_lo[:], wqT[:], wq_hi[:].bitcast(F32), ALU.subtract).then_inc(w_ready, 1)
            dve.wait_ge(k_ready, 1)
            dve.wait_ge(k_hi_ready, 1)
            dve.tensor_tensor(k_lo[:], k_all[:], k_hi[:].bitcast(F32), ALU.subtract).then_inc(k_split, 1)
            dve.wait_ge(thr_full, 1)
            dve.tensor_copy(thr_col[:, 0:XC - 1], pb[:, 2, 0:XC - 1])
            dve.tensor_copy(thr_col[0:XL, XC - 1:XC], pb[0:XL, 2, XC - 1:XC]).then_inc(setup_read, 1)
            dve.wait_ge(setup_read, 1)
            token_rests(dve, pb, xnT_hi, xnT_lo, xnT_hi_ready, xnT_ready)

            def read(n, kind, i, b, banks):
                dve.wait_ge(prep_full, n + 1)
                if kind == "q":
                    dve.wait_ge(q_hi_ready, b + 1)
                    last = dve.scalar_tensor_tensor(out=q_lo[:, b % 2, :], in0=pb[:, 0, :], scalar=bias[:, 0:1],
                                                    in1=q_hi[:, b % 2, :].bitcast(F32), op0=ALU.add, op1=ALU.subtract)
                elif kind == "v":
                    wait_for(dve, vals_ready, b * len(V_CHUNKS))
                    for r, js in v_pieces(i):
                        at = (js.start - V_CHUNKS[i].start) * D
                        last = dve.tensor_tensor(vals[0:r, js], pb[0:r, banks[0], at:at + (js.stop - js.start) * D]
                                                 .rearrange("p (j d) -> p j d", d=D), own_head[0:r, js], ALU.mult)
                elif kind == "max":
                    for c, heads in enumerate(cuts):
                        w = (heads.stop - heads.start) * XK
                        last = dve.tensor_reduce(neg_max[:, i, heads], pb[:, c, 0:w].rearrange("p (h k) -> p h k", k=XK),
                                                 AX.X, ALU.max, negate=True)
                elif kind == "turn":
                    last = dve.tensor_copy(neg_maxT[:, b % 2, :], pb[0:XH, 0, :])
                else:
                    if b == 0:
                        dve.wait_ge(bo_added, 1)
                    last = dve.tensor_tensor(x[:, 4 * b:4 * b + 4, :], x[:, 4 * b:4 * b + 4, :],
                                             pb[:, banks[0], :].rearrange("p (t d) -> p t d", t=4), ALU.add)
                last.then_inc(prep_read, 1)

            def finish(b, stage):
                half = slice(S // 2 * (stage - 1), S // 2 * stage)
                if stage == 0:
                    dve.wait_ge(chunk_done, (b + 1) * XC)
                    chain.link(dve.tensor_scalar(none[:], z[:], 0.0, None, ALU.is_equal))
                    chain.wait()
                    chain.link(dve.scalar_tensor_tensor(out=total[:], in0=none[:], scalar=float(XK), in1=z[:],
                                                        op0=ALU.mult, op1=ALU.add))
                    wait_for(dve, outT_ready, b)
                    dve.scalar_tensor_tensor(out=num[:], in0=none[:], scalar=v_sum[:, b:b + 1], in1=ov[:],
                                             op0=ALU.mult, op1=ALU.add).then_inc(group_read, 1)
                elif stage < 3:
                    chain.wait()
                    chain.link(dve.reciprocal(inv[:, half], total[:, half]))
                else:
                    chain.wait()
                    dve.wait_ge(group_read, b + 1)
                    dve.tensor_tensor(num[:], num[:], inv[:], ALU.mult).then_inc(num_ready, 1)

            for n, kind, i, b, banks, _ in prep_of(-1):
                read(n, kind, i, b, banks)
            for n in range(B * XC):
                b, j, r = n // XC, n % XC, rows_of(n % XC)
                if b > 0 and j == 3:
                    finish(b - 1, 0)
                dve.wait_ge(raw_full, n + 1)
                dve.tensor_scalar(mask[0:r, n % 3], sc[0:r, n % 3], thr_col[0:r, j:j + 1], MASKED,
                                  ALU.is_le, ALU.mult).then_inc(mask_ready, 1)
                for job in prep_of(b):
                    if PREP.index((job[1], job[2], job[4])) == j:
                        read(*job[:5])
                if b > 0 and 4 <= j < 7:
                    finish(b - 1, j - 3)
            for stage in range(4):
                finish(B - 1, stage)
            for job in prep_of(B):
                read(*job[:5])

        @block.tensor
        def _(pe):
            pe.wait_ge(w_in, 80)
            pe.wait_ge(c_in, 32)
            pe.wait_ge(h_in, 64)
            pe.wait_ge(sum_ready, 1)
            pe.matmul(pb[:, 0, 0:B * XK], wkT[:], ctxT[:].rearrange("p b k -> p (b k)"), start=True, stop=True)
            pe.matmul(pb[:, 1, 0:B], wvT[:], ctx_sum[:], start=True, stop=True).then_inc(first_full, 1)
            pe.wait_ge(thr_done, 3)
            for j in range(XC):
                r = rows_of(j)
                last = pe.matmul(pb[0:r, 2, j:j + 1], head_row[:, j * P:j * P + r], thr[:, 0:1], start=True, stop=True)
            last.then_inc(thr_full, 1)
            pe.wait_ge(setup_read, 1)
            transpose_tokens(pe, xn, ident, pb, xn_ready, xnT_full, xnT_ready)

            def prepare(n, kind, i, b, banks, needs):
                wait_for(pe, prep_read, needs)
                if kind == "q":
                    if b == 0:
                        pe.wait_ge(w_ready, 1)
                    at = slice(b * S, (b + 1) * S)
                    pe.matmul(pb[:, 0, :], wq_hi[:], xnT_hi[:, at], start=True, stop=False)
                    pe.matmul(pb[:, 0, :], wq_hi[:], xnT_lo[:, at], start=False, stop=False)
                    last = pe.matmul(pb[:, 0, :], wq_lo[:], xnT_hi[:, at], start=False, stop=True)
                elif kind == "v":
                    if i == 0:
                        pe.wait_ge(rep_in, 64)
                    for c, j in enumerate(V_CHUNKS[i]):
                        r = rows_of(j)
                        last = pe.matmul(pb[0:r, banks[0], c * D:(c + 1) * D], ctx_rep[:, b, j * P:j * P + r], wvT[:],
                                         start=True, stop=True)
                elif kind == "max":
                    if i == 0:
                        pe.wait_ge(q_hi_ready, b + 1)
                        pe.wait_ge(keys_ready, 4 * b + 4)
                    for c, heads in enumerate(cuts):
                        w = (heads.stop - heads.start) * XK
                        last = pe.matmul(pb[:, c, 0:w], q_hi[:, b % 2, i * P:(i + 1) * P],
                                         keys_hi[:, b % 2, heads, :].rearrange("p h k -> p (h k)"), start=True, stop=True)
                elif kind == "turn":
                    pe.wait_ge(prep_read, index["max", 3, b] + 1)
                    for i in range(4):
                        last = pe.transpose(pb[0:XH, 0, i * P:(i + 1) * P], neg_max[:, i, :], ident[:])
                else:
                    pe.wait_ge(outT_ready, b + 1)
                    for i in range(4):
                        last = pe.matmul(pb[:, banks[0], i * D:(i + 1) * D], out_T[:, i * P:(i + 1) * P], woT[:],
                                         start=True, stop=True)
                last.then_inc(prep_full, 1)

            flat = lambda a, b: a[:, b % 2].rearrange("p h k -> p (h k)")

            def raw(b, j):
                n, r = b * XC + j, rows_of(j)
                cut = slice(j * P, j * P + r)
                wait_for(pe, p_hi_ready, n - 2)
                if j == 0:
                    pe.wait_ge(prep_read, index["turn", 0, b] + 1)
                out = sc[0:r, n % 3, :]
                pe.matmul(out, flat(keys_hi, b)[:, cut], q_hi[:, b % 2, :], start=True, stop=False)
                pe.matmul(out, flat(keys_hi, b)[:, cut], q_lo[:, b % 2, :], start=False, stop=False)
                pe.matmul(out, flat(keys_lo, b)[:, cut], q_hi[:, b % 2, :], start=False, stop=True).then_inc(raw_full, 1)

            def shift(b, j):
                n, r = b * XC + j, rows_of(j)
                out = sc[0:r, n % 3, :]
                pe.wait_ge(mask_ready, n + 1)
                pe.matmul(out, head_row_r[:, j * P:j * P + r], neg_maxT[:, b % 2, :], start=False, stop=False,
                          skip_group_check=True)
                pe.matmul(out, ident_b[0:r, 0:r], mask[0:r, n % 3, :], start=False, stop=True,
                          skip_group_check=True).then_inc(shifted, 1)

            def weighted(b, j):
                n, r = b * XC + j, rows_of(j)
                first, last = j == 0, j == XC - 1
                hi, lo = p_hi[0:r, n % 4, :], p_lo[0:r, n % 4, :]
                if first:
                    wait_for(pe, group_read, b)
                    pe.wait_ge(vals_ready, (b + 1) * len(V_CHUNKS))
                pe.wait_ge(p_hi_ready, n + 1)
                pe.matmul(ov[:], vals_hi[0:r, b % 2, j, :], hi, start=first, stop=False)
                pe.matmul(ov[:], vals_lo[0:r, b % 2, j, :], hi, start=False, stop=False)
                pe.matmul(z[:], own_head_r[0:r, j, :], hi, start=first, stop=False)
                pe.wait_ge(p_lo_ready, n + 1)
                pe.matmul(ov[:], vals_hi[0:r, b % 2, j, :], lo, start=False, stop=last)
                pe.matmul(z[:], own_head_r[0:r, j, :], lo, start=False, stop=last).then_inc(chunk_done, 1)

            pe.wait_ge(xnT_ready, 4)
            for job in prep_of(-1):
                prepare(*job)
            pe.wait_ge(head_row_ready, 1)
            pe.wait_ge(consts_ready, 1)
            for n in range(B * XC + 3):
                if n < B * XC:
                    raw(n // XC, n % XC)
                    for job in prep_of(n // XC):
                        if PREP.index((job[1], job[2], job[4])) == n % XC:
                            prepare(*job)
                if 1 <= n <= B * XC:
                    shift((n - 1) // XC, (n - 1) % XC)
                if n >= 3:
                    weighted((n - 3) // XC, (n - 3) % XC)
            for job in prep_of(B):
                prepare(*job)


EXPERT_WEIGHTS = {"up": [P, E + 1, 2, HID],
                  "down": [P, HC, D], "router": [P, E], "route_bias": [P, E], "expert_no": [P, E]}
EXPERT_LOADS = 9


def mixture(nc, sb, psum, sem, t):
    x, ident = t["x"], t["ident"]
    xn = sb("xn3", [P, NT, D], F32)
    xnT_hi, xnT_lo = sb("xnT3_hi", [P, B * S], F32R), sb("xnT3_lo", [P, B * S], F32R)
    stats, moments = sb("stats3", [P, NT, 6], F32), sb("moments3", [P, NT, 2], F32)
    rstd, work = sb("rstd3", [P, 2, NT], F32), sb("work3", [P, 3, NT], F32)
    up, down, router, route_bias, expert_no = (t[n] for n in EXPERT_WEIGHTS)
    up_hi, up_lo = sb("up_hi", [P, E + 1, 2, HID], F32R), sb("up_lo", [P, E + 1, 2, HID], F32R)
    router_hi, router_lo = sb("router_hi", [P, E], F32R), sb("router_lo", [P, E], F32R)
    logits, top, place = sb("logits", [P, NT, E], F32), sb("top", [P, NT, 8], F32), sb("place", [P, NT, 8], U32)
    place_f = sb("place_f", [P, NT, 2], F32)
    gap, gap_e, weight = sb("gap", [P, NT], F32), sb("gap_e", [P, 2, NT], F32), sb("weight", [P, 2, NT], F32)
    hit, cw = sb("hit", [P, 2, NT, E], F32), sb("cw", [P, NT, E], F32)
    gate = sb("gate", [P, 3, S], F32)
    hidden = sb("hidden", [P, 3, S], F32)

    g, u, y = psum("g", [P, 3, S], F32), psum("u", [P, 3, S], F32), psum("y", [P, 2, S], F32)

    loaded, all_loaded = t["loaded"], 16 * EXPERT_LOADS
    root_wanted, root_ready, dve_chain = sem("root_wanted3"), sem("root_ready3"), sem("dve_chain3")
    xn_ready, xnT_full, xnT_hi_ready, xnT_ready = sem("xn_ready3"), sem("xnT_full3"), sem("xnT_hi_ready3"), sem("xnT_ready3")
    router_hi_ready, router_ready, up_hi_ready, up_ready = sem("router_hi_ready"), sem("router_ready"), sem("up_hi_ready"), sem("up_ready")
    logits_full, gap_ready, gap_e_ready = sem("logits_full"), sem("gap_ready"), sem("gap_e_ready")
    gu_full, gate_ready, hidden_ready = sem("gu_full"), sem("gate_ready"), sem("hidden_ready")
    y_full, y_added, stored = sem("y_full"), sem("y_added"), sem("stored")
    NE = E + 1

    with nc.Block() as block:
        @block.sync
        def _(sp):
            with sp.Fori(0, B) as b:
                sp.wait_ge(y_added, (b + 1) * NE + 1)
                sp.dma_start(t["out"][:, bass.ds(b * 4, 4), :], x[:, bass.ds(b * 4, 4), :]).then_inc(stored, 16)
            sp.wait_ge(stored, 16 * B)

        @block.gpsimd
        def _(pool):
            for n in range(NE):
                pool.wait_ge(up_hi_ready, n + 1)
                pool.tensor_tensor(up_lo[:, n], up[:, n], up_hi[:, n].bitcast(F32), ALU.subtract).then_inc(up_ready, 1)

        @block.scalar
        def _(act):
            act.wait_ge(root_wanted, 1)
            act.activation(work[:, 2, :], work[:, 0, :], ACT.Sqrt).then_inc(root_ready, 1)
            act.wait_ge(loaded, all_loaded)
            act.activation(router_hi[:], router[:], ACT.Copy).then_inc(router_hi_ready, 1)
            for n in range(3):
                act.activation(up_hi[:, n], up[:, n], ACT.Copy).then_inc(up_hi_ready, 1)
            round_tokens(act, g, xnT_hi, xnT_full, xnT_hi_ready)
            for n in range(3, NE):
                act.activation(up_hi[:, n], up[:, n], ACT.Copy).then_inc(up_hi_ready, 1)
            act.wait_ge(gap_ready, 1)
            act.activation(gap_e[:, 0, :], gap[:], ACT.Exp).then_inc(gap_e_ready, 1)
            with act.Fori(0, B) as b:
                for c in range(HC):
                    n = b * HC + c
                    act.wait_ge(gu_full, n + 1)
                    act.activation(gate[:, c % 3, :], g[:, c % 3, :], ACT.Silu).then_inc(gate_ready, 1)

        @block.vector
        def _(dve):
            chain = Chain(dve, dve_chain)
            normalize(dve, chain, x, stats, moments, rstd, work, xn, root_wanted, root_ready, xn_ready)
            dve.wait_ge(router_hi_ready, 1)
            dve.tensor_tensor(router_lo[:], router[:], router_hi[:].bitcast(F32), ALU.subtract).then_inc(router_ready, 1)
            token_rests(dve, g, xnT_hi, xnT_lo, xnT_hi_ready, xnT_ready)
            dve.wait_ge(loaded, all_loaded)
            row = lambda a: a.rearrange("p (o e) -> p o e", o=1).broadcast_to([P, NT, E])
            col = lambda a: a.rearrange("p (t o) -> p t o", o=1).broadcast_to([P, NT, E])
            dve.wait_ge(logits_full, 1)
            chain.link(dve.tensor_tensor(logits[:], y[:, 0, 0:NT * E].rearrange("p (t e) -> p t e", e=E),
                                         row(route_bias[:]), ALU.add))
            chain.wait()
            for i in range(NT):
                chain.link(dve.max(top[:, i, :], logits[:, i, :]))
            chain.wait()
            dve.tensor_tensor(gap[:], top[:, :, 1], top[:, :, 0], ALU.subtract).then_inc(gap_ready, 1)
            for i in range(NT):
                chain.link(dve.max_index(place[:, i, :], top[:, i, :], logits[:, i, :]))
            chain.wait()
            chain.link(dve.tensor_copy(place_f[:], place[:, :, 0:2]))
            dve.wait_ge(gap_e_ready, 1)
            chain.link(dve.tensor_scalar(gap_e[:, 1, :], gap_e[:, 0, :], 1.0, None, ALU.add))
            chain.wait()
            chain.link(dve.reciprocal(weight[:, 0, :], gap_e[:, 1, :]))
            chain.wait()
            chain.link(dve.tensor_tensor(weight[:, 1, :], weight[:, 0, :], gap_e[:, 0, :], ALU.mult))
            for i in range(2):
                chain.link(dve.tensor_tensor(hit[:, i], row(expert_no[:]), col(place_f[:, :, i]), ALU.is_equal))
            chain.wait()
            for i in range(2):
                chain.link(dve.tensor_tensor(hit[:, i], hit[:, i], col(weight[:, i, :]), ALU.mult))
            chain.wait()
            dve.tensor_tensor(cw[:], hit[:, 0], hit[:, 1], ALU.add).then_inc(y_added, 1)
            dve.wait_ge(y_added, 1)
            with dve.Fori(0, B) as b:
                def add(e):
                    dve.wait_ge(y_full, b * NE + e + 1)
                    tiles = bass.ds(b * 4, 4)
                    if e > 0:
                        dve.wait_ge(y_added, b * NE + e + 1)
                    if e == E:
                        last = dve.tensor_tensor(x[:, tiles, :], x[:, tiles, :],
                                                 y[:, e % 2, :].rearrange("p (t d) -> p t d", t=4), ALU.add)
                    else:
                        for i in range(4):
                            tile = bass.ds(b * 4 + i, 1)
                            rows = x[:, tile, :].rearrange("p o d -> p (o d)")
                            last = dve.scalar_tensor_tensor(out=rows, in0=y[:, e % 2, i * D:(i + 1) * D],
                                                            scalar=cw[:, tile, e:e + 1].rearrange("p o e -> p (o e)"),
                                                            in1=rows, op0=ALU.mult, op1=ALU.add)
                    last.then_inc(y_added, 1)

                for c in range(HC):
                    n = b * HC + c
                    dve.wait_ge(gate_ready, n + 1)
                    dve.tensor_tensor(hidden[:, c % 3, :], gate[:, c % 3, :], u[:, c % 3, :],
                                      ALU.mult).then_inc(hidden_ready, 1)
                    if c >= 3 and c % 2 == 1:
                        add((c - 3) // 2)
                add(E)

        @block.tensor
        def _(pe):
            transpose_tokens(pe, xn, ident, g, xn_ready, xnT_full, xnT_ready)
            pe.wait_ge(xnT_ready, 4)
            pe.wait_ge(router_ready, 1)
            for i in range(NT):
                cut, out = slice(i * P, (i + 1) * P), y[:, 0, i * E:(i + 1) * E]
                pe.matmul(out, xnT_hi[:, cut], router_hi[:], start=True, stop=False)
                pe.matmul(out, xnT_lo[:, cut], router_hi[:], start=False, stop=False)
                last = pe.matmul(out, xnT_hi[:, cut], router_lo[:], start=False, stop=True)
            last.then_inc(logits_full, 1)
            pe.wait_ge(loaded, all_loaded)

            def up_project(b, c):
                e, half = c // 2, slice(c % 2 * P, c % 2 * P + P)
                if c >= 3:
                    pe.wait_ge(hidden_ready, b * HC + c - 2)
                if c % 2 == 0:
                    pe.wait_ge(up_ready, e + 1)
                at = bass.ds(b * S, S)
                for w, bank in enumerate((g, u)):
                    out = bank[:, c % 3, :]
                    pe.matmul(out, up_hi[:, e, w, half], xnT_hi[:, at], start=True, stop=False)
                    pe.matmul(out, up_hi[:, e, w, half], xnT_lo[:, at], start=False, stop=False)
                    last = pe.matmul(out, up_lo[:, e, w, half], xnT_hi[:, at], start=False, stop=True)
                last.then_inc(gu_full, 1)

            def down_project(b, c):
                e = c // 2
                pe.wait_ge(hidden_ready, b * HC + c + 1)
                if c % 2 == 0:
                    pe.wait_ge(y_added, b * NE + max(e, 1))
                for i in range(4):
                    last = pe.matmul(y[:, e % 2, i * D:(i + 1) * D], hidden[:, c % 3, i * P:(i + 1) * P],
                                     down[:, c, :], start=(c % 2 == 0 and i == 0), stop=(c % 2 == 1),
                                     skip_group_check=True)
                if c % 2 == 1:
                    last.then_inc(y_full, 1)

            with pe.Fori(0, B) as b:
                for c in range(HC + 2):
                    if c < HC:
                        up_project(b, c)
                    if c >= 2:
                        down_project(b, c - 2)


def build(nc, t):
    with ExitStack() as all_:
        t["x"] = all_.enter_context(nc.sbuf_tensor("x_res", [P, NT, D], F32))
        t["ident"] = all_.enter_context(nc.sbuf_tensor("ident", [P, P], F32))
        t["loaded"] = all_.enter_context(nc.semaphore("experts_loaded"))
        for layer in (self_attention, cross_attention, mixture):
            if layer is cross_attention:
                for name, shape in EXPERT_WEIGHTS.items():
                    t[name] = all_.enter_context(nc.sbuf_tensor(name, shape, F32))
            with ExitStack() as own:
                layer(nc, lambda n, s, d: own.enter_context(nc.sbuf_tensor(n, s, d)),
                      lambda n, s, d: own.enter_context(nc.psum_tensor(n, s, d)),
                      lambda n: all_.enter_context(nc.semaphore(n)), t)


def kernel(**inputs):
    import numpy as np
    import concourse.bacc as bacc
    from concourse.bass_utils import run_bass_kernel_spmd

    def get(name):
        return np.asarray(inputs[name])

    def constant(a):
        return np.asarray(a, np.float32)

    pairs = np.arange(XC * P)
    pair_head = np.where(pairs < XF, pairs // XK, -1)
    feature_head = np.arange(D) // XD
    arrays = {
        "wqT": get("L0_attn_wq").T.reshape(D, C, DH),
        "wkT": get("L0_attn_wk").T.reshape(D, C, DH),
        "wvT": get("L0_attn_wv").T,
        "woT": get("L0_attn_wo").T.reshape(C // 2, P, D).transpose(1, 0, 2),
        "ident": constant(np.eye(P)),
        "xwqT": get("L0_xattn_Wq").T, "xwkT": get("L0_xattn_Wk").T,
        "xwvT": get("L0_xattn_Wv").T, "xwoT": get("L0_xattn_Wo").T,
        "xbias": np.stack([get("L0_xattn_bq"), get("L0_xattn_bk"), get("L0_xattn_bv")], 1),
        "bo": get("L0_xattn_bo"),
        "ctxT": get("ctx_1024").transpose(2, 0, 1),
        "thr": get("L0_xattn_raw_thresholds").reshape(XH, 1),
        "head_row": constant(pair_head[None, :XF] == np.arange(XH)[:, None]),
        "head_col": constant(feature_head[:, None] == np.arange(XH)[None]),
        "own_head": constant(pair_head[:, None] == feature_head[None]).reshape(XC, P, D).transpose(1, 0, 2),
        "router": get("L0_ffn_router_w").T,
        "route_bias": get("L0_ffn_experts_bias"),
        "expert_no": constant(np.arange(E)),
        "up0": get("L0_ffn_w1").transpose(1, 0, 2), "up1": get("L0_ffn_w3").transpose(1, 0, 2),
        "shared0": get("L0_ffn_sw1")[0], "shared1": get("L0_ffn_sw3")[0],
        "down": get("L0_ffn_w2").reshape(2 * E, P, D).transpose(1, 0, 2),
        "shared_down": get("L0_ffn_sw2")[0].reshape(2, P, D).transpose(1, 0, 2),
        "x": get("x"),
    }
    nc = bacc.Bacc("TRN2", target_bir_lowering=False, num_devices=1)
    t, feeds = {}, {}
    for name, a in arrays.items():
        a = np.ascontiguousarray(a)
        feeds[f"in_{name}"] = a
        t[f"{name}_in"] = nc.dram_tensor(f"in_{name}", a.shape, F32, kind="ExternalInput").ap()
    by_tile = "b (t p) d -> p (b t) d"
    t["x_in"] = t["x_in"].rearrange(by_tile, p=P)
    t["out"] = nc.dram_tensor("out", (B, S, D), F32, kind="ExternalOutput").ap().rearrange(by_tile, p=P)
    build(nc, t)
    result = run_bass_kernel_spmd(nc, [feeds], core_ids=[0])
    return result.results[0]["out"]
```

```python
from contextlib import ExitStack

import concourse.bass as bass
from concourse import mybir

F32 = mybir.dt.float32
F32R = mybir.dt.float32r
U32 = mybir.dt.uint32
BF16 = mybir.dt.bfloat16
ALU = mybir.AluOpType
ACT = mybir.ActivationFunctionType
AX = mybir.AxisListType

P = 128
B, S, D = 4, 512, 128
NT = B * S // P
EPS = 1e-5
MASKED = -1e30

C, DH = 16, 64
GT = 32
POS = GT * C
HG = 8
PT = HG * GT
PARTS = B * S // PT
KB = POS // P
STEPS = HG * KB
LAG_ST, LAG_SM = 3, 11
FIRST_MEANS, MEANS_EARLY = 5, NT - PT // P
EARLY_TILES, LATE_TILES = slice(0, MEANS_EARLY), slice(MEANS_EARLY, NT)
FIRST_BATCHES, LAST_BATCH = slice(0, NT - 4), slice(NT - 4, NT)
VL = DH + 2

XH, XD, XK = 16, 8, 77
XF = XH * XK
HF, HD = XF // 2, D // 2
HX = (HF + P - 1) // P
XC = 2 * HX
XL = HF - (HX - 1) * P

E, HID = 8, 256
HC = (E + 1) * HID // P


def wait_for(eng, sem, count):
    if not (isinstance(count, int) and count <= 0):
        eng.wait_ge(sem, count)


class Chain:

    def __init__(self, eng, sem):
        self.eng, self.sem, self.count = eng, sem, 0

    def link(self, instruction):
        self.count += 1
        instruction.then_inc(self.sem, 1)
        return instruction

    def wait(self):
        self.eng.wait_ge(self.sem, self.count)


def means(dve, chain, x, stats, moments, tiles=range(NT)):
    for t in tiles:
        chain.link(dve.bn_stats(stats[:, t, :], x[:, t, :]))
    chain.wait()
    for t in tiles:
        chain.link(dve.bn_aggr(moments[:, t, :], stats[:, t, :]))


def inverse_roots(dve, chain, moments, rstd, work, root_wanted, root_ready, tiles=slice(0, NT), turn=1):
    chain.wait()
    var = work[:, 0, tiles]
    dve.tensor_scalar(var, moments[:, tiles, 1], EPS, None, ALU.add).then_inc(root_wanted, 1)
    dve.wait_ge(root_ready, turn)
    chain.link(dve.reciprocal(rstd[:, 0, tiles], work[:, 2, tiles]))
    chain.wait()
    chain.link(dve.tensor_tensor(work[:, 1, tiles], rstd[:, 0, tiles], rstd[:, 0, tiles], ALU.mult))
    chain.wait()
    chain.link(dve.tensor_tensor(work[:, 1, tiles], work[:, 1, tiles], var, ALU.mult))
    chain.wait()
    chain.link(dve.tensor_scalar(work[:, 1, tiles], work[:, 1, tiles], -0.5, 1.5, ALU.mult, ALU.add))
    chain.wait()
    chain.link(dve.tensor_tensor(rstd[:, 1, tiles], rstd[:, 0, tiles], work[:, 1, tiles], ALU.mult))
    chain.wait()


def root(act, work, root_wanted, root_ready, tiles=slice(0, NT), turn=1):
    act.wait_ge(root_wanted, turn)
    act.activation(work[:, 2, tiles], work[:, 0, tiles], ACT.Sqrt).then_inc(root_ready, 1)


def normalize_batch(dve, b, x, moments, rstd, xn, xn_ready):
    for i in range(4 * b, 4 * b + 4):
        last = dve.tensor_scalar(xn[:, i, :], x[:, i, :], moments[:, i, 0:1], rstd[:, 1, i:i + 1],
                                 ALU.subtract, ALU.mult)
    last.then_inc(xn_ready, 1)


def statistics(dve, chain, x, stats, moments, rstd, work, root_wanted, root_ready):
    means(dve, chain, x, stats, moments)
    inverse_roots(dve, chain, moments, rstd, work, root_wanted, root_ready)


JOBS = {1: ("xt", 0), 2: ("wo", 0), **{s: ("qk", s - 3) for s in range(3, 19)},
        19: ("v", 0), 22: ("v", 1), 26: ("v", 2), 31: ("v", 3)}
ORDER = list(JOBS.values())
FIRST_JOBS = [j for j in ORDER if j[0] != "wo"]


WEIGHT_PIECES = [(w, slice(c, c + C // 4)) for c in range(0, C, C // 4) for w in range(2)]

START = [("s", 0), ("s", 1), ("s", 2), ("s", 3), ("v", 0), ("turn", 0), ("s", 4), ("v", 1), ("s", 5), ("st", 0),
         ("s", 6), ("st", 1), ("v", 2), ("s", 7), ("s", 8), ("v", 3), ("st", 2), ("s", 9), ("turn", 1), ("s", 10)]


def jobs_of(has_before, has_next):
    return {s: j for s, j in JOBS.items() if (has_before if j[0] == "wo" else has_next)}


def jobs_before(part):
    return (part + 1) * len(FIRST_JOBS)


def job_before(job, part, jobs):
    n = ORDER.index(job) - 2
    while n >= 0 and ORDER[n] not in jobs:
        n -= 2
    return (ORDER[n], part) if n >= 0 else (ORDER[n], part - 1)


def self_attention(nc, sb, psum, sem, t):
    x = t["x"]
    xn = sb("xn_part", [P, PT // P, D], F32)
    xT_hi, xT_lo = sb("xT_hi", [P, PT], F32R), sb("xT_lo", [P, PT], F32R)
    x_part = sb("x_part", [P, PT], F32)
    w_hi = t["wqk_hi"]
    w_lo = t["wqk_lo"]
    wvT, woT = sb("wvT", [P, C * DH], F32), sb("woT", [P, C // 2, D], F32)
    qk = [sb(f"qk{s}", [P, 2, HG, C, GT], F32R) for s in range(2)]
    q_lo = [sb(f"q_lo{s}", [P, HG, C, GT], F32R) for s in range(2)]
    keys_ones = sb("keys_ones", [P, 2, POS], F32R)
    v_hi = sb("v_hi", [P, HG, KB, 2, DH], F32R)
    v_lo = sb("v_lo", [P, HG, KB, VL], F32R)
    probs = sb("probs", [P, 2, POS], F32)
    p_hi, p_lo = sb("p_hi", [P, 4, POS], F32R), sb("p_lo", [P, 4, POS], F32R)
    attn = sb("attn", [P, C // 2, PT], F32)
    neg_max = sb("neg_max", [P, 4, KB], F32)
    turned_and_inverse = sb("turned_and_inverse", [P, POS], F32)
    turned, inv_sum = turned_and_inverse[0:DH, :], turned_and_inverse[DH:P, 0:POS // 32]
    moments, rstd = sb("moments", [P, NT, 2], F32), sb("rstd", [P, 2, NT], F32)
    stats = probs[:, 0, 0:NT * 6].rearrange("p (t n) -> p t n", n=6)
    work = probs[:, 1, 0:NT * 3].rearrange("p (n t) -> p n t", t=NT)
    ident = t["ident"]
    w_raw = attn[:].rearrange("p a b -> p (a b)").rearrange("p (w c d) -> p w c d", w=2, c=C)

    sc = psum("scores", [P, 2, POS], F32)
    st = psum("scoresT", [P, 2, POS], F32)
    ov = psum("out_and_sum", [P, 2, POS], F32)
    pj = psum("projected", [P, 2, POS], F32)

    x_loaded, w_loaded, wv_loaded = sem("x_loaded"), sem("w_loaded"), sem("wv_loaded")
    root_wanted, root_ready = sem("root_wanted"), sem("root_ready")
    dve_chain = sem("dve_chain")
    xn_ready, xT_hi_ready, xT_ready = sem("xn_ready"), sem("xT_hi_ready"), sem("xT_ready")
    w_hi_ready, w_ready, w_rest_ready, ones_ready = sem("w_hi_ready"), sem("w_ready"), sem("w_rest_ready"), sem("ones_ready")
    x_part_ready = sem("x_part_ready")
    job_full, hi_ready, qk_ready = sem("job_full"), sem("hi_ready"), sem("qk_ready")
    v_hi_ready, v_ready = sem("v_hi_ready"), sem("v_ready")
    x_added = sem("x_added")
    sc_full, max_ready = sem("sc_full"), sem("max_ready")
    max_turned, max_rows_ready = sem("max_turned"), sem("max_rows_ready")
    keys_ones_ready = sem("keys_ones_ready")
    st_full, p_hi_ready, p_lo_ready = sem("st_full"), sem("p_hi_ready"), sem("p_lo_ready")
    ov_full, div_step, inv_ready, attn_ready = sem("ov_full"), sem("div_step"), sem("inv_ready"), sem("attn_ready")
    wo_full = sem("wo_full")

    def freed(job, part):
        kind, i = job
        if kind == "xt":
            return xT_ready, part + 2
        if kind == "qk":
            return qk_ready, (part + 1) * C + i + 1
        if kind == "v":
            return v_ready, (part + 1) * (HG // 2) + i + 1
        return x_added, part

    def bank_of(job, part):
        kind, i = job
        if kind == "qk" and isinstance(part, int) and part < 0:
            return (pj, ov)[i // 2 % 2][:, i % 2, :]
        return pj[:, ORDER.index(job) % 2, :]

    def twice(a):
        return a.rearrange("p c (o d) -> p c o d", o=1).broadcast_to([P, C // 4, 2, DH])

    def weights_low(eng, pieces):
        for n in pieces:
            w, cs = WEIGHT_PIECES[n]
            eng.wait_ge(w_hi_ready, n + 1)
            eng.tensor_tensor(w_lo[:, w, cs], twice(w_raw[:, w, cs]), w_hi[:, w, cs].bitcast(F32), ALU.subtract)\
               .then_inc(w_ready if n < 2 else w_rest_ready, 1)

    def for_parts(eng, steps):
        steps(0, 0, False, True)
        with eng.Fori(0, (PARTS - 2) // 2) as r:
            steps(r * 2 + 1, 1, True, True)
            steps(r * 2 + 2, 0, True, True)
        steps(PARTS - 1, (PARTS - 1) % 2, True, False)

    with nc.Block() as block:
        @block.sync
        def _(sp):
            for q in range(4):
                sp.dma_start(x[:, 4 * q:4 * q + 4, :], t["x_in"][:, 4 * q:4 * q + 4, :]).then_inc(x_loaded, 16)
            sp.dma_start(ident[:], t["ident_in"]).then_inc(w_loaded, 16)
            sp.dma_start(w_raw[:, 0], t["wqT_in"]).then_inc(w_loaded, 16)
            sp.dma_start(w_raw[:, 1], t["wkT_in"]).then_inc(w_loaded, 16)
            sp.dma_start(wvT[:], t["wvT_in"]).then_inc(wv_loaded, 16)
            sp.dma_start(woT[:], t["woT_in"]).then_inc(wv_loaded, 16)
            sp.wait_ge(job_full, jobs_before(PARTS - 1))
            for name in EARLY:
                source = t["bo_in"].partition_broadcast(P) if name == "bo" else t[f"{name}_in"]
                sp.dma_start(t[name], source).then_inc(t["early_loaded"], 16)

        @block.gpsimd
        def _(pool):
            for s in range(2):
                pool.memset(q_lo[s][:].bitcast(F32), 0.0).then_inc(ones_ready, 1)
            pool.memset(keys_ones[:].bitcast(F32), 1.0).then_inc(ones_ready, 1)
            pool.memset(v_hi[:, :, :, 1, :].bitcast(F32), 1.0).then_inc(ones_ready, 1)
            pool.memset(v_lo[:, :, :, DH:VL].bitcast(F32), 0.0).then_inc(ones_ready, 1)

            def whole_tokens(target):
                pool.wait_ge(xT_ready, target + 1)
                pool.tensor_tensor(x_part[:], xT_hi[:].bitcast(F32), xT_lo[:].bitcast(F32), ALU.add)\
                    .then_inc(x_part_ready, 1)

            def low_probs(m, ml):
                pool.wait_ge(p_hi_ready, m + 1)
                pool.tensor_tensor(p_lo[:, ml % 4], probs[:, ml % 2], p_hi[:, ml % 4].bitcast(F32),
                                   ALU.subtract).then_inc(p_lo_ready, 1)

            def steps(part, slot, has_before, has_next):
                for k in range(STEPS):
                    if has_next or k + LAG_ST < STEPS:
                        low_probs(part * STEPS + k + LAG_ST, k + LAG_ST)
                    if k == 6 and has_next:
                        whole_tokens(part + 1)

            weights_low(pool, range(2, len(WEIGHT_PIECES)))
            whole_tokens(0)
            for m in range(LAG_ST):
                low_probs(m, m)
            for_parts(pool, steps)

        @block.scalar
        def _(act):
            root(act, work, root_wanted, root_ready)
            act.wait_ge(w_loaded, 48)
            for w, cs in WEIGHT_PIECES:
                act.activation(w_hi[:, w, cs], twice(w_raw[:, w, cs]), ACT.Copy).then_inc(w_hi_ready, 1)

            def evacuate(job, slot, part):
                (kind, i), bank = job, bank_of(job, part)
                if kind == "xt":
                    act.activation(xT_hi[:], bank[:, 0:PT], ACT.Copy).then_inc(xT_hi_ready, 1)
                elif kind == "qk":
                    act.activation(qk[slot][:, :, :, i, :], bank.rearrange("p (w g t) -> p w g t", w=2, g=HG),
                                   ACT.Copy).then_inc(hi_ready, 1)
                elif kind == "v":
                    act.activation(v_hi[:, 2 * i:2 * i + 2, :, 0, :],
                                   bank.rearrange("p (g b d) -> p g b d", g=2, b=KB),
                                   ACT.Copy).then_inc(v_hi_ready, 1)

            def exponentials(m, ml):
                act.wait_ge(st_full, m + 1)
                wait_for(act, p_lo_ready, m - 1)
                act.activation(probs[:, ml % 2, :], st[:, ml % 2, :], ACT.Exp, scale=DH ** -0.5)
                act.activation(p_hi[:, ml % 4, :], st[:, ml % 2, :], ACT.Exp, scale=DH ** -0.5).then_inc(p_hi_ready, 1)

            def steps(part, slot, has_before, has_next):
                jobs = jobs_of(has_before, has_next)
                for k in range(STEPS):
                    if has_next or k + LAG_ST < STEPS:
                        exponentials(part * STEPS + k + LAG_ST, k + LAG_ST)
                    if k % KB == 1 and (has_next or k + 2 * KB < STEPS):
                        ahead = k // KB + 2
                        high_keys(part * HG + ahead, ahead, part + ahead // HG, slot)
                    if k in jobs and jobs[k][0] != "wo":
                        act.wait_ge(job_full, jobs_before(part) + FIRST_JOBS.index(jobs[k]) + 1)
                        evacuate(jobs[k], 1 - slot, part)
                    if k % KB == 2 and (has_next or k // KB + 2 < HG):
                        ahead = k // KB + 2
                        max_rows(part * HG + ahead, ahead, slot)

            def max_rows(g, gl, slot):
                act.wait_ge(max_turned, g + 1)
                row = q_lo[slot if gl < HG else 1 - slot][0:KB, gl % HG].rearrange("p c t -> p (c t)")
                for b in range(KB):
                    last = act.activation(row[:, b * P:(b + 1) * P], ov[0:KB, (gl + 1) % 2, 0:P], ACT.Copy,
                                          scale=ident[0:KB, b:b + 1])
                last.then_inc(max_rows_ready, 1)

            def high_keys(g, gl, own_part, slot):
                s = slot if gl < HG else 1 - slot
                act.wait_ge(hi_ready, (own_part + 1) * C)
                act.activation(keys_ones[DH:P, gl % 2, :], qk[s][0:DH, 1, gl % HG].rearrange("p c t -> p (c t)"),
                               ACT.Copy).then_inc(keys_ones_ready, 1)

            def first(job):
                act.wait_ge(job_full, FIRST_JOBS.index(job) + 1)
                evacuate(job, 0, -1)

            for job in FIRST_JOBS:
                if job[0] != "v":
                    first(job)
            act.wait_ge(ones_ready, 5)
            for g in range(2):
                high_keys(g, g, 0, 0)
            for kind, i in START:
                if kind == "v":
                    first((kind, i))
                elif kind == "turn":
                    max_rows(i, i, 0)
                elif kind == "st":
                    exponentials(i, i)
            for_parts(act, steps)
            root(act, t["work2"], root_wanted, root_ready, EARLY_TILES, 2)

        @block.vector
        def _(dve):
            chain = Chain(dve, dve_chain)
            dve.wait_ge(x_loaded, 64)
            statistics(dve, chain, x, stats, moments, rstd, work, root_wanted, root_ready)

            def tokens(target):
                for i in range(PT // P):
                    tile = bass.ds(target * (PT // P) + i, 1)
                    last = dve.tensor_scalar(xn[:, i, :], x[:, tile, :].rearrange("p o d -> p (o d)"),
                                             moments[:, tile, 0:1].rearrange("p o e -> p (o e)"),
                                             rstd[:, 1, tile], ALU.subtract, ALU.mult)
                last.then_inc(xn_ready, 1)

            tokens(0)
            weights_low(dve, range(2))

            def maximum(m, ml):
                dve.wait_ge(sc_full, m + 1)
                dve.tensor_reduce(neg_max[:, ml // KB % 4, ml % KB:ml % KB + 1], sc[:, ml % 2, :], AX.X, ALU.max,
                                  negate=True).then_inc(max_ready, 1)

            def rest(job, slot, part):
                (kind, i), bank = job, bank_of(job, part)
                half = bank.rearrange("p (w g t) -> p w g t", w=2, g=HG)
                if kind == "xt":
                    dve.wait_ge(xT_hi_ready, part + 2)
                    dve.tensor_tensor(xT_lo[:], bank[:, 0:PT], xT_hi[:].bitcast(F32), ALU.subtract).then_inc(xT_ready, 1)
                elif kind == "v":
                    dve.wait_ge(v_hi_ready, (part + 1) * (HG // 2) + i + 1)
                    flat = lambda a: a.rearrange("p g b d -> p (g b) d")
                    dve.tensor_tensor(flat(v_lo[:, 2 * i:2 * i + 2, :, 0:DH]),
                                      bank.rearrange("p (n d) -> p n d", d=DH),
                                      flat(v_hi[:, 2 * i:2 * i + 2, :, 0, :]).bitcast(F32),
                                      ALU.subtract).then_inc(v_ready, 1)
                elif kind == "qk":
                    dve.wait_ge(hi_ready, (part + 1) * C + i + 1)
                    dve.tensor_tensor(q_lo[slot][DH:P, :, i, :], half[DH:P, 0], qk[slot][DH:P, 0, :, i, :].bitcast(F32),
                                      ALU.subtract)
                    k_lo = qk[slot][DH:P, 1, :, i, :]
                    dve.tensor_tensor(k_lo, half[DH:P, 1], k_lo.bitcast(F32), ALU.subtract).then_inc(qk_ready, 1)
                elif kind == "wo":
                    dve.wait_ge(wo_full, part)
                    tiles = bass.ds((part - 1) * (PT // P), PT // P)
                    dve.tensor_tensor(x[:, tiles, :], x[:, tiles, :], bank[:, 0:PT].rearrange("p (n d) -> p n d", d=D),
                                      ALU.add).then_inc(x_added, 1)

            def divide_first(g, gl):
                done = g * 2
                dve.wait_ge(ov_full, g + 1)
                wait_for(dve, attn_ready, g)
                dve.transpose(turned, ov[DH:P, gl % 2, :]).then_inc(div_step, 1)
                dve.wait_ge(div_step, done + 1)
                dve.reciprocal(inv_sum, turned.rearrange("p (n r) -> p n r", r=32)[:, :, 0]).then_inc(div_step, 1)

            def divide_last(g, gl):
                dve.wait_ge(div_step, g * 2 + 2)
                dve.transpose(turned, inv_sum.rearrange("p (n o) -> p n o", o=1).broadcast_to([DH, POS // 32, 32]))\
                   .then_inc(inv_ready, 1)
                dve.wait_ge(inv_ready, g + 1)
                for odd in range(2):
                    view = lambda a: a.rearrange("p (c t) -> p c t", c=C)[:, odd::2, :]
                    out = dve.tensor_tensor(attn[DH * odd:DH * odd + DH, :, gl * GT:(gl + 1) * GT],
                                            view(ov[0:DH, gl % 2, :]), view(turned), ALU.mult)
                out.then_inc(attn_ready, 1)

            def steps(part, slot, has_before, has_next):
                jobs = jobs_of(has_before, has_next)
                for k in range(STEPS):
                    if k == 0 and has_next:
                        tokens(part + 1)
                    if has_next or k + LAG_SM < STEPS:
                        maximum(part * STEPS + k + LAG_SM, k + LAG_SM)
                    if k % KB == KB - 1:
                        divide_first(part * HG + k // KB, k // KB)
                    if k in jobs:
                        rest(jobs[k], 1 - slot, part)
                    if not has_next and FIRST_MEANS <= k <= FIRST_MEANS + MEANS_EARLY:
                        if k == FIRST_MEANS:
                            dve.wait_ge(job_full, jobs_before(PARTS - 1))
                            dve.wait_ge(x_added, PARTS - 1)
                        if k > FIRST_MEANS:
                            chain.wait()
                            tile = k - FIRST_MEANS - 1
                            chain.link(dve.bn_aggr(t["moments2"][:, tile, :], t["stats2"][:, tile, :]))
                        if k < FIRST_MEANS + MEANS_EARLY:
                            chain.link(dve.bn_stats(t["stats2"][:, k - FIRST_MEANS, :], x[:, k - FIRST_MEANS, :]))
                    if k % KB == 0 and (k > 0 or has_before):
                        if k == KB:
                            wait_for(dve, wo_full, part)
                        divide_last(part * HG + k // KB - 1, (k // KB - 1) % HG)

            dve.wait_ge(ones_ready, 5)
            for job in FIRST_JOBS:
                if job[0] != "v":
                    rest(job, 0, -1)
            for kind, i in START:
                if kind == "v":
                    rest((kind, i), 0, -1)
                elif kind == "s":
                    maximum(i, i)
            for_parts(dve, steps)
            divide_last(PARTS * HG - 1, HG - 1)
            chain.wait()
            inverse_roots(dve, chain, t["moments2"], t["rstd2"], t["work2"], root_wanted, root_ready, EARLY_TILES, 2)
            for b in range(2):
                normalize_batch(dve, b, x, t["moments2"], t["rstd2"], t["xn2"], t["xn2_ready"])
            rest(("wo", 0), 0, PARTS)

        @block.tensor
        def _(pe):
            pe.wait_ge(w_loaded, 48)

            def project(job, target, free, part):
                (kind, i), bank = job, bank_of(job, part)
                if free is not None:
                    wait_for(pe, *free)
                if kind == "xt":
                    pe.wait_ge(xn_ready, target + 1)
                    for n in range(PT // P):
                        last = pe.transpose(bank[:, n * P:(n + 1) * P], xn[:, n, :], ident[:])
                elif kind == "qk":
                    if i == 0:
                        pe.wait_ge(xT_ready, target + 1)
                        pe.wait_ge(w_ready, 2)
                    elif i % 4 == 0 and isinstance(part, int) and part < 0:
                        pe.wait_ge(w_rest_ready, i // 2)
                    for w in range(2):
                        out = bank[:, w * PT:(w + 1) * PT]
                        hi = w_hi[:, w, i].rearrange("p o d -> p (o d)")
                        lo = w_lo[:, w, i].rearrange("p o d -> p (o d)")
                        pe.matmul(out, hi, xT_hi[:], start=True, stop=False)
                        pe.matmul(out, hi, xT_lo[:], start=False, stop=False)
                        last = pe.matmul(out, lo, xT_hi[:], start=False, stop=True)
                elif kind == "v":
                    if i == 0:
                        pe.wait_ge(x_part_ready, target + 1)
                    wv = wvT[:].rearrange("p (b j d) -> p b j d", b=KB, j=4)
                    for e in range(2):
                        gl = 2 * i + e
                        for j in range(4):
                            last = pe.matmul(bank[GT * j:GT * j + GT, e * 256:(e + 1) * 256],
                                             x_part[:, gl * GT:(gl + 1) * GT], wv[:, :, j, :], start=True, stop=True)
                else:
                    for n in range(PT // P):
                        pe.wait_ge(attn_ready, target * HG + (n + 1) * (P // GT))
                        for c in range(C // 2):
                            last = pe.matmul(bank[:, n * D:(n + 1) * D], attn[:, c, n * P:(n + 1) * P], woT[:, c, :],
                                             start=(c == 0), stop=(c == C // 2 - 1))
                    last.then_inc(wo_full, 1)
                    return
                last.then_inc(job_full, 1)

            def scores(m, ml, slot):
                b, g = ml % KB, ml // KB % HG
                wait_for(pe, max_ready, m - 1)
                flat = lambda w: qk[slot][:, w, g].rearrange("p c t -> p (c t)")
                pe.matmul(sc[:, ml % 2, :], flat(0)[:, b * P:(b + 1) * P], flat(1), start=True, stop=True)\
                  .then_inc(sc_full, 1)

            def turn_maxima(g, gl):
                pe.wait_ge(max_ready, (g + 1) * KB)
                pe.transpose(ov[0:KB, (gl + 1) % 2, 0:P], neg_max[:, gl % 4, :], ident[:]).then_inc(max_turned, 1)

            def weighted(m, ml, g, has_next):
                b, gl = ml % KB, ml // KB % HG
                pe.wait_ge(p_hi_ready, m + 1)
                if b == 0:
                    wait_for(pe, attn_ready, g - 1)
                    if has_next or gl + 1 < HG:
                        pe.wait_ge(max_rows_ready, g + 2)
                hi = v_hi[:, gl, b].rearrange("p o d -> p (o d)")
                pe.matmul(ov[:, gl % 2, :], hi, p_hi[:, ml % 4, :], start=(b == 0), stop=False)
                pe.matmul(ov[0:VL, gl % 2, :], v_lo[:, gl, b], p_hi[:, ml % 4, :], start=False, stop=False)
                pe.wait_ge(p_lo_ready, m + 1)
                last = pe.matmul(ov[:, gl % 2, :], hi, p_lo[:, ml % 4, :], start=False, stop=(b == KB - 1))
                if b == KB - 1:
                    last.then_inc(ov_full, 1)

            def scores_t_of(part, k, slot):
                b = k % KB
                g_of = k // KB % HG
                s = slot if k < STEPS else 1 - slot
                flat = lambda w: qk[s][:, w, g_of].rearrange("p c t -> p (c t)")
                keys = flat(1)[:, b * P:(b + 1) * P]
                out = st[:, k % 2, :]
                wait_for(pe, p_hi_ready, part * STEPS + k - 1)
                pe.matmul(out, keys, flat(0), start=True, stop=False)
                if b == 0:
                    pe.wait_ge(max_rows_ready, part * HG + k // KB + 1)
                    pe.wait_ge(keys_ones_ready, part * HG + k // KB + 1)
                pe.matmul(out, keys_ones[:, k // KB % 2, b * P:(b + 1) * P],
                          q_lo[s][:, g_of].rearrange("p c t -> p (c t)"), start=False, stop=True).then_inc(st_full, 1)

            def steps(part, slot, has_before, has_next):
                jobs = jobs_of(has_before, has_next)
                for k in range(STEPS):
                    if k % (2 * KB) == 0:
                        pe.wait_ge(v_ready, part * (HG // 2) + k // (2 * KB) + 1)
                    weighted(part * STEPS + k, k, part * HG + k // KB, has_next)
                    if has_next or k + LAG_ST < STEPS:
                        scores_t_of(part, k + LAG_ST, slot)
                    if has_next or k + LAG_SM < STEPS:
                        ahead = k + LAG_SM
                        if ahead == STEPS:
                            pe.wait_ge(qk_ready, (part + 2) * C)
                        scores(part * STEPS + ahead, ahead, slot if ahead < STEPS else 1 - slot)
                    if k in jobs:
                        job = jobs[k]
                        project(job, part - 1 if job[0] == "wo" else part + 1,
                                freed(*job_before(job, part, jobs.values())), part)
                    if k % KB == 2 and (has_next or k // KB + 2 < HG):
                        wait_for(pe, attn_ready, part * HG + k // KB)
                        turn_maxima(part * HG + k // KB + 2, k // KB + 2)

            for job in FIRST_JOBS:
                if job[0] != "v":
                    project(job, 0, (qk_ready, job[1] - 3) if job[0] == "qk" else None, -1)
            pe.wait_ge(qk_ready, C)
            pe.wait_ge(ones_ready, 5)
            pe.wait_ge(wv_loaded, 32)
            for kind, i in START:
                if kind == "s":
                    scores(i, i, 0)
                elif kind == "v":
                    project((kind, i), 0, (v_ready, i - 1), -1)
                elif kind == "turn":
                    turn_maxima(i, i)
                else:
                    scores_t_of(0, i, 0)
            for_parts(pe, steps)
            project(("wo", 0), PARTS - 1, freed(("wo", 0), PARTS - 1), PARTS)


EARLY = {"xwqT": (P, D), "xwkT": (P, D), "xwvT": (P, D), "xwoT": (P, D), "xbias": (P, 3), "ctxT": (P, B * XK),
         "thr": (XH, 1), "head_row": (XH, XF), "head_col": (P, XH), "bo": (P, D), "own_head": (P, XC * HD)}

PREP = [("xt", 0, (2,), 0), ("v", 0, (0,), 0), ("v", 1, (1,), 1), ("q", 0, (0,), 2), ("v", 2, (1,), 3),
        ("max", 0, (0, 1, 2), 4), ("max", 1, (0, 1, 2), 5), ("max", 2, (0, 1, 2), 6), ("max", 3, (0, 1, 2), 7),
        ("turn", 0, (0,), 8), ("wo", 0, (1,), 9)]
V_CHUNKS = [range(0, HX - 1), range(HX, XC - 1), range(HX - 1, XC, HX)]
MAX_HEADS = [range(0, 6), range(6, 12), range(12, 16)]


def prepare_plan():
    plan, reader = [], {}
    for round_ in range(-1, B + 1):
        for kind, i, banks, chunk in PREP:
            if round_ < 0 and kind == "max" and i % 2 == 1:
                banks = (3, 4, 5)
            batch = round_ - 1 if kind == "wo" else round_ + 1
            if 0 <= batch < B:
                needs = max([reader[b] + 1 for b in banks if b in reader], default=0)
                for b in banks:
                    reader[b] = len(plan)
                plan.append((kind, i, batch, banks, needs, round_, chunk))
    return plan


PLAN = prepare_plan()


KEYS_AT = (0, 1, 2, 3)


def rows_of(j):
    return P if j % HX < HX - 1 else XL


def pairs_of(j):
    at = j // HX * HF + j % HX * P
    return slice(at, at + rows_of(j))


def features_of(j):
    return slice(j // HX * HD, j // HX * HD + HD)


def cross_attention(nc, sb, psum, sem, t):
    x, ident = t["x"], t["ident"]
    xn = t["xn2"]
    xnT_hi, xnT_lo = sb("xnT2_hi", [P, B * S], F32R), sb("xnT2_lo", [P, B * S], F32R)
    stats, moments = t["stats2"], t["moments2"]
    stats3, moments3 = t["stats3"], t["moments3"]
    rstd, work = t["rstd2"], t["work2"]
    wqT, wkT, wvT, woT = (t[n] for n in ("xwqT", "xwkT", "xwvT", "xwoT"))
    wq_hi, wq_lo = sb("xwq_hi", [P, D], F32R), sb("xwq_lo", [P, D], F32R)
    bias = t["xbias"]
    bo = t["bo"]
    ctxT = t["ctxT"]
    ctx_rep = sb("ctx_rep", [P, B, XF], F32)
    ctx_sum, v_sum = sb("ctx_sum", [P, B], F32), sb("v_sum", [P, B], F32)
    own_head = t["own_head"]
    head_row, head_row_r = t["head_row"], sb("head_row_r", [XH, XF], F32R)
    head_col = t["head_col"]
    k_all = sb("k_all", [P, B, XK], F32)
    k_hi, k_lo = sb("k_hi", [P, B, XK], F32R), sb("k_lo", [P, B, XK], F32R)
    keys_hi, keys_lo = sb("keys_hi", [P, 2, XH, XK], F32R), sb("keys_lo", [P, 2, XH, XK], F32R)
    vals = sb("vals", [P, XC, HD], F32)
    vals_hi, vals_lo = sb("vals_hi", [P, 2, XC, D], F32R), sb("vals_lo", [P, 2, XC, D], F32R)
    q_hi, q_lo = sb("q2_hi", [P, 2, S], F32R), sb("q2_lo", [P, 2, S], F32R)
    neg_max, neg_maxT = sb("neg_max2", [P, 4, XH], F32), sb("neg_maxT", [XH, 2, S], F32R)
    thr = sb("thr_work", [XH, 6], F32)
    thr_col = sb("thr_col", [P, XC], F32)
    ident_b, mask = sb("ident_b", [P, P], BF16), sb("mask", [P, 3, S], BF16)
    e, p_hi, p_lo = sb("e", [P, 2, S], F32), sb("e_hi", [P, 4, S], F32R), sb("e_lo", [P, 4, S], F32R)
    none, total, inv, num, sums, outs = (sb(n, [P, S], F32) for n in ("none", "total", "inv", "num", "sums", "outs"))
    few = sb("few", [P, S // 32, 32 // XD], F32)
    out_T = sb("out_T", [P, S], F32)

    sc = psum("scores2", [P, 3, S], F32)
    pb = psum("prepare", [P, 3, S], F32)
    acc = psum("out_and_sum2", [P, 2, S], F32)

    loaded, all_loaded, rep_in = t["early_loaded"], 16 * len(EARLY), [sem(f"rep{b}_loaded") for b in range(B)]
    root_wanted, root_ready, dve_chain = sem("root_wanted2"), sem("root_ready2"), sem("dve_chain2")
    xn_ready, xnT_hi_ready = t["xn2_ready"], sem("xnT_hi_ready2")
    w_hi_ready, w_ready, head_row_ready = sem("xw_hi_ready"), sem("xw_ready"), sem("head_row_ready")
    sum_ready, first_full = sem("sum_ready"), sem("first_full")
    k_ready, k_hi_ready, k_split = sem("k_ready"), sem("k_hi_ready"), sem("k_split")
    thr_step, thr_done, thr_full, setup_read = sem("thr_step"), sem("thr_done"), sem("thr_full"), sem("setup_read")
    bo_added, keys_ready = sem("bo_added"), sem("keys_ready")
    prep_full, prep_read, q_hi_ready = sem("prep_full"), sem("prep_read"), sem("q2_hi_ready")
    raw_full, mask_ready, shifted = sem("raw_full"), sem("mask_ready"), sem("shifted")
    p_hi_ready, p_lo_ready = sem("e_hi_ready"), sem("e_lo_ready")
    vals_hi_ready, vals_ready = sem("vals_hi_ready"), sem("vals_ready")
    group_read, num_ready, outT_ready = sem("group_read"), sem("num_ready"), sem("outT_ready")
    chunk_done, consts_ready, zeros_ready, taken = sem("chunk_done"), sem("consts_ready"), sem("zeros_ready"), sem("taken")

    index = {(kind, i, batch): n for n, (kind, i, batch, *_) in enumerate(PLAN)}
    cuts = [slice(h.start, h.stop) for h in MAX_HEADS]

    def v_pieces(i):
        js = V_CHUNKS[i]
        chunks = [js] if i < 2 else [range(j, j + 1) for j in js]
        return [(rows_of(c[0]), slice(c.start, c.stop), features_of(c[0])) for c in chunks]

    first_half, second_half = slice(0, HX), slice(HX, XC)
    low, high = slice(0, HD), slice(HD, D)

    def prep_of(round_):
        return [(n, *j[:5]) for n, j in enumerate(PLAN) if j[5] == round_]

    def prep_at(batch, chunk):
        return [(n, *j[:5]) for n, j in enumerate(PLAN) if j[5:] == (batch, chunk)]

    def bank(n):
        return pb[:, n, :] if n < 3 else sc[:, n - 3, :]

    with nc.Block() as block:
        @block.sync
        def _(sp):
            for b in range(B):
                src = t["ctxT_in"][:, b, :].rearrange("p (o k) -> p o k", o=1).broadcast_to([P, XH, XK])
                sp.dma_start(ctx_rep[:, b, :].rearrange("p (h k) -> p h k", h=XH), src).then_inc(rep_in[b], 16)
            sp.dma_start(t["router"][:], t["router_in"]).then_inc(t["loaded"], 16)
            sp.dma_start(t["route_bias"][:], t["route_bias_in"].partition_broadcast(P)).then_inc(t["loaded"], 16)
            sp.dma_start(t["expert_no"][:], t["expert_no_in"].partition_broadcast(P)).then_inc(t["loaded"], 16)
            for w in range(2):
                sp.dma_start(t["up"][:, 0:E, w, :], t[f"up{w}_in"]).then_inc(t["loaded"], 16)
                sp.dma_start(t["up"][:, E, w, :], t[f"shared{w}_in"]).then_inc(t["loaded"], 16)
            sp.dma_start(t["down"][:, 0:2 * E, :], t["down_in"]).then_inc(t["loaded"], 16)
            sp.dma_start(t["down"][:, 2 * E:HC, :], t["shared_down_in"]).then_inc(t["loaded"], 16)

        @block.gpsimd
        def _(pool):
            def keys(b, part):
                w, half = part // 2, slice(8 * (part % 2), 8 * (part % 2) + 8)
                src, dst = ((k_hi, keys_hi), (k_lo, keys_lo))[w]
                pool.tensor_tensor(dst[:, b % 2, half, :],
                                   src[:, b, :].bitcast(F32).rearrange("p (o k) -> p o k", o=1).broadcast_to([P, 8, XK]),
                                   head_col[:, half].rearrange("p (h o) -> p h o", o=1).broadcast_to([P, 8, XK]),
                                   ALU.mult).then_inc(keys_ready, 1)

            def add_bias(b):
                pool.wait_ge(xn_ready, b + 1)
                tiles = slice(4 * b, 4 * b + 4)
                pool.tensor_tensor(x[:, tiles, :], x[:, tiles, :], bo.rearrange("p (o d) -> p o d", o=1).broadcast_to([P, 4, D]),
                                   ALU.add).then_inc(bo_added, 1)

            for slot in range(2):
                pool.memset(vals_lo[:, slot, first_half, high].bitcast(F32), 0.0)
                pool.memset(vals_lo[:, slot, second_half, low].bitcast(F32), 0.0).then_inc(zeros_ready, 1)
            pool.wait_ge(loaded, all_loaded)
            pool.wait_ge(k_hi_ready, 1)
            keys(0, 0)
            keys(0, 1)
            pool.wait_ge(k_split, 1)
            keys(0, 2)
            keys(0, 3)
            for part in range(4):
                keys(1, part)

            def values_low(b, i):
                pool.wait_ge(vals_hi_ready, b * len(V_CHUNKS) + i + 1)
                for r, js, at in v_pieces(i):
                    last = pool.tensor_tensor(vals_lo[0:r, b % 2, js, at], vals[0:r, js], vals_hi[0:r, b % 2, js, at].bitcast(F32),
                                              ALU.subtract)
                last.then_inc(vals_ready, 1)

            for i in range(len(V_CHUNKS)):
                values_low(0, i)
            add_bias(0)
            for n in range(B * XC):
                b, j, r = n // XC, n % XC, rows_of(n % XC)
                pool.wait_ge(p_hi_ready, n + 1)
                pool.tensor_tensor(p_lo[0:r, n % 4], e[0:r, n % 2], p_hi[0:r, n % 4].bitcast(F32), ALU.subtract)\
                    .then_inc(p_lo_ready, 1)
                if b + 1 < B:
                    if j in KEYS_AT and b > 0:
                        keys(b + 1, KEYS_AT.index(j))
                    if 4 <= j < 4 + len(V_CHUNKS):
                        values_low(b + 1, j - 4)
                    elif j == 8:
                        add_bias(b + 1)

        @block.scalar
        def _(act):
            act.wait_ge(loaded, all_loaded)
            act.wait_ge(thr_done, 2)
            act.activation(thr[:, 3:4], thr[:, 2:3], ACT.Exp).then_inc(thr_step, 1)
            act.wait_ge(thr_step, 1)
            act.activation(thr[:, 4:5], thr[:, 3:4], ACT.Ln, bias=1.0).then_inc(thr_step, 1)
            act.wait_ge(k_ready, 1)
            act.activation(k_hi[:], k_all[:], ACT.Copy).then_inc(k_hi_ready, 1)
            act.activation(wq_hi[:], wqT, ACT.Copy).then_inc(w_hi_ready, 1)
            act.activation(head_row_r[:], head_row, ACT.Copy).then_inc(head_row_ready, 1)
            root(act, work, root_wanted, root_ready, LATE_TILES)

            def tokens_high(n, b):
                act.wait_ge(prep_full, n + 1)
                act.activation(xnT_hi[:, b * S:(b + 1) * S], bank(PLAN[n][3][0]), ACT.Copy).then_inc(xnT_hi_ready, 1)

            def q_high(n, b):
                act.wait_ge(prep_full, n + 1)
                act.activation(q_hi[:, b % 2, :], pb[:, 0, :], ACT.Identity, bias=bias[:, 0:1]).then_inc(q_hi_ready, 1)

            def values_high(b, i):
                act.wait_ge(prep_read, index["v", i, b] + 1)
                for r, js, at in v_pieces(i):
                    last = act.activation(vals_hi[0:r, b % 2, js, at], vals[0:r, js], ACT.Copy)
                last.then_inc(vals_hi_ready, 1)

            def outputs(b):
                act.wait_ge(num_ready, b + 1)
                act.activation(out_T[:], num[:], ACT.Identity, bias=bias[:, 2:3]).then_inc(outT_ready, 1)

            act.activation(ident_b[:], ident[:], ACT.Copy)
            for slot in range(2):
                act.activation(vals_hi[:, slot, first_half, high], own_head[:, first_half], ACT.Copy)
                act.activation(vals_hi[:, slot, second_half, low], own_head[:, second_half], ACT.Copy).then_inc(consts_ready, 1)

            def take(b, half):
                wait_for(act, group_read, b)
                act.wait_ge(chunk_done, b * XC + (half + 1) * HX)
                own, other = ((low, high), (high, low))[half]
                act.activation(sums[own, :], acc[other, half, :], ACT.Copy)
                act.activation(outs[own, :], acc[own, half, :], ACT.Copy).then_inc(taken, 1)

            tokens_high(index["xt", 0, 0], 0)
            values_high(0, 0)
            values_high(0, 1)
            q_high(index["q", 0, 0], 0)
            values_high(0, 2)
            for n in range(B * XC):
                b, j, r = n // XC, n % XC, rows_of(n % XC)
                if b + 1 < B:
                    if j == 0:
                        tokens_high(index["xt", 0, b + 1], b + 1)
                    if j == 2:
                        q_high(index["q", 0, b + 1], b + 1)
                if j == 8 and b > 0:
                    outputs(b - 1)
                act.wait_ge(shifted, n + 1)
                wait_for(act, p_lo_ready, n - 1)
                act.activation(e[0:r, n % 2], sc[0:r, n % 3], ACT.Exp, scale=XD ** -0.5)
                act.activation(p_hi[0:r, n % 4], sc[0:r, n % 3], ACT.Exp, scale=XD ** -0.5).then_inc(p_hi_ready, 1)
                if b + 1 < B and j in (1, 2, 4):
                    values_high(b + 1, (1, 2, 4).index(j))
                if b > 0 and j == 2:
                    take(b - 1, 1)
                if j == HX + 3:
                    take(b, 0)
            take(B - 1, 1)
            outputs(B - 1)
            root(act, t["work3"], root_wanted, root_ready, FIRST_BATCHES, 2)

        @block.vector
        def _(dve):
            chain = Chain(dve, dve_chain)
            dve.wait_ge(loaded, all_loaded)
            chain.link(dve.tensor_scalar(thr[:, 1:2], t["thr"], -1.0, None, ALU.mult))
            dve.tensor_reduce(ctx_sum[:], ctxT, AX.X, ALU.add).then_inc(sum_ready, 1)
            chain.wait()
            dve.tensor_tensor(thr[:, 2:3], t["thr"], thr[:, 1:2], ALU.min).then_inc(thr_done, 1)
            dve.tensor_scalar(thr[:, 5:6], t["thr"], 0.0, None, ALU.max).then_inc(thr_done, 1)
            dve.wait_ge(first_full, 1)
            dve.tensor_scalar(k_all[:].rearrange("p b k -> p (b k)"), sc[:, 0, 0:B * XK], bias[:, 1:2], None,
                              ALU.add).then_inc(k_ready, 1)
            dve.tensor_copy(v_sum[:], sc[:, 1, 0:B])
            dve.wait_ge(thr_done, 2)
            dve.wait_ge(thr_step, 2)
            chain.link(dve.tensor_tensor(thr[:, 1:2], thr[:, 4:5], thr[:, 5:6], ALU.add))
            chain.wait()
            dve.tensor_scalar(thr[:, 0:1], thr[:, 1:2], XD ** 0.5, None, ALU.mult).then_inc(thr_done, 1)
            means(dve, chain, x, stats, moments, range(NT - PT // P, NT))
            dve.wait_ge(k_ready, 1)
            dve.wait_ge(k_hi_ready, 1)
            dve.tensor_tensor(k_lo[:], k_all[:], k_hi[:].bitcast(F32), ALU.subtract).then_inc(k_split, 1)
            inverse_roots(dve, chain, moments, rstd, work, root_wanted, root_ready, LATE_TILES)
            dve.wait_ge(w_hi_ready, 1)
            dve.tensor_tensor(wq_lo[:], wqT, wq_hi[:].bitcast(F32), ALU.subtract).then_inc(w_ready, 1)
            dve.wait_ge(thr_full, 1)
            for js in V_CHUNKS:
                r = rows_of(js[0])
                cut = slice(js.start, js.stop, js.step)
                last = dve.tensor_copy(thr_col[0:r, cut], sc[0:r, 2, cut])
            last.then_inc(setup_read, 1)
            dve.wait_ge(setup_read, 1)

            def read(n, kind, i, b, banks):
                dve.wait_ge(prep_full, n + 1)
                if kind == "xt":
                    dve.wait_ge(xnT_hi_ready, b + 1)
                    cols = slice(b * S, (b + 1) * S)
                    last = dve.tensor_tensor(xnT_lo[:, cols], bank(banks[0]), xnT_hi[:, cols].bitcast(F32), ALU.subtract)
                elif kind == "q":
                    dve.wait_ge(q_hi_ready, b + 1)
                    last = dve.scalar_tensor_tensor(out=q_lo[:, b % 2, :], in0=pb[:, 0, :], scalar=bias[:, 0:1],
                                                    in1=q_hi[:, b % 2, :].bitcast(F32), op0=ALU.add, op1=ALU.subtract)
                elif kind == "v":
                    wait_for(dve, vals_ready, b * len(V_CHUNKS))
                    c = 0
                    for r, js, _ in v_pieces(i):
                        n = js.stop - js.start
                        last = dve.tensor_tensor(vals[0:r, js], pb[0:r, banks[0], c * HD:(c + n) * HD]
                                                 .rearrange("p (j d) -> p j d", d=HD), own_head[0:r, js], ALU.mult)
                        c += n
                elif kind == "max":
                    for c, heads in enumerate(cuts):
                        w = (heads.stop - heads.start) * XK
                        last = dve.tensor_reduce(neg_max[:, i, heads], bank(banks[c])[:, 0:w].rearrange("p (h k) -> p h k", k=XK),
                                                 AX.X, ALU.max, negate=True)
                elif kind == "turn":
                    last = dve.tensor_copy(neg_maxT[:, b % 2, :], pb[0:XH, 0, :])
                else:
                    dve.wait_ge(bo_added, b + 1)
                    last = dve.tensor_tensor(x[:, 4 * b:4 * b + 4, :], x[:, 4 * b:4 * b + 4, :],
                                             pb[:, banks[0], :].rearrange("p (t d) -> p t d", t=4), ALU.add)
                last.then_inc(prep_read, 1)

            def finish(b, stage):
                if stage == 0:
                    dve.wait_ge(taken, 2 * b + 2)
                    chain.link(dve.tensor_scalar(none[:], sums[:], 0.0, None, ALU.is_equal))
                    chain.wait()
                    chain.link(dve.scalar_tensor_tensor(out=total[:], in0=none[:], scalar=float(XK), in1=sums[:],
                                                        op0=ALU.mult, op1=ALU.add))
                elif stage == 1:
                    chain.wait()
                    chain.link(dve.transpose(inv[:], total[:]))
                    chain.wait()
                    chain.link(dve.reciprocal(few[:], inv[:].rearrange("p (n g e) -> p n g e", g=32 // XD, e=XD)[:, :, :, 0]))
                elif stage == 2:
                    chain.wait()
                    chain.link(dve.transpose(inv[:], few[:].rearrange("p n g -> p (n g)").rearrange("p (m o) -> p m o", o=1)
                                             .broadcast_to([P, S // XD, XD])))
                else:
                    wait_for(dve, outT_ready, b)
                    dve.scalar_tensor_tensor(out=num[:], in0=none[:], scalar=v_sum[:, b:b + 1], in1=outs[:],
                                             op0=ALU.mult, op1=ALU.add).then_inc(group_read, 1)
                    chain.wait()
                    dve.wait_ge(group_read, b + 1)
                    dve.tensor_tensor(num[:], num[:], inv[:], ALU.mult).then_inc(num_ready, 1)

            for n, kind, i, b, banks, _ in prep_of(-1):
                read(n, kind, i, b, banks)
            for n in range(B * XC):
                b, j, r = n // XC, n % XC, rows_of(n % XC)
                dve.wait_ge(raw_full, n + 1)
                dve.tensor_scalar(mask[0:r, n % 3], sc[0:r, n % 3], thr_col[0:r, j:j + 1], MASKED,
                                  ALU.is_le, ALU.mult).then_inc(mask_ready, 1)
                for job in prep_at(b, j):
                    read(*job[:5])
                if j == XC - 1 and b + 2 < B:
                    normalize_batch(dve, b + 2, x, moments, rstd, xn, xn_ready)
                if b == B - 1 and j in (1, 2):
                    dve.wait_ge(prep_read, index["wo", 0, j - 1] + 1)
                    means(dve, chain, x, stats3, moments3, range(4 * (j - 1), 4 * j))
                if b > 0 and 4 <= j < 4 + 4:
                    finish(b - 1, j - 4)
            for stage in range(4):
                finish(B - 1, stage)
            dve.wait_ge(prep_read, index["wo", 0, B - 2] + 1)
            means(dve, chain, x, stats3, moments3, range(4 * (B - 2), 4 * (B - 1)))
            inverse_roots(dve, chain, moments3, t["rstd3"], t["work3"], root_wanted, root_ready, FIRST_BATCHES, 2)
            for job in prep_of(B):
                read(*job[:5])

        @block.tensor
        def _(pe):
            pe.wait_ge(loaded, all_loaded)
            pe.matmul(sc[:, 0, 0:B * XK], wkT, ctxT.rearrange("p b k -> p (b k)"), start=True, stop=True)
            pe.wait_ge(sum_ready, 1)
            pe.matmul(sc[:, 1, 0:B], wvT, ctx_sum[:], start=True, stop=True).then_inc(first_full, 1)
            pe.wait_ge(thr_done, 3)
            for j in range(XC):
                r = rows_of(j)
                last = pe.matmul(sc[0:r, 2, j:j + 1], head_row[:, pairs_of(j)], thr[:, 0:1], start=True, stop=True)
            last.then_inc(thr_full, 1)

            def prepare(n, kind, i, b, banks, needs):
                wait_for(pe, prep_read, needs)
                if kind == "xt":
                    pe.wait_ge(xn_ready, b + 1)
                    for i in range(4):
                        last = pe.transpose(bank(banks[0])[:, i * P:(i + 1) * P], xn[:, 4 * b + i, :], ident[:])
                elif kind == "q":
                    if b == 0:
                        pe.wait_ge(w_ready, 1)
                    pe.wait_ge(prep_read, index["xt", 0, b] + 1)
                    at = slice(b * S, (b + 1) * S)
                    pe.matmul(pb[:, 0, :], wq_hi[:], xnT_hi[:, at], start=True, stop=False)
                    pe.matmul(pb[:, 0, :], wq_hi[:], xnT_lo[:, at], start=False, stop=False)
                    last = pe.matmul(pb[:, 0, :], wq_lo[:], xnT_hi[:, at], start=False, stop=True)
                elif kind == "v":
                    if i == 0:
                        pe.wait_ge(rep_in[b], 16)
                    for c, j in enumerate(V_CHUNKS[i]):
                        r = rows_of(j)
                        last = pe.matmul(pb[0:r, banks[0], c * HD:(c + 1) * HD], ctx_rep[:, b, pairs_of(j)],
                                         wvT[:, features_of(j)], start=True, stop=True)
                elif kind == "max":
                    if i == 0:
                        pe.wait_ge(q_hi_ready, b + 1)
                        pe.wait_ge(keys_ready, 4 * b + 2)
                    for c, heads in enumerate(cuts):
                        w = (heads.stop - heads.start) * XK
                        last = pe.matmul(bank(banks[c])[:, 0:w], q_hi[:, b % 2, i * P:(i + 1) * P],
                                         keys_hi[:, b % 2, heads, :].rearrange("p h k -> p (h k)"), start=True, stop=True)
                elif kind == "turn":
                    pe.wait_ge(prep_read, index["max", 3, b] + 1)
                    for i in range(4):
                        last = pe.transpose(pb[0:XH, 0, i * P:(i + 1) * P], neg_max[:, i, :], ident[:])
                else:
                    pe.wait_ge(outT_ready, b + 1)
                    for i in range(4):
                        last = pe.matmul(pb[:, banks[0], i * D:(i + 1) * D], out_T[:, i * P:(i + 1) * P], woT,
                                         start=True, stop=True)
                last.then_inc(prep_full, 1)

            flat = lambda a, b: a[:, b % 2].rearrange("p h k -> p (h k)")

            def raw(b, j):
                n, r = b * XC + j, rows_of(j)
                cut = pairs_of(j)
                wait_for(pe, p_hi_ready, n - 2)
                if j == 0:
                    pe.wait_ge(prep_read, index["turn", 0, b] + 1)
                    pe.wait_ge(keys_ready, 4 * b + 4)
                out = sc[0:r, n % 3, :]
                pe.matmul(out, flat(keys_hi, b)[:, cut], q_hi[:, b % 2, :], start=True, stop=False)
                pe.matmul(out, flat(keys_hi, b)[:, cut], q_lo[:, b % 2, :], start=False, stop=False)
                pe.matmul(out, flat(keys_lo, b)[:, cut], q_hi[:, b % 2, :], start=False, stop=True).then_inc(raw_full, 1)

            def shift(b, j):
                n, r = b * XC + j, rows_of(j)
                out = sc[0:r, n % 3, :]
                pe.wait_ge(mask_ready, n + 1)
                pe.matmul(out, head_row_r[:, pairs_of(j)], neg_maxT[:, b % 2, :], start=False, stop=False,
                          skip_group_check=True)
                pe.matmul(out, ident_b[0:r, 0:r], mask[0:r, n % 3, :], start=False, stop=True,
                          skip_group_check=True).then_inc(shifted, 1)

            def weighted(b, j):
                n, r = b * XC + j, rows_of(j)
                first, last = j % HX == 0, j % HX == HX - 1
                hi, lo = p_hi[0:r, n % 4, :], p_lo[0:r, n % 4, :]
                out = acc[:, j // HX, :]
                if first:
                    wait_for(pe, taken, 2 * b - 1 + j // HX)
                if j == 0:
                    pe.wait_ge(vals_ready, (b + 1) * len(V_CHUNKS))
                pe.wait_ge(p_hi_ready, n + 1)
                pe.matmul(out, vals_hi[0:r, b % 2, j, :], hi, start=first, stop=False)
                pe.matmul(out, vals_lo[0:r, b % 2, j, :], hi, start=False, stop=False)
                pe.wait_ge(p_lo_ready, n + 1)
                pe.matmul(out, vals_hi[0:r, b % 2, j, :], lo, start=False, stop=last).then_inc(chunk_done, 1)

            for job in prep_of(-1):
                if job[1] == "max":
                    pe.wait_ge(setup_read, 1)
                prepare(*job)
            pe.wait_ge(head_row_ready, 1)
            pe.wait_ge(consts_ready, 2)
            pe.wait_ge(zeros_ready, 2)
            for n in range(B * XC + 3):
                if n < B * XC:
                    raw(n // XC, n % XC)
                    for job in prep_at(n // XC, n % XC):
                        prepare(*job)
                if 1 <= n <= B * XC:
                    shift((n - 1) // XC, (n - 1) % XC)
                if n >= 3:
                    weighted((n - 3) // XC, (n - 3) % XC)
            for job in prep_of(B):
                prepare(*job)


EXPERT_WEIGHTS = {"up": [P, E + 1, 2, HID],
                  "down": [P, HC, D], "router": [P, E], "route_bias": [P, E], "expert_no": [P, E]}
EXPERT_LOADS = 9


def mixture(nc, sb, psum, sem, t):
    x, ident = t["x"], t["ident"]
    xn = sb("xn3", [P, NT, D], F32)
    xnT_hi, xnT_lo = sb("xnT3_hi", [P, B * S], F32R), sb("xnT3_lo", [P, B * S], F32R)
    xnT = sb("xnT3", [P, B * S], F32)
    stats, moments = t["stats3"], t["moments3"]
    rstd, work = t["rstd3"], t["work3"]
    up, down, router, route_bias, expert_no = (t[n] for n in EXPERT_WEIGHTS)
    up_hi, up_lo = sb("up_hi", [P, E + 1, 2, HID], F32R), sb("up_lo", [P, E + 1, 2, HID], F32R)
    logits, top, place = sb("logits", [P, NT, E], F32), sb("top", [P, NT, 8], F32), sb("place", [P, NT, 8], U32)
    place_f = sb("place_f", [P, NT, 2], F32)
    gap, gap_e, weight = sb("gap", [P, NT], F32), sb("gap_e", [P, 2, NT], F32), sb("weight", [P, 2, NT], F32)
    hit, cw = sb("hit", [P, 2, NT, E], F32), sb("cw", [P, NT, E], F32)
    gate = sb("gate", [P, 3, S], F32)
    hidden = sb("hidden", [P, 3, S], F32)

    g, u, y = psum("g", [P, 3, S], F32), psum("u", [P, 3, S], F32), psum("y", [P, 2, S], F32)

    loaded, all_loaded = t["loaded"], 16 * EXPERT_LOADS
    root_wanted, root_ready, dve_chain = sem("root_wanted3"), sem("root_ready3"), sem("dve_chain3")
    xn_ready, xnT_full, xnT_hi_ready, xnT_ready = sem("xn_ready3"), sem("xnT_full3"), sem("xnT_hi_ready3"), sem("xnT_ready3")
    xnT_whole, up_hi_ready, up_ready = sem("xnT_whole"), sem("up_hi_ready"), sem("up_ready")
    logits_full, gap_ready, gap_e_ready = sem("logits_full"), sem("gap_ready"), sem("gap_e_ready")
    gu_full, gate_ready, hidden_ready = sem("gu_full"), sem("gate_ready"), sem("hidden_ready")
    y_full, y_added, stored = sem("y_full"), sem("y_added"), sem("stored")
    NE = E + 1
    turning = (y[:, 0, :], y[:, 1, :], u[:, 2, :], g[:, 2, :])

    with nc.Block() as block:
        @block.sync
        def _(sp):
            with sp.Fori(0, B) as b:
                sp.wait_ge(y_added, (b + 1) * NE + 1)
                sp.dma_start(t["out"][:, bass.ds(b * 4, 4), :], x[:, bass.ds(b * 4, 4), :]).then_inc(stored, 16)
            sp.wait_ge(stored, 16 * B)

        @block.gpsimd
        def _(pool):
            for n in range(NE):
                pool.wait_ge(up_hi_ready, n + 1)
                pool.tensor_tensor(up_lo[:, n], up[:, n], up_hi[:, n].bitcast(F32), ALU.subtract).then_inc(up_ready, 1)

        @block.scalar
        def _(act):
            def up_high(n):
                act.activation(up_hi[:, n], up[:, n], ACT.Copy).then_inc(up_hi_ready, 1)

            def tokens(b):
                act.wait_ge(xnT_full, b + 1)
                cols = slice(b * S, (b + 1) * S)
                act.activation(xnT[:, cols], turning[b], ACT.Copy).then_inc(xnT_whole, 1)
                act.wait_ge(xnT_whole, b + 1)
                act.activation(xnT_hi[:, cols], xnT[:, cols], ACT.Copy).then_inc(xnT_hi_ready, 1)

            act.wait_ge(loaded, all_loaded)
            up_high(0)
            tokens(0)
            tokens(1)
            root(act, work, root_wanted, root_ready, LAST_BATCH)
            up_high(1)
            tokens(2)
            tokens(3)
            for n in range(2, NE):
                up_high(n)
            act.wait_ge(gap_ready, 1)
            act.activation(gap_e[:, 0, :], gap[:], ACT.Exp).then_inc(gap_e_ready, 1)
            with act.Fori(0, B) as b:
                for c in range(HC):
                    n = b * HC + c
                    act.wait_ge(gu_full, n + 1)
                    act.activation(gate[:, c % 3, :], g[:, c % 3, :], ACT.Silu).then_inc(gate_ready, 1)

        @block.vector
        def _(dve):
            chain = Chain(dve, dve_chain)
            def token_rest(b):
                cols = slice(b * S, (b + 1) * S)
                dve.wait_ge(xnT_hi_ready, b + 1)
                dve.tensor_tensor(xnT_lo[:, cols], xnT[:, cols], xnT_hi[:, cols].bitcast(F32), ALU.subtract)\
                   .then_inc(xnT_ready, 1)

            normalized = lambda b: normalize_batch(dve, b, x, moments, rstd, xn, xn_ready)
            normalized(0)
            normalized(1)
            means(dve, chain, x, stats, moments, range(NT - 4, NT))
            token_rest(0)
            normalized(2)
            inverse_roots(dve, chain, moments, rstd, work, root_wanted, root_ready, LAST_BATCH)
            normalized(3)
            for b in range(1, B):
                token_rest(b)
            dve.wait_ge(loaded, all_loaded)
            row = lambda a: a.rearrange("p (o e) -> p o e", o=1).broadcast_to([P, NT, E])
            col = lambda a: a.rearrange("p (t o) -> p t o", o=1).broadcast_to([P, NT, E])
            dve.wait_ge(logits_full, 1)
            chain.link(dve.tensor_tensor(logits[:], y[:, 0, 0:NT * E].rearrange("p (t e) -> p t e", e=E),
                                         row(route_bias[:]), ALU.add))
            chain.wait()
            for i in range(NT):
                chain.link(dve.max(top[:, i, :], logits[:, i, :]))
            chain.wait()
            dve.tensor_tensor(gap[:], top[:, :, 1], top[:, :, 0], ALU.subtract).then_inc(gap_ready, 1)
            for i in range(NT):
                chain.link(dve.max_index(place[:, i, :], top[:, i, :], logits[:, i, :]))
            chain.wait()
            chain.link(dve.tensor_copy(place_f[:], place[:, :, 0:2]))
            dve.wait_ge(gap_e_ready, 1)
            chain.link(dve.tensor_scalar(gap_e[:, 1, :], gap_e[:, 0, :], 1.0, None, ALU.add))
            chain.wait()
            chain.link(dve.reciprocal(weight[:, 0, :], gap_e[:, 1, :]))
            chain.wait()
            chain.link(dve.tensor_tensor(weight[:, 1, :], weight[:, 0, :], gap_e[:, 0, :], ALU.mult))
            for i in range(2):
                chain.link(dve.tensor_tensor(hit[:, i], row(expert_no[:]), col(place_f[:, :, i]), ALU.is_equal))
            chain.wait()
            for i in range(2):
                chain.link(dve.tensor_tensor(hit[:, i], hit[:, i], col(weight[:, i, :]), ALU.mult))
            chain.wait()
            dve.tensor_tensor(cw[:], hit[:, 0], hit[:, 1], ALU.add).then_inc(y_added, 1)
            dve.wait_ge(y_added, 1)
            with dve.Fori(0, B) as b:
                def add(e):
                    dve.wait_ge(y_full, b * NE + e + 1)
                    tiles = bass.ds(b * 4, 4)
                    if e > 0:
                        dve.wait_ge(y_added, b * NE + e + 1)
                    if e == E:
                        last = dve.tensor_tensor(x[:, tiles, :], x[:, tiles, :],
                                                 y[:, e % 2, :].rearrange("p (t d) -> p t d", t=4), ALU.add)
                    else:
                        for i in range(4):
                            tile = bass.ds(b * 4 + i, 1)
                            rows = x[:, tile, :].rearrange("p o d -> p (o d)")
                            last = dve.scalar_tensor_tensor(out=rows, in0=y[:, e % 2, i * D:(i + 1) * D],
                                                            scalar=cw[:, tile, e:e + 1].rearrange("p o e -> p (o e)"),
                                                            in1=rows, op0=ALU.mult, op1=ALU.add)
                    last.then_inc(y_added, 1)

                for c in range(HC):
                    n = b * HC + c
                    dve.wait_ge(gate_ready, n + 1)
                    dve.tensor_tensor(hidden[:, c % 3, :], gate[:, c % 3, :], u[:, c % 3, :],
                                      ALU.mult).then_inc(hidden_ready, 1)
                    if c >= 3 and c % 2 == 1:
                        add((c - 3) // 2)
                add(E)

        @block.tensor
        def _(pe):
            def turn(b):
                pe.wait_ge(xn_ready, b + 1)
                for i in range(4):
                    last = pe.transpose(turning[b][:, i * P:(i + 1) * P], xn[:, 4 * b + i, :], ident[:])
                last.then_inc(xnT_full, 1)

            def route(b):
                pe.wait_ge(xnT_whole, b + 1)
                for i in range(4 * b, 4 * b + 4):
                    last = pe.matmul(y[:, 0, i * E:(i + 1) * E], xnT[:, i * P:(i + 1) * P], router[:], start=True, stop=True)
                return last

            turn(0)
            turn(1)
            pe.wait_ge(loaded, all_loaded)
            route(0)
            turn(2)
            route(1)
            route(2)
            turn(3)
            last = route(3)
            last.then_inc(logits_full, 1)

            def up_project(b, c):
                e, half = c // 2, slice(c % 2 * P, c % 2 * P + P)
                if c >= 3:
                    pe.wait_ge(hidden_ready, b * HC + c - 2)
                if c % 2 == 0:
                    pe.wait_ge(up_ready, e + 1)
                if c == 0:
                    pe.wait_ge(xnT_ready, b + 1)
                if c == 2:
                    pe.wait_ge(xnT_whole, B)
                at = bass.ds(b * S, S)
                for w, bank in enumerate((g, u)):
                    out = bank[:, c % 3, :]
                    pe.matmul(out, up_hi[:, e, w, half], xnT_hi[:, at], start=True, stop=False)
                    pe.matmul(out, up_hi[:, e, w, half], xnT_lo[:, at], start=False, stop=False)
                    last = pe.matmul(out, up_lo[:, e, w, half], xnT_hi[:, at], start=False, stop=True)
                last.then_inc(gu_full, 1)

            def down_project(b, c):
                e = c // 2
                pe.wait_ge(hidden_ready, b * HC + c + 1)
                if c % 2 == 0:
                    pe.wait_ge(y_added, b * NE + max(e, 1))
                for i in range(4):
                    last = pe.matmul(y[:, e % 2, i * D:(i + 1) * D], hidden[:, c % 3, i * P:(i + 1) * P],
                                     down[:, c, :], start=(c % 2 == 0 and i == 0), stop=(c % 2 == 1),
                                     skip_group_check=True)
                if c % 2 == 1:
                    last.then_inc(y_full, 1)

            with pe.Fori(0, B) as b:
                for c in range(HC + 2):
                    if c < HC:
                        up_project(b, c)
                    if c >= 2:
                        down_project(b, c - 2)


def build(nc, t):
    with ExitStack() as all_:
        t["x"] = all_.enter_context(nc.sbuf_tensor("x_res", [P, NT, D], F32))
        t["ident"] = all_.enter_context(nc.sbuf_tensor("ident", [P, P], F32))
        t["loaded"] = all_.enter_context(nc.semaphore("experts_loaded"))
        t["early_loaded"] = all_.enter_context(nc.semaphore("early_loaded"))
        with nc.sbuf_tensor("wqk_hi", [P, 2, C, 2, DH], F32R) as weights:
            t["wqk_hi"] = weights
        t["early"] = all_.enter_context(nc.sbuf_tensor("early", [P, 2 * 2 * C * DH], F32))
        with nc.sbuf_tensor("wqk_lo", [P, 2, C, 2, DH], F32R) as weights:
            t["wqk_lo"] = weights
        t["xn2"] = all_.enter_context(nc.sbuf_tensor("xn2", [P, NT, D], F32))
        t["xn2_ready"] = all_.enter_context(nc.semaphore("xn2_ready"))
        at = 0
        for name, (rows, words) in EARLY.items():
            t[name] = t["early"][0:rows, at:at + words]
            at += words
        t["ctxT"] = t["ctxT"].rearrange("p (b k) -> p b k", b=B)
        t["own_head"] = t["own_head"].rearrange("p (j d) -> p j d", d=HD)
        t["stats2"] = t["early"][:, at:at + NT * 6].rearrange("p (t n) -> p t n", n=6)
        at += NT * 6
        t["moments2"] = t["early"][:, at:at + NT * 2].rearrange("p (t n) -> p t n", n=2)
        at += NT * 2
        t["stats3"] = t["early"][:, at:at + NT * 6].rearrange("p (t n) -> p t n", n=6)
        at += NT * 6
        t["moments3"] = t["early"][:, at:at + NT * 2].rearrange("p (t n) -> p t n", n=2)
        at += NT * 2
        for name, n in (("rstd2", 2), ("work2", 3), ("rstd3", 2), ("work3", 3)):
            t[name] = t["early"][:, at:at + n * NT].rearrange("p (n t) -> p n t", t=NT)
            at += n * NT
        rest = ExitStack()
        rest.enter_context(nc.sbuf_tensor("wqk_lo_rest", [P, NT, D], F32))
        for layer in (self_attention, cross_attention, mixture):
            if layer is cross_attention:
                rest.close()
                for name, shape in EXPERT_WEIGHTS.items():
                    t[name] = all_.enter_context(nc.sbuf_tensor(name, shape, F32))
            with ExitStack() as own:
                layer(nc, lambda n, s, d: own.enter_context(nc.sbuf_tensor(n, s, d)),
                      lambda n, s, d: own.enter_context(nc.psum_tensor(n, s, d)),
                      lambda n: all_.enter_context(nc.semaphore(n)), t)


def kernel(**inputs):
    import numpy as np
    import concourse.bacc as bacc
    from concourse.bass_utils import run_bass_kernel_spmd

    def get(name):
        return np.asarray(inputs[name])

    def constant(a):
        return np.asarray(a, np.float32)

    pair_head = np.arange(XF) // XK
    feature_head = np.arange(D) // XD
    own_head = np.zeros((P, XC, HD))
    for j in range(XC):
        heads = pair_head[pairs_of(j)]
        own_head[0:len(heads), j] = heads[:, None] == feature_head[None, features_of(j)]
    arrays = {
        "wqT": get("L0_attn_wq").T.reshape(D, C, DH),
        "wkT": get("L0_attn_wk").T.reshape(D, C, DH),
        "wvT": get("L0_attn_wv").T,
        "woT": get("L0_attn_wo").T.reshape(C // 2, P, D).transpose(1, 0, 2),
        "ident": constant(np.eye(P)),
        "xwqT": get("L0_xattn_Wq").T, "xwkT": get("L0_xattn_Wk").T,
        "xwvT": get("L0_xattn_Wv").T, "xwoT": get("L0_xattn_Wo").T,
        "xbias": np.stack([get("L0_xattn_bq"), get("L0_xattn_bk"), get("L0_xattn_bv")], 1),
        "bo": get("L0_xattn_bo"),
        "ctxT": get("ctx_1024").transpose(2, 0, 1),
        "thr": get("L0_xattn_raw_thresholds").reshape(XH, 1),
        "head_row": constant(pair_head[None] == np.arange(XH)[:, None]),
        "head_col": constant(feature_head[:, None] == np.arange(XH)[None]),
        "own_head": constant(own_head),
        "router": get("L0_ffn_router_w").T,
        "route_bias": get("L0_ffn_experts_bias"),
        "expert_no": constant(np.arange(E)),
        "up0": get("L0_ffn_w1").transpose(1, 0, 2), "up1": get("L0_ffn_w3").transpose(1, 0, 2),
        "shared0": get("L0_ffn_sw1")[0], "shared1": get("L0_ffn_sw3")[0],
        "down": get("L0_ffn_w2").reshape(2 * E, P, D).transpose(1, 0, 2),
        "shared_down": get("L0_ffn_sw2")[0].reshape(2, P, D).transpose(1, 0, 2),
        "x": get("x"),
    }
    nc = bacc.Bacc("TRN2", target_bir_lowering=False, num_devices=1)
    t, feeds = {}, {}
    for name, a in arrays.items():
        a = np.ascontiguousarray(a)
        feeds[f"in_{name}"] = a
        t[f"{name}_in"] = nc.dram_tensor(f"in_{name}", a.shape, F32, kind="ExternalInput").ap()
    by_tile = "b (t p) d -> p (b t) d"
    t["x_in"] = t["x_in"].rearrange(by_tile, p=P)
    t["out"] = nc.dram_tensor("out", (B, S, D), F32, kind="ExternalOutput").ap().rearrange(by_tile, p=P)
    build(nc, t)
    result = run_bass_kernel_spmd(nc, [feeds], core_ids=[0])
    return result.results[0]["out"]
```
